# Optimizing a Trainium2 kernel written in Bass

```python
import numpy as np
import jax
import jax.numpy as jnp

def _softmax(x, axis=-1):
    return jax.nn.softmax(x, axis=axis)

def _gelu(x):
    return jax.nn.gelu(x, approximate=True)

def _silu(x):
    return jax.nn.silu(x)

def _sigmoid(x):
    return jax.nn.sigmoid(x)

def _layernorm(x, axis=-1, eps=1e-05):
    m = jnp.mean(x, axis=axis, keepdims=True)
    v = jnp.var(x, axis=axis, keepdims=True)
    return (x - m) / jnp.sqrt(v + eps)

def _scatter_add(tgt, idx, src, axis=0):
    return tgt.at[idx].add(src)

def _segment_sum(src, seg, n):
    return jax.ops.segment_sum(src, seg, n)
kernel_name = 'mk_gnn_resnorm_d4_gnn_r8_0bc39b'

def setup_inputs(seed: int=0):
    np.random.seed(seed)
    _w = jnp.asarray

    def _rec_inputs():
        import jax
        import jax.numpy as jnp
        _gk = jax.random.key(seed)
        x = -0.000202 + 1 * jax.random.normal(jax.random.fold_in(_gk, 1), (12500, 128), jnp.float32)
        src = jax.random.randint(jax.random.fold_in(_gk, 2), (200000,), 0, 12500, jnp.int32)
        dst = jax.random.randint(jax.random.fold_in(_gk, 3), (200000,), 0, 12500, jnp.int32)
        _o = jnp.argsort(dst, stable=True)
        src = src[_o]
        dst = dst[_o]
        edge_type_4 = jax.random.randint(jax.random.fold_in(_gk, 13), (200000,), 0, 4, jnp.int32)
        edge_weight = jax.random.uniform(jax.random.fold_in(_gk, 14), (200000,), jnp.float32, 0.0, 0.999998)
        edge_weight1 = jax.random.uniform(jax.random.fold_in(_gk, 15), (200000, 1), jnp.float32, 0.0, 1)
        return (x, src, dst, edge_type_4, edge_weight, edge_weight1)
    x, src, dst, edge_type_4, edge_weight, edge_weight1 = _rec_inputs()

    def _L0_gnn_setup():
        import jax, jax.numpy as jnp
        import numpy as np
        N = 6250
        E = 100000
        IN_F = 128
        OUT_F = 128
        key = jax.random.key(seed)
        k1, k2, k3, k4, k5 = jax.random.split(key, 5)
        x = jax.random.normal(k1, (N, IN_F), dtype=jnp.float32)
        edge_index = jax.random.randint(k2, (2, E), 0, N, dtype=jnp.int64)
        edge_weight = jax.random.uniform(k3, (E,), dtype=jnp.float32)
        W = jax.random.normal(k4, (OUT_F, IN_F), dtype=jnp.float32) * (1.0 / np.sqrt(IN_F))
        b = jax.random.normal(k5, (OUT_F,), dtype=jnp.float32) * 0.01
        return {'x': x, 'edge_index': edge_index, 'edge_weight': edge_weight, 'W': W, 'b': b}
    _L0_gnn_all = _L0_gnn_setup()
    _L0_gnn_in = {k: v for k, v in _L0_gnn_all.items() if k in ('W', 'b')}
    del _L0_gnn_all

    def _L1_gnn_setup():
        import jax, jax.numpy as jnp
        import numpy as np
        N = 6250
        E = 100000
        C_IN = 128
        C_HID = 128
        key = jax.random.key(seed)
        ks = jax.random.split(key, 8)
        node_embed = jax.random.normal(ks[0], (N, C_IN), dtype=jnp.float32)
        edge_dist = jax.random.uniform(ks[1], (E, 1), dtype=jnp.float32)
        edge_index = jax.random.randint(ks[2], (2, E), 0, N, dtype=jnp.int64)
        msg_in = 2 * C_IN + 1
        W_res = jax.random.uniform(ks[3], (C_IN, C_HID), dtype=jnp.float32, minval=-1, maxval=1) / np.sqrt(C_IN)
        W_msg = jax.random.uniform(ks[4], (msg_in, C_HID), dtype=jnp.float32, minval=-1, maxval=1) / np.sqrt(msg_in)
        b_msg = jnp.zeros((C_HID,), dtype=jnp.float32)
        W_upd = jax.random.uniform(ks[5], (C_IN + C_HID, C_HID), dtype=jnp.float32, minval=-1, maxval=1) / np.sqrt(C_IN + C_HID)
        b_upd = jnp.zeros((C_HID,), dtype=jnp.float32)
        return {'node_embed': node_embed, 'edge_dist': edge_dist, 'edge_index': edge_index, 'W_res': W_res, 'W_msg': W_msg, 'b_msg': b_msg, 'W_upd': W_upd, 'b_upd': b_upd}
    _L1_gnn_all = _L1_gnn_setup()
    _L1_gnn_in = {k: v for k, v in _L1_gnn_all.items() if k in ('W_res', 'W_msg', 'b_msg', 'W_upd', 'b_upd')}
    del _L1_gnn_all

    def _L2_gnn_setup():
        import jax, jax.numpy as jnp
        import numpy as np
        N, E, IN_C, H, C = (6250, 100000, 128, 4, 32)
        key = jax.random.key(seed)
        ks = jax.random.split(key, 10)
        s = 1.0 / np.sqrt(IN_C)
        x = jax.random.normal(ks[0], (N, IN_C), dtype=jnp.float32)
        edge_index = jax.random.randint(ks[1], (2, E), 0, N, dtype=jnp.int64)
        Wq = jax.random.uniform(ks[2], (IN_C, H * C), jnp.float32, -s, s)
        bq = jax.random.uniform(ks[3], (H * C,), jnp.float32, -s, s)
        Wk = jax.random.uniform(ks[4], (IN_C, H * C), jnp.float32, -s, s)
        bk = jax.random.uniform(ks[5], (H * C,), jnp.float32, -s, s)
        Wv = jax.random.uniform(ks[6], (IN_C, H * C), jnp.float32, -s, s)
        bv = jax.random.uniform(ks[7], (H * C,), jnp.float32, -s, s)
        Wr = jax.random.uniform(ks[8], (IN_C, H * C), jnp.float32, -s, s)
        br = jax.random.uniform(ks[9], (H * C,), jnp.float32, -s, s)
        return {'x': x, 'edge_index': edge_index, 'Wq': Wq, 'bq': bq, 'Wk': Wk, 'bk': bk, 'Wv': Wv, 'bv': bv, 'Wr': Wr, 'br': br}
    _L2_gnn_all = _L2_gnn_setup()
    _L2_gnn_in = {k: v for k, v in _L2_gnn_all.items() if k in ('Wq', 'bq', 'Wk', 'bk', 'Wv', 'bv', 'Wr', 'br')}
    del _L2_gnn_all

    def _L3_gnn_setup():
        import jax, jax.numpy as jnp
        import numpy as np
        N, E, IN, OUT = (6250, 100000, 128, 128)
        R = 5
        key = jax.random.key(seed)
        k = jax.random.split(key, 6)
        x = jax.random.normal(k[0], (N, IN), jnp.float32)
        src = jax.random.randint(k[1], (E,), 0, N)
        dst = jax.random.randint(k[2], (E,), 0, N)
        rel = jax.random.randint(k[3], (E,), 0, R - 1)
        xavier = np.sqrt(2.0) * np.sqrt(6.0 / (IN + OUT))
        weight = jax.random.uniform(k[4], (R, IN, OUT), jnp.float32, -xavier, xavier)
        bias = jax.random.uniform(k[5], (R, OUT), jnp.float32, -xavier, xavier)
        return dict(x=x, weight=weight, bias=bias, src=src, dst=dst, rel=rel)
    _L3_gnn_all = _L3_gnn_setup()
    _L3_gnn_in = {k: v for k, v in _L3_gnn_all.items() if k in ('weight', 'bias')}
    del _L3_gnn_all
    return {'x': x, 'src': src, 'dst': dst, 'edge_type_4': edge_type_4, 'edge_weight': edge_weight, 'edge_weight1': edge_weight1, 'L0_gnn_W': _L0_gnn_in['W'], 'L0_gnn_b': _L0_gnn_in['b'], 'L1_gnn_W_res': _L1_gnn_in['W_res'], 'L1_gnn_W_msg': _L1_gnn_in['W_msg'], 'L1_gnn_b_msg': _L1_gnn_in['b_msg'], 'L1_gnn_W_upd': _L1_gnn_in['W_upd'], 'L1_gnn_b_upd': _L1_gnn_in['b_upd'], 'L2_gnn_Wq': _L2_gnn_in['Wq'], 'L2_gnn_bq': _L2_gnn_in['bq'], 'L2_gnn_Wk': _L2_gnn_in['Wk'], 'L2_gnn_bk': _L2_gnn_in['bk'], 'L2_gnn_Wv': _L2_gnn_in['Wv'], 'L2_gnn_bv': _L2_gnn_in['bv'], 'L2_gnn_Wr': _L2_gnn_in['Wr'], 'L2_gnn_br': _L2_gnn_in['br'], 'L3_gnn_weight': _L3_gnn_in['weight'], 'L3_gnn_bias': _L3_gnn_in['bias']}

def reference(x, src, dst, edge_type_4, edge_weight, edge_weight1, L0_gnn_W, L0_gnn_b, L1_gnn_W_res, L1_gnn_W_msg, L1_gnn_b_msg, L1_gnn_W_upd, L1_gnn_b_upd, L2_gnn_Wq, L2_gnn_bq, L2_gnn_Wk, L2_gnn_bk, L2_gnn_Wv, L2_gnn_bv, L2_gnn_Wr, L2_gnn_br, L3_gnn_weight, L3_gnn_bias):
    import jax
    import jax.numpy as jnp

    def _L0_gnn_ref(x, edge_index, edge_weight, W, b):
        import jax, jax.numpy as jnp
        import numpy as np
        N = 6250
        E = 100000
        IN_F = 128
        OUT_F = 128
        hidden = jnp.einsum('ni,oi->no', x, W) + b
        dst = edge_index[0]
        src = edge_index[1]
        msgs = edge_weight[:, None] * hidden[src]
        out = jax.ops.segment_sum(msgs, dst, num_segments=x.shape[0])
        return out

    def _L1_gnn_ref(node_embed, edge_dist, edge_index, W_res, W_msg, b_msg, W_upd, b_upd):
        import jax, jax.numpy as jnp
        import numpy as np
        N = 6250
        E = 100000
        C_IN = 128
        C_HID = 128
        row, col = (edge_index[0], edge_index[1])
        msg_repr = jnp.concatenate((node_embed[row], node_embed[col], edge_dist), axis=-1)
        node_messages = jax.nn.relu(msg_repr @ W_msg + b_msg)
        aggr = jax.ops.segment_sum(node_messages, col, num_segments=node_embed.shape[0])
        upd_in = jnp.concatenate((node_embed, aggr), axis=-1)
        new_node_embed = node_embed @ W_res + jax.nn.relu(upd_in @ W_upd + b_upd)
        return new_node_embed

    def _L2_gnn_ref(x, edge_index, Wq, bq, Wk, bk, Wv, bv, Wr, br):
        import jax, jax.numpy as jnp
        import numpy as np
        N, E, IN_C, H, C = (6250, 100000, 128, 4, 32)
        n = x.shape[0]
        row, col = (edge_index[0], edge_index[1])
        q = (x @ Wq + bq).reshape(n, H, C)
        k = (x @ Wk + bk).reshape(n, H, C)
        v = (x @ Wv + bv).reshape(n, H, C)
        scores = jnp.einsum('ehc,ehc->eh', q[col], k[row]) / np.sqrt(C)
        m = jax.ops.segment_max(scores, col, num_segments=n)
        ex = jnp.exp(scores - m[col])
        denom = jax.ops.segment_sum(ex, col, num_segments=n)
        w = ex / denom[col]
        out = jax.ops.segment_sum(v[row] * w[:, :, None], col, num_segments=n)
        out = out.reshape(n, H * C)
        root = x @ Wr + br
        return out + root

    def _L3_gnn_ref(x, weight, bias, src, dst, rel):
        import jax, jax.numpy as jnp
        import numpy as np
        N, E, IN, OUT = (6250, 100000, 128, 128)
        R = 5
        num_nodes = x.shape[0]
        num_edge_rels = weight.shape[0] - 1
        x_src = x[src]
        msg = jnp.zeros((src.shape[0], weight.shape[2]), x.dtype)
        for r in range(num_edge_rels):
            hr = x_src @ weight[r] + bias[r]
            msg = jnp.where((rel == r)[:, None], hr, msg)
        agg = jax.ops.segment_max(msg, dst, num_segments=num_nodes)
        deg = jax.ops.segment_sum(jnp.ones_like(dst, jnp.float32), dst, num_segments=num_nodes)
        agg = jnp.where((deg > 0)[:, None], agg, jnp.zeros((), x.dtype))
        h = x @ weight[-1] + bias[-1] + agg
        return h
    edge_index = jnp.stack([src, dst])
    x = _layernorm(x + _L0_gnn_ref(x, edge_index, edge_weight, L0_gnn_W, L0_gnn_b), axis=-1)
    x = _layernorm(x + _L1_gnn_ref(x, edge_weight1, edge_index, L1_gnn_W_res, L1_gnn_W_msg, L1_gnn_b_msg, L1_gnn_W_upd, L1_gnn_b_upd), axis=-1)
    x = _layernorm(x + _L2_gnn_ref(x, edge_index, L2_gnn_Wq, L2_gnn_bq, L2_gnn_Wk, L2_gnn_bk, L2_gnn_Wv, L2_gnn_bv, L2_gnn_Wr, L2_gnn_br), axis=-1)
    x = _layernorm(x + _L3_gnn_ref(x, L3_gnn_weight, L3_gnn_bias, src, dst, edge_type_4), axis=-1)
    return x

_drawn_inputs = setup_inputs


def setup_inputs(seed=0):
    import zlib

    import numpy as np

    out = dict(_drawn_inputs(seed))
    spreads = {'L1_gnn_b_msg': (0.0, 0.1), 'L1_gnn_b_upd': (0.0, 0.1)}
    factors = {'edge_weight1': 8.0, 'L2_gnn_bq': 8.0, 'L2_gnn_bk': 8.0}
    for name, (base, spread) in spreads.items():
        noise = np.random.default_rng([zlib.crc32(name.encode()), seed]).standard_normal(out[name].shape)
        drawn = base * np.exp(spread * noise) if base else spread * noise
        out[name] = jnp.asarray(drawn.astype(out[name].dtype))
    for name, factor in factors.items():
        out[name] = (out[name] * factor).astype(out[name].dtype)
    return out
```

```python
from contextlib import ExitStack

import concourse.bass as bass
import numpy as np
from concourse import mybir

F32, BF16, I32, U32 = mybir.dt.float32, mybir.dt.bfloat16, mybir.dt.int32, mybir.dt.uint32
ALU, ACT, AX = mybir.AluOpType, mybir.ActivationFunctionType, mybir.AxisListType

P = 128
D = 128
N, E = 12500, 200000
QUAD = 4
QE = QUAD * P
TILES = 16
QUADS = TILES // QUAD
GE = TILES * P
GROUPS = -(-E // GE)
EP = GROUPS * GE
NT = EP // P
NB = -(-N // P)
NP = NB * P
STEP = 7
STEPS = NB // STEP
FB, FSTEP = 100, 10
HEADS, HC = 4, 32
RELS = 4
ACCS = 4
TW = D + HEADS
FAR = 3.0e38
EPS = 1e-5


def made(n):
    return n + 1


def free(n):
    return n - 1


def landed(k, dmas):
    return 16 * dmas * (k + 1)


def landed_before(k, dmas):
    return 16 * dmas * k


def any_yet(count):
    return not isinstance(count, int) or count > 0


def skewed(eng, steps, front, back):
    last = steps // 2 - 1
    front(0, 0, 0)
    front(1, 1, 0)
    back(0, 0, 0)
    front(2, 0, 1)
    back(1, 1, 0)
    with eng.Fori(1, last) as i:
        front(2 * i + 1, 1, i)
        back(2 * i, 0, i)
        front(2 * i + 2, 0, i + 1)
        back(2 * i + 1, 1, i)
    front(steps - 1, 1, last)
    back(steps - 2, 0, last)
    back(steps - 1, 1, last)


def pool_wait(pool, sem, value):
    pool.wait_ge(sem, value)
    pool.nop(nofuse=True)


class Memory:
    def __init__(self, nc, ctx, phase):
        self.nc, self.ctx, self.phase, self.sems = nc, ctx, phase, []
        ctx.callback(self.release)

    def sb(self, name, shape, dt=F32):
        return self.ctx.enter_context(self.nc.sbuf_tensor(f"{self.phase}_{name}", shape, dt))

    def ps(self, name, shape):
        return self.ctx.enter_context(self.nc.psum_tensor(f"{self.phase}_{name}_psum", shape, F32))

    def sem(self, name):
        self.sems.append(self.nc.alloc_semaphore(name=f"{self.phase}_{name}"))
        return self.sems[-1]

    def release(self):
        if self.sems:
            self.nc.clear_and_free_semaphores(self.sems)
            self.nc.all_engine_barrier()


def by_group(flat, n):
    return flat.rearrange("(g p t) f -> p g (t f)", p=P, t=TILES)[:, bass.ds(n, 1), :].rearrange("p o e -> p (o e)")


def edge_row(v, after, row, edge, part, part2):
    after(v.tensor_scalar(part, edge, P - 1, 4, ALU.bitwise_and, ALU.logical_shift_left))
    after(v.tensor_scalar(part2, edge, 7, TILES - 1, ALU.logical_shift_right, ALU.bitwise_and))
    after(v.tensor_tensor(part, part, part2, ALU.bitwise_or))
    after(v.tensor_scalar(part2, edge, 11, 11, ALU.logical_shift_right, ALU.logical_shift_left))
    after(v.tensor_tensor(row, part, part2, ALU.bitwise_or))


def by_step(flat, n):
    return flat.rearrange("(b p) f -> p b f", p=P)[:, bass.ds(n * STEP, STEP), :]


def row_to_all(row, n):
    return row[0:1, bass.ds(n * GE, GE)].broadcast_to([P, GE])


def prologue(nc, a, t, keep):
    with ExitStack() as ctx:
        m = Memory(nc, ctx, "pro")
        cur, prev, src = m.sb("cur", [GROUPS, GE], I32), m.sb("prev", [GROUPS, GE], I32), m.sb("src", [GROUPS, GE], I32)
        place, inside = m.sb("place", [GROUPS, GE]), m.sb("inside", [GROUPS, GE])
        same, far, seed = m.sb("same", [GROUPS, GE], BF16), m.sb("far", [GROUPS, GE], BF16), m.sb("seed", [GROUPS, GE], BF16)
        starts, digit = m.sb("starts", [GROUPS, GE]), m.sb("digit", [GROUPS, GE], I32)
        digits = m.sb("digits", [GROUPS, 2, GE], BF16)
        typ, srcg, row3 = m.sb("typ", [P, NT], I32), m.sb("srcg", [P, NT], I32), m.sb("row3", [P, NT], U32)
        firsti, first, junk = m.sb("firsti", [P, NT], I32), m.sb("first", [P, NT]), m.sb("junk", [P, NT])
        nid = m.sb("nid", [P, FB])
        spare = m.sb("spare", [P, NB])
        before, tile_of, within, rs = (m.sb(x, [P, FB]) for x in ("before", "tileof", "within", "rs"))
        tile_ix = m.sb("tileix", [P, FB], U32)
        stage = m.sb("stage", [P, 2, FSTEP], U32)
        rows = m.sb("rows", [P, 2, FSTEP, P], I32)
        junk2 = m.sb("junk2", [P, P])
        rs_next = m.sb("rsnext", [P, NB])
        edge, part, part2 = (m.sb(x, [P, NB], I32) for x in ("edge", "part", "part2"))
        zero = m.sb("zero", [P, TILES * D])
        consts_in, edges_in, more_in = m.sem("consts_in"), m.sem("edges_in"), m.sem("more_in")
        dve, zeroed, stored, rs_out, rs_in = m.sem("dve"), m.sem("zeroed"), m.sem("stored"), m.sem("rs_out"), m.sem("rs_in")
        within_made = m.sem("within_made")
        zero_made, staged, counted = m.sem("zero_made"), m.sem("staged"), m.sem("counted")
        rows_in = [m.sem("rows_in0"), m.sem("rows_in1")]
        rows_ready = m.sem("rows_ready")
        block = ctx.enter_context(nc.Block())
        ROWS_READY = 4
        seeds = t["seeds"]

        @block.sync
        def _(sp):
            for to, of in ((nid, a["nid"]), (spare, a["spare"]), (keep.ident, a["ident"]), (keep.iota, a["iota"]), (keep.eps, a["eps"]), (keep.first_ix, a["dst_first"].rearrange("(g t) -> g t", t=TILES).bitcast(U32))):
                sp.dma_start(to[:, :], of).then_inc(consts_in, 16)
            sp.dma_start(firsti[:, :], a["dst_first"].rearrange("(o t) -> o t", o=1).broadcast_to([P, NT])).then_inc(consts_in, 16)
            sp.dma_start(cur[:, :], a["dst_prev"][1:1 + EP].rearrange("(g e) -> g e", e=GE)).then_inc(edges_in, 16)
            sp.dma_start(prev[:, :], a["dst_prev"][0:EP].rearrange("(g e) -> g e", e=GE)).then_inc(edges_in, 16)
            sp.dma_start(place[:, :], a["place"]).then_inc(edges_in, 16)
            sp.dma_start(inside[:, :], a["inside"]).then_inc(edges_in, 16)
            sp.dma_start(src[:, :], a["src_flat"].rearrange("(g e) -> g e", e=GE)).then_inc(more_in, 16)
            sp.dma_start(typ[:, :], a["typ_grp"].rearrange("(p e) -> p e", p=P)).then_inc(more_in, 16)
            sp.dma_start(srcg[:, :], a["src_grp"].rearrange("(p e) -> p e", p=P)).then_inc(more_in, 16)
            sp.wait_ge(rows_ready, ROWS_READY)
            sp.dma_start(t["same"].rearrange("o (g e) -> (o g) e", e=GE), same[:, :]).then_inc(stored, 16)
            sp.dma_start(t["far"].rearrange("o (g e) -> (o g) e", e=GE), far[:, :]).then_inc(stored, 16)
            sp.dma_start(t["seed"].rearrange("o (g e) -> (o g) e", e=GE), seed[:, :]).then_inc(stored, 16)
            sp.dma_start(t["digits"].rearrange("d (g e) -> g d e", e=GE), digits[:, :, :]).then_inc(stored, 16)
            sp.dma_start(t["row3"].rearrange("(p e) -> p e", p=P), row3[:, :]).then_inc(stored, 16)
            sp.wait_ge(counted, 1)
            with nc.allow_non_contiguous_dma("a node's number per partition"):
                sp.dma_start(t["rs"][0:FB * P].rearrange("(b p) -> p b", p=P), rs[:, :]).then_inc(rs_out, 16)
                sp.wait_ge(rs_out, 16)
                sp.dma_start(rs_next[:, :], t["rs"][1:1 + NP].rearrange("(b p) -> p b", p=P)).then_inc(rs_in, 16)
            sp.wait_ge(stored, 16 * 5)

        @block.scalar
        def _(act):
            act.wait_ge(zero_made, 1)
            with act.Fori(0, GROUPS) as g:
                nc.scalar.dma_start(seeds[bass.ds(g * GE, GE), :].rearrange("(p t) f -> p (t f)", p=P), zero[:, :]).then_inc(zeroed, 16)
            for k in range(ACCS):
                rows_k = (NP + P) // P
                for lo in range(0, rows_k, TILES):
                    w = min(TILES, rows_k - lo)
                    act.dma_start(t[f"acc{k}"].rearrange("(p t) f -> p (t f)", p=P)[:, lo * D:(lo + w) * D], zero[:, 0:w * D]).then_inc(zeroed, 16)
            act.wait_ge(zeroed, 16 * (GROUPS + ACCS * -(-((NP + P) // P) // TILES)))

        @block.gpsimd
        def _(pool):
            def gather(n, h, k):
                pool_wait(pool, staged, made(n))
                for c in range(FSTEP):
                    pool.indirect_dma_start(out=rows[:, h, c, :], out_offset=None, in_=a["dst_tiles"][:, :], in_offset=bass.IndirectOffsetOnAxis(ap=stage[:, h, c:c + 1], axis=0)).then_inc(rows_in[h], 16)

            skewed(pool, FB // FSTEP, gather, lambda n, h, k: None)

        @block.vector
        def _(v):
            steps = 0

            def after(ins):
                nonlocal steps
                ins.then_inc(dve, 1)
                steps += 1
                v.wait_ge(dve, steps)

            v.memset(zero[:, :], 0.0).then_inc(zero_made, 1)
            v.wait_ge(edges_in, 16 * 4)
            after(v.tensor_tensor(same[:, :], cur[:, :], prev[:, :], ALU.is_equal))
            v.tensor_scalar(far[:, :], same[:, :], -1.0, FAR, ALU.add, ALU.mult).then_inc(rows_ready, 1)
            after(v.tensor_scalar(starts[:, :], same[:, :], -1.0, 1.0, ALU.mult, ALU.add))
            after(v.tensor_tensor(starts[:, :], starts[:, :], place[:, :], ALU.mult))
            v.tensor_tensor_scan(seed[:, :], inside[:, :], starts[:, :], 0.0, ALU.mult, ALU.max).then_inc(rows_ready, 1)
            v.wait_ge(more_in, 16 * 3)
            after(v.tensor_scalar(digit[:, :], src[:, :], 7, None, ALU.logical_shift_right))
            after(v.tensor_copy(digits[:, 0, :], digit[:, :]))
            after(v.tensor_scalar(digit[:, :], src[:, :], P - 1, None, ALU.bitwise_and))
            v.tensor_copy(digits[:, 1, :], digit[:, :]).then_inc(rows_ready, 1)
            v.scalar_tensor_tensor(row3[:, :], typ[:, :], float(NP), srcg[:, :], ALU.mult, ALU.add).then_inc(rows_ready, 1)
            v.wait_ge(consts_in, 16 * 7)
            after(v.tensor_copy(first[:, :], firsti[:, :]))
            for b in range(FB):
                after(v.tensor_scalar(junk[:, :], first[:, :], nid[:, b:b + 1], 0.0, ALU.is_lt, ALU.add, accum_out=before[:, b:b + 1]))
            after(v.tensor_scalar(tile_of[:, :], before[:, :], -1.0, 0.0, ALU.add, ALU.max))
            after(v.tensor_copy(tile_ix[:, :], tile_of[:, :]))

            def to_stage(n, h, k):
                if any_yet(landed_before(k, FSTEP)):
                    v.wait_ge(rows_in[h], landed_before(k, FSTEP))
                v.tensor_copy(stage[:, h, :], tile_ix[:, bass.ds(n * FSTEP, FSTEP)]).then_inc(staged, 1)

            def count(n, h, k):
                v.wait_ge(rows_in[h], landed(k, FSTEP))
                for c in range(FSTEP):
                    counted_one = v.tensor_scalar(junk2[:, :], rows[:, h, c, :], nid[:, bass.ds(n * FSTEP + c, 1)], 0.0, ALU.is_lt, ALU.add, accum_out=within[:, bass.ds(n * FSTEP + c, 1)])
                    counted_one.then_inc(within_made, 1)
                    v.wait_ge(within_made, FSTEP * n + c + 1)

            skewed(v, FB // FSTEP, to_stage, count)
            v.scalar_tensor_tensor(rs[:, :], tile_of[:, :], float(P), within[:, :], ALU.mult, ALU.add).then_inc(counted, 1)
            v.wait_ge(rs_in, 16)
            v.wait_ge(counted, 1)
            after(v.tensor_tensor(keep.has[:, :], rs_next[:, :], rs[:, 0:NB], ALU.is_gt))
            after(v.tensor_scalar(edge[:, :], rs_next[:, :], -1.0, 0.0, ALU.add, ALU.max))
            edge_row(v, after, keep.last_ix[:, :].bitcast(I32), edge[:, :], part[:, :], part2[:, :])
            after(v.tensor_copy(edge[:, :], rs[:, 0:NB]))
            edge_row(v, after, part[:, :], edge[:, :], part[:, :], part2[:, :])
            after(v.tensor_copy(rs_next[:, :], part[:, :]))
            after(v.tensor_tensor(rs_next[:, :], rs_next[:, :], spare[:, :], ALU.subtract))
            after(v.tensor_tensor(rs_next[:, :], rs_next[:, :], keep.has[:, :], ALU.mult))
            after(v.tensor_tensor(keep.seed_ix[:, :], rs_next[:, :], spare[:, :], ALU.add))


def seed_tiles(nc, t, keep, phase):
    with ExitStack() as ctx:
        m = Memory(nc, ctx, phase)
        rows = m.sb("rows", [GROUPS, TILES, D])
        gathered, stored = m.sem("gathered"), m.sem("stored")
        block = ctx.enter_context(nc.Block())
        firsts = t["seeds"][0:EP, :].rearrange("(g p t) f -> g p t f", p=P, t=TILES)[:, 0, :, :]

        @block.gpsimd
        def _(pool):
            for c in range(TILES):
                pool.indirect_dma_start(out=rows[:, c, :], out_offset=None, in_=t["nodes"][:, :], in_offset=bass.IndirectOffsetOnAxis(ap=keep.first_ix[:, c:c + 1], axis=0)).then_inc(gathered, 16)

        @block.sync
        def _(sp):
            sp.wait_ge(gathered, 16 * TILES)
            sp.dma_start(firsts, rows[:, :, :]).then_inc(stored, 16)
            sp.wait_ge(stored, 16)


def node_phase(nc, a, t, keep, layer, out):
    ins = [["x"], ["x", "acc0", "acc1", "acc2", "acc3"], ["own", "upd"], ["own"], ["own"]][layer]
    cat = [D, 4 * D, 4 * D, 5 * D, 0][layer]
    own = [None, 2 * D, 3 * D, 4 * D, None][layer]
    seeded = [0, D, 2 * D, None, None][layer]
    outs = [[("nodes", 0, D)],
            [("a1", 0, D), ("nodes", D, D), ("own", 2 * D, D), ("upd", 3 * D, D)],
            [("kv", 0, 2 * D), ("nodes", 2 * D, D), ("own", 3 * D, D)],
            [("rel0", 0, D), ("rel1", D, D), ("rel2", 2 * D, D), ("rel3", 3 * D, D), ("own", 4 * D, D)],
            []][layer]
    got = [0, 0, D, TW, D][layer]
    norm = layer > 0
    if layer in (2, 3, 4):
        ins = [f"own{layer - 1}" if x == "own" else x for x in ins]
    outs = [(f"own{layer}" if x == "own" else x, c, w) for x, c, w in outs]
    with ExitStack() as ctx:
        m = Memory(nc, ctx, f"node{layer}")
        xin = [m.sb(f"in_{x}", [P, 2, STEP, D]) for x in ins]
        xh = m.sb("xh", [P, 2, STEP, D])
        ixs = m.sb("ixs", [P, 2, 2 * STEP], U32)
        if got:
            res = m.sb("res", [P, 2, STEP, got])
            resT = m.sb("resT", [P, STEP * P])
        if norm:
            stats, mv = m.sb("stats", [P, STEP, 6]), m.sb("mv", [P, STEP, 2])
            dev, inv = m.sb("dev", [P, STEP]), m.sb("inv", [P, STEP])
        if layer == 2:
            wupd = m.sb("wupd", [P, D])
            upd_ps = m.ps("upd_ps", [P, 1024])
        if layer == 3:
            den = m.sb("den", [P, STEP, HEADS])
        if cat:
            w, bias = m.sb("w", [P, cat]), m.sb("bias", [P, cat])
            xT = m.sb("xT", [P, 2, STEP * P])
            res_out = m.sb("out", [P, 2, STEP, cat])
            mm_ps = [m.ps(f"mm{i}", [P, 1024]) for i in range(2)]
        tr_ps = m.ps("tr", [P, 1024])
        weights_in = m.sem("weights_in")
        in_landed = [m.sem("in_landed0"), m.sem("in_landed1")]
        res_landed = [m.sem("res_landed0"), m.sem("res_landed1")]
        out_landed = [m.sem("out_landed0"), m.sem("out_landed1")]
        seeds_landed = [m.sem("seeds_landed0"), m.sem("seeds_landed1")]
        staged, xh_made, tr_made, xT_made = (m.sem(x) for x in ("staged", "xh_made", "tr_made", "xT_made"))
        mm_made, mm_used, dev_made, mv_made, dve = (m.sem(x) for x in ("mm_made", "mm_used", "dev_made", "mv_made", "dve"))
        pre_made, preT_made, upd_made, res_masked = (m.sem(x) for x in ("pre_made", "preT_made", "upd_made", "res_masked"))
        block = ctx.enter_context(nc.Block())
        n_out = len(outs) if outs else 1
        n_weights = (2 if cat else 0) + (layer == 2)
        nothing = lambda n, h, k: None

        @block.sync
        def _(sp):
            if cat:
                sp.dma_start(w[:, :], a[f"w{layer}"]).then_inc(weights_in, 16)
                sp.dma_start(bias[:, :], a[f"b{layer}"].rearrange("(o c) -> o c", o=1).broadcast_to([P, cat])).then_inc(weights_in, 16)
            if layer == 2:
                sp.dma_start(wupd[:, :], a["w_upd"]).then_inc(weights_in, 16)

            def load(n, h, k):
                if any_yet(free(n)):
                    sp.wait_ge(xh_made, free(n))
                for x, to in zip(ins, xin):
                    sp.dma_start(to[:, h, :, :], by_step(t[x], n)).then_inc(in_landed[h], 16)

            def store(n, h, k):
                if cat:
                    sp.wait_ge(mm_used, STEP * (n + 1))
                    for x, c, wd in outs:
                        sp.dma_start(by_step(t[x], n), res_out[:, h, :, c:c + wd]).then_inc(out_landed[h], 16)
                else:
                    sp.wait_ge(xh_made, made(n))
                    sp.dma_start(by_step(out, n), xh[:, h, :, :]).then_inc(out_landed[h], 16)

            skewed(sp, STEPS, load, store)
            for h in range(2):
                sp.wait_ge(out_landed[h], landed(STEPS // 2 - 1, n_out))

        @block.gpsimd
        def _(pool):
            table = {2: "sum1", 3: "sum2", 4: "max3"}.get(layer)

            def gather(n, h, k):
                pool_wait(pool, staged, made(n))
                if any_yet(free(n)):
                    pool_wait(pool, xh_made, free(n))
                for b in range(STEP):
                    pool.indirect_dma_start(out=res[:, h, b, :], out_offset=None, in_=t[table][:, :], in_offset=bass.IndirectOffsetOnAxis(ap=ixs[:, h, b:b + 1], axis=0)).then_inc(res_landed[h], 16)

            def scatter(n, h, k):
                pool_wait(pool, staged, made(n))
                pool_wait(pool, mm_used, STEP * (n + 1))
                for b in range(STEP):
                    pool.indirect_dma_start(out=t["seeds"][:, :], out_offset=bass.IndirectOffsetOnAxis(ap=ixs[:, h, STEP + b:STEP + b + 1], axis=0), in_=res_out[:, h, b, seeded:seeded + D], in_offset=None).then_inc(seeds_landed[h], 16)

            skewed(pool, STEPS, gather if got else nothing, scatter if seeded is not None else nothing)
            if seeded is not None:
                for h in range(2):
                    pool_wait(pool, seeds_landed[h], landed(STEPS // 2 - 1, STEP))

        @block.tensor
        def _(pe):
            if n_weights:
                pe.wait_ge(weights_in, 16 * n_weights)

            def front(n, h, k):
                if layer == 2:
                    pe.wait_ge(res_masked, made(n))
                    if any_yet(made(n - 1)):
                        pe.wait_ge(xT_made, made(n - 1))
                    for b in range(STEP):
                        mm = pe.transpose(tr_ps[:, b * P:(b + 1) * P], res[:, h, b, :], keep.ident[:, :])
                    mm.then_inc(pre_made, 1)
                    pe.wait_ge(preT_made, made(n))
                    for b in range(STEP):
                        mm = pe.matmul(upd_ps[:, b * P:(b + 1) * P], resT[:, b * P:(b + 1) * P], wupd[:, :], start=True, stop=True)
                    mm.then_inc(upd_made, 1)
                pe.wait_ge(xh_made, made(n))
                if any_yet(made(n - 1)):
                    pe.wait_ge(xT_made, made(n - 1))
                for b in range(STEP):
                    mm = pe.transpose(tr_ps[:, b * P:(b + 1) * P], xh[:, h, b, :], keep.ident[:, :])
                mm.then_inc(tr_made, 1)

            def back(n, h, k):
                pe.wait_ge(xT_made, made(n))
                for b in range(STEP):
                    if any_yet(STEP * n + b - 1):
                        pe.wait_ge(mm_used, STEP * n + b - 1)
                    slot = mm_ps[(h * STEP + b) % 2]
                    rows = xT[:, h, b * P:(b + 1) * P]
                    mm = pe.matmul(slot[:, 0:min(cat, 512)], rows, w[:, 0:min(cat, 512)], start=True, stop=own is None or own >= 512)
                    if own is not None and own < 512:
                        mm = pe.matmul(slot[:, own:own + D], rows, keep.ident[:, :], start=False, stop=True)
                    if cat > 512:
                        pe.matmul(slot[:, 512:cat], rows, w[:, 512:cat], start=True, stop=False)
                        mm = pe.matmul(slot[:, own:own + D], rows, keep.ident[:, :], start=False, stop=True)
                    mm.then_inc(mm_made, 1)

            if cat:
                skewed(pe, STEPS, front, back)

        @block.scalar
        def _(act):

            def front(n, h, k):
                if layer == 2:
                    act.wait_ge(pre_made, made(n))
                    if any_yet(made(n - 1)):
                        act.wait_ge(upd_made, made(n - 1))
                    act.copy(resT[:, :], tr_ps[:, 0:STEP * P]).then_inc(preT_made, 1)
                if norm:
                    act.wait_ge(mv_made, made(n))
                    act.activation(dev[:, :], mv[:, :, 1], ACT.Sqrt, bias=keep.eps[:, :]).then_inc(dev_made, 1)
                if cat:
                    act.wait_ge(tr_made, made(n))
                    if any_yet(STEP * free(n)):
                        act.wait_ge(mm_made, STEP * free(n))
                    act.copy(xT[:, h, :], tr_ps[:, 0:STEP * P]).then_inc(xT_made, 1)

            skewed(act, STEPS, front, nothing)

        @block.vector
        def _(v):
            if cat:
                v.wait_ge(weights_in, 16 * n_weights)
            chain = {0: 0, 1: 6, 2: 4, 3: 7, 4: 4}[layer]
            done = 0

            def after(ins, n):
                nonlocal done
                ins.then_inc(dve, 1)
                done += 1
                v.wait_ge(dve, chain * n + done)

            def front(n, h, k):
                nonlocal done
                done = 0
                if seeded is not None:
                    if any_yet(landed_before(k, STEP)):
                        v.wait_ge(seeds_landed[h], landed_before(k, STEP))
                if got or seeded is not None:
                    if got:
                        if any_yet(landed_before(k, STEP)):
                            v.wait_ge(res_landed[h], landed_before(k, STEP))
                    v.tensor_copy(ixs[:, h, 0:STEP], keep.last_ix[:, bass.ds(n * STEP, STEP)])
                    v.tensor_copy(ixs[:, h, STEP:], keep.seed_ix[:, bass.ds(n * STEP, STEP)]).then_inc(staged, 1)
                v.wait_ge(in_landed[h], landed(k, len(ins)))
                if got:
                    v.wait_ge(res_landed[h], landed(k, STEP))
                    has = keep.has[:, bass.ds(n * STEP, STEP)]
                y = xin[0][:, h, :, :]
                if layer == 0:
                    if any_yet(free(n)):
                        v.wait_ge(tr_made, free(n))
                    v.tensor_copy(xh[:, h, :, :], y).then_inc(xh_made, 1)
                    return
                if layer == 1:
                    for other in xin[1:]:
                        after(v.tensor_tensor(y, y, other[:, h, :, :], ALU.add), n)
                if layer in (2, 4):
                    masked = v.tensor_tensor(res[:, h, :, :], res[:, h, :, :], has.unsqueeze(2).broadcast_to([P, STEP, D]), ALU.mult)
                if layer == 2:
                    masked.then_inc(res_masked, 1)
                    z = xin[1][:, h, :, :]
                    v.wait_ge(upd_made, made(n))
                    after(v.tensor_tensor(z, z, upd_ps[:, 0:STEP * P].rearrange("p (b f) -> p b f", f=D), ALU.add), n)
                    after(v.scalar_tensor_tensor(y, z, 0.0, y, ALU.max, ALU.add), n)
                if layer == 3:
                    after(v.tensor_scalar(den[:, :, :], res[:, h, :, D:TW], 1.0, None, ALU.max), n)
                    after(v.reciprocal(den[:, :, :], den[:, :, :]), n)
                    after(v.tensor_tensor(den[:, :, :], den[:, :, :], has.unsqueeze(2).broadcast_to([P, STEP, HEADS]), ALU.mult), n)
                    num = res[:, h, :, 0:D].rearrange("p b (a c) -> p b a c", c=HC)
                    after(v.tensor_tensor(num, num, den[:, :, :].unsqueeze(3).broadcast_to([P, STEP, HEADS, HC]), ALU.mult), n)
                    after(v.tensor_tensor(y, y, res[:, h, :, 0:D], ALU.add), n)
                if layer == 4:
                    after(masked, n)
                    after(v.tensor_tensor(y, y, res[:, h, :, :], ALU.add), n)
                for b in range(STEP):
                    st = v.bn_stats(stats[:, b, :], y[:, b, :])
                after(st, n)
                if any_yet(made(n - 1)):
                    v.wait_ge(dev_made, made(n - 1))
                v.nop(nofuse=True)
                for b in range(STEP):
                    ag = v.bn_aggr(mv[:, b, :], stats[:, b, :])
                ag.then_inc(mv_made, 1)
                v.wait_ge(dev_made, made(n))
                after(v.reciprocal(inv[:, :], dev[:, :]), n)
                if cat:
                    if any_yet(free(n)):
                        v.wait_ge(tr_made, free(n))
                else:
                    if any_yet(landed_before(k, n_out)):
                        v.wait_ge(out_landed[h], landed_before(k, n_out))
                for b in range(STEP):
                    last = v.tensor_scalar(xh[:, h, b, :], y[:, b, :], mv[:, b, 0:1], inv[:, b:b + 1], ALU.subtract, ALU.mult)
                last.then_inc(xh_made, 1)
                assert done == chain, (layer, done)

            def back(n, h, k):
                if any_yet(landed_before(k, n_out)):
                    v.wait_ge(out_landed[h], landed_before(k, n_out))
                if seeded is not None:
                    if any_yet(landed_before(k, STEP)):
                        v.wait_ge(seeds_landed[h], landed_before(k, STEP))
                for b in range(STEP):
                    v.wait_ge(mm_made, STEP * n + b + 1)
                    v.tensor_tensor(res_out[:, h, b, :], mm_ps[(h * STEP + b) % 2][:, 0:cat], bias[:, :], ALU.add).then_inc(mm_used, 1)

            skewed(v, STEPS, front, back if cat else nothing)


def edges_sum0(nc, a, t, keep):
    with ExitStack() as ctx:
        m = Memory(nc, ctx, "edge0")
        seeds, seed = m.sb("seeds", [P, 2, TILES, D]), m.sb("seed", [P, 2, GE], BF16)
        spread = m.sb("spread", [P, 2, GE])
        digits, srci, w = m.sb("digits", [2, 2, GE], BF16), m.sb("srci", [P, 2, TILES], I32), m.sb("w", [P, 2, TILES])
        srcf, dup, flag, ix = m.sb("srcf", [P, 2, TILES]), m.sb("dup", [P, TILES]), m.sb("flag", [P, TILES]), m.sb("ix", [P, 2, TILES], U32)
        away = m.sb("away", [P, TILES])
        lower, trash = m.sb("lower", [P, P]), m.sb("trash", [P, 1])
        place_value_in, place_value = m.sb("place_value_in", [2, P]), m.sb("place_value", [2, P], BF16)
        equal, masked = m.sb("equal", [P, 2, QUAD, P]), m.sb("masked", [P, QUAD, P])
        weighted, sums = m.sb("weighted", [P, 2, QUAD, D]), m.sb("sums", [P, 2, TILES, D])
        src_ps, row_ps, sum_ps = ([m.ps(f"{x}{i}", [P, QE]) for i in range(2)] for x in ("src", "row", "sum"))
        consts_in, place_value_made = m.sem("consts_in"), m.sem("place_value_made")
        edges_in = [m.sem("edges_in0"), m.sem("edges_in1")]
        spread_made, src_made, equal_made, row_made, weighted_made, sum_made, sums_made, ix_made, dve = (
            m.sem(x) for x in ("spread_made", "src_made", "equal_made", "row_made", "weighted_made", "sum_made", "sums_made", "ix_made", "dve"))
        added = [m.sem(f"added{k}") for k in range(ACCS)]
        block = ctx.enter_context(nc.Block())
        PER_ACC = TILES // ACCS
        nothing = lambda n, h, k: None

        @block.sync
        def _(sp):
            for to, of in ((lower, a["lower"]), (trash, a["trash"]), (place_value_in, a["place_value"])):
                sp.dma_start(to[:, :], of).then_inc(consts_in, 16)

            def load(n, h, k):
                if any_yet(QUADS * free(n)):
                    sp.wait_ge(weighted_made, QUADS * free(n))
                if any_yet(free(n)):
                    sp.wait_ge(ix_made, free(n))
                sp.dma_start(seeds[:, h, :, :].rearrange("p t f -> p (t f)"), by_group(t["seeds"][0:EP, :], n)).then_inc(edges_in[h], 16)
                sp.dma_start(seed[:, h, :], row_to_all(t["seed"], n)).then_inc(edges_in[h], 16)
                sp.dma_start(digits[:, h, :], t["digits"][:, bass.ds(n * GE, GE)]).then_inc(edges_in[h], 16)
                sp.dma_start(srci[:, h, :], a["src_grp"].rearrange("(g p e) -> p g e", p=P, e=TILES)[:, bass.ds(n, 1), :].rearrange("p o e -> p (o e)")).then_inc(edges_in[h], 16)
                sp.dma_start(w[:, h, :], a["w_grp"].rearrange("(g p e) -> p g e", p=P, e=TILES)[:, bass.ds(n, 1), :].rearrange("p o e -> p (o e)")).then_inc(edges_in[h], 16)

            skewed(sp, GROUPS, load, nothing)

        @block.gpsimd
        def _(pool):

            def add(n, h, k):
                pool_wait(pool, ix_made, made(n))
                for j in range(QUADS):
                    pool_wait(pool, sums_made, QUADS * n + j + 1)
                    for c in range(QUAD):
                        e = j * QUAD + c
                        if any_yet(16 * (PER_ACC * n + e // ACCS)):
                            pool_wait(pool, added[e % ACCS], 16 * (PER_ACC * n + e // ACCS))
                        pool.indirect_dma_start(out=t[f"acc{e % ACCS}"][:, :], out_offset=bass.IndirectOffsetOnAxis(ap=ix[:, h, e:e + 1], axis=0), in_=sums[:, h, e, :], in_offset=None, compute_op=ALU.add).then_inc(added[e % ACCS], 16)

            skewed(pool, GROUPS, nothing, add)
            for k in range(ACCS):
                pool_wait(pool, added[k], 16 * PER_ACC * GROUPS)

        @block.tensor
        def _(pe):
            pe.wait_ge(place_value_made, 1)

            def group(n, h, k):
                def spread_quad(j):
                    q = QUADS * n + j
                    cols = slice(j * QE, (j + 1) * QE)
                    if any_yet(free(q)):
                        pe.wait_ge(equal_made, free(q))
                    pe.matmul(src_ps[j % 2][:, :], place_value[:, :], digits[:, h, cols], start=True, stop=True).then_inc(src_made, 1)
                    if any_yet(q - 1):
                        pe.wait_ge(weighted_made, q - 1)
                    for c in range(QUAD):
                        e = j * QUAD + c
                        mm = pe.matmul(row_ps[j % 2][:, c * D:(c + 1) * D], spread[:, h, e * P:(e + 1) * P], seeds[:, h, e, :], start=True, stop=True)
                    mm.then_inc(row_made, 1)

                def sum_quad(j):
                    q = QUADS * n + j
                    pe.wait_ge(equal_made, made(q))
                    pe.wait_ge(weighted_made, q + 1)
                    if any_yet(q - 1):
                        pe.wait_ge(sums_made, q - 1)
                    for c in range(QUAD):
                        mm = pe.matmul(sum_ps[j % 2][:, c * D:(c + 1) * D], equal[:, j % 2, c, :], weighted[:, j % 2, c, :], start=True, stop=True)
                    mm.then_inc(sum_made, 1)

                pe.wait_ge(edges_in[h], landed(k, 5))
                pe.wait_ge(spread_made, made(n))
                spread_quad(0)
                for j in range(1, QUADS):
                    spread_quad(j)
                    sum_quad(j - 1)
                sum_quad(QUADS - 1)

            skewed(pe, GROUPS, nothing, group)

        @block.scalar
        def _(act):

            def group(n, h, k):
                def weigh(j):
                    q = QUADS * n + j
                    act.wait_ge(row_made, q + 1)
                    if any_yet(free(q)):
                        act.wait_ge(sum_made, free(q))
                    for c in range(QUAD):
                        e = j * QUAD + c
                        ins = act.activation(weighted[:, j % 2, c, :], row_ps[j % 2][:, c * D:(c + 1) * D], ACT.Copy, scale=w[:, h, e:e + 1])
                    ins.then_inc(weighted_made, 1)

                def out(j):
                    act.wait_ge(sum_made, made(QUADS * n + j))
                    act.copy(sums[:, h, j * QUAD:(j + 1) * QUAD, :], sum_ps[j % 2][:, :].rearrange("p (c f) -> p c f", f=D)).then_inc(sums_made, 1)

                act.wait_ge(edges_in[h], landed(k, 5))
                weigh(0)
                for s in added:
                    if any_yet(16 * PER_ACC * free(n)):
                        act.wait_ge(s, 16 * PER_ACC * free(n))
                for j in range(1, QUADS):
                    weigh(j)
                    out(j - 1)
                out(QUADS - 1)

            skewed(act, GROUPS, nothing, group)

        @block.vector
        def _(v):
            v.wait_ge(consts_in, 16 * 3)
            v.tensor_copy(place_value[:, :], place_value_in[:, :]).then_inc(place_value_made, 1)
            CHAIN = 2 * QUADS + 3

            def spread_group(n, h, k):
                v.wait_ge(edges_in[h], landed(k, 5))
                if any_yet(QUADS * free(n)):
                    v.wait_ge(row_made, QUADS * free(n))
                v.tensor_copy(srcf[:, h, :], srci[:, h, :])
                v.tensor_scalar(spread[:, h, :], seed[:, h, :], keep.iota[:, 0:1], None, ALU.is_equal).then_inc(spread_made, 1)

            def compare(n, h, k):
                done = 0

                def after(ins):
                    nonlocal done
                    ins.then_inc(dve, 1)
                    done += 1
                    v.wait_ge(dve, CHAIN * n + done)

                v.wait_ge(spread_made, made(n))
                after(v.tensor_scalar(away[:, :], srcf[:, h, :], -1.0, trash[:, 0:1], ALU.mult, ALU.add))
                for j in range(QUADS):
                    q = QUADS * n + j
                    v.wait_ge(src_made, q + 1)
                    if any_yet(free(q)):
                        v.wait_ge(sum_made, free(q))
                    own = srcf[:, h, j * QUAD:(j + 1) * QUAD].unsqueeze(2).broadcast_to([P, QUAD, P])
                    v.tensor_tensor(equal[:, j % 2, :, :], src_ps[j % 2][:, :].rearrange("p (c f) -> p c f", f=P), own, ALU.is_equal).then_inc(equal_made, 1)
                    v.wait_ge(equal_made, made(q))
                    after(v.tensor_tensor(masked[:, :, :], equal[:, j % 2, :, :], lower[:, :].unsqueeze(1).broadcast_to([P, QUAD, P]), ALU.mult))
                    after(v.tensor_reduce(dup[:, j * QUAD:(j + 1) * QUAD], masked[:, :, :], AX.X, ALU.add))
                after(v.tensor_scalar(flag[:, :], dup[:, :], 0.0, None, ALU.is_gt))
                after(v.tensor_tensor(flag[:, :], flag[:, :], away[:, :], ALU.mult))
                for s in added:
                    if any_yet(16 * PER_ACC * free(n)):
                        v.wait_ge(s, 16 * PER_ACC * free(n))
                v.tensor_tensor(ix[:, h, :], flag[:, :], srcf[:, h, :], ALU.add).then_inc(ix_made, 1)
                assert done == CHAIN

            skewed(v, GROUPS, spread_group, compare)


def edges_sum1(nc, a, t, keep):
    with ExitStack() as ctx:
        m = Memory(nc, ctx, "edge1")
        seeds, seed, same = m.sb("seeds", [P, 2, TILES, D]), m.sb("seed", [P, 2, GE], BF16), m.sb("same", [P, 2, GE], BF16)
        dist, w_dist, ix = m.sb("dist", [1, 2, GE]), m.sb("w_dist", [1, D]), m.sb("ix", [P, 2, TILES], U32)
        spread, rows = m.sb("spread", [P, 2, GE]), m.sb("rows", [P, 2, TILES, D])
        msg, run = m.sb("msg", [P, 2, QE]), m.sb("run", [P, 2, QE])
        out = m.sb("out", [P, 2, TILES, D])
        msg_ps, turn_ps = ([m.ps(f"{x}{i}", [P, QE]) for i in range(2)] for x in ("msg", "turn"))
        consts_in = m.sem("consts_in")
        edges_in, ix_in, rows_in, stored = ([m.sem(f"{x}{i}") for i in range(2)] for x in ("edges_in", "ix_in", "rows_in", "stored"))
        spread_made, pre_made, msg_made, run_made, turned, out_made, zeroed = (m.sem(x) for x in ("spread_made", "pre_made", "msg_made", "run_made", "turned", "out_made", "zeroed"))
        block = ctx.enter_context(nc.Block())
        EDGE_DMAS = 4
        nothing = lambda n, h, k: None

        @block.sync
        def _(sp):
            sp.dma_start(w_dist[:, :], a["w_dist"]).then_inc(consts_in, 16)

            def load(n, h, k):
                if any_yet(landed_before(k, TILES)):
                    sp.wait_ge(rows_in[h], landed_before(k, TILES))
                sp.dma_start(ix[:, h, :], a["src_grp"].bitcast(U32).rearrange("(g p e) -> p g e", p=P, e=TILES)[:, bass.ds(n, 1), :].rearrange("p o e -> p (o e)")).then_inc(ix_in[h], 16)
                if any_yet(QUADS * free(n)):
                    sp.wait_ge(run_made, QUADS * free(n))
                sp.dma_start(seeds[:, h, :, :].rearrange("p t f -> p (t f)"), by_group(t["seeds"][0:EP, :], n)).then_inc(edges_in[h], 16)
                sp.dma_start(seed[:, h, :], row_to_all(t["seed"], n)).then_inc(edges_in[h], 16)
                sp.dma_start(same[:, h, :], row_to_all(t["same"], n)).then_inc(edges_in[h], 16)
                sp.dma_start(dist[:, h, :], a["ed_row"][:, bass.ds(n * GE, GE)]).then_inc(edges_in[h], 16)

            def store(n, h, k):
                sp.wait_ge(out_made, QUADS * made(n))
                sp.dma_start(by_group(t["sum1"], n), out[:, h, :, :].rearrange("p t f -> p (t f)")).then_inc(stored[h], 16)

            skewed(sp, GROUPS, load, store)
            for h in range(2):
                sp.wait_ge(stored[h], landed(GROUPS // 2 - 1, 1))

        @block.gpsimd
        def _(pool):
            def gather(n, h, k):
                pool_wait(pool, ix_in[h], landed(k, 1))
                if any_yet(QUADS * free(n)):
                    pool_wait(pool, pre_made, QUADS * free(n))
                for e in range(TILES):
                    pool.indirect_dma_start(out=rows[:, h, e, :], out_offset=None, in_=t["a1"][:, :], in_offset=bass.IndirectOffsetOnAxis(ap=ix[:, h, e:e + 1], axis=0)).then_inc(rows_in[h], 16)

            skewed(pool, GROUPS, gather, nothing)

        @block.tensor
        def _(pe):
            pe.wait_ge(consts_in, 16)

            def group(n, h, k):
                def sum_quad(j):
                    q = QUADS * n + j
                    ps = msg_ps[j % 2]
                    if any_yet(free(q)):
                        pe.wait_ge(msg_made, free(q))
                    pe.matmul(ps[:, :], w_dist[:, :], dist[:, h, j * QE:(j + 1) * QE], start=True, stop=False)
                    for c in range(QUAD):
                        e = j * QUAD + c
                        cols = ps[:, c * P:(c + 1) * P]
                        pe.matmul(cols, seeds[:, h, e, :], spread[:, h, e * P:(e + 1) * P], start=False, stop=False)
                        mm = pe.matmul(cols, rows[:, h, e, :], keep.ident[:, :], start=False, stop=c == QUAD - 1)
                    mm.then_inc(pre_made, 1)

                def turn_quad(j):
                    q = QUADS * n + j
                    pe.wait_ge(run_made, made(q))
                    if any_yet(free(q)):
                        pe.wait_ge(out_made, free(q))
                    for c in range(QUAD):
                        mm = pe.transpose(turn_ps[j % 2][:, c * P:(c + 1) * P], run[:, j % 2, c * P:(c + 1) * P], keep.ident[:, :])
                    mm.then_inc(turned, 1)

                pe.wait_ge(edges_in[h], landed(k, EDGE_DMAS))
                pe.wait_ge(spread_made, made(n))
                pe.wait_ge(rows_in[h], landed(k, TILES))
                sum_quad(0)
                for j in range(1, QUADS):
                    sum_quad(j)
                    turn_quad(j - 1)
                turn_quad(QUADS - 1)

            skewed(pe, GROUPS, nothing, group)

        @block.scalar
        def _(act):
            def group(n, h, k):
                def relu(j):
                    q = QUADS * n + j
                    act.wait_ge(pre_made, made(q))
                    if any_yet(free(q)):
                        act.wait_ge(run_made, free(q))
                    act.activation(msg[:, j % 2, :], msg_ps[j % 2][:, :], ACT.Relu).then_inc(msg_made, 1)

                def copy_out(j):
                    act.wait_ge(turned, made(QUADS * n + j))
                    act.copy(out[:, h, j * QUAD:(j + 1) * QUAD, :], turn_ps[j % 2][:, :].rearrange("p (c f) -> p c f", f=D)).then_inc(out_made, 1)

                relu(0)
                if any_yet(landed_before(k, 1)):
                    act.wait_ge(stored[h], landed_before(k, 1))
                for j in range(1, QUADS):
                    relu(j)
                    copy_out(j - 1)
                copy_out(QUADS - 1)

            skewed(act, GROUPS, nothing, group)

        @block.vector
        def _(v):
            v.memset(run[:, 1, QE - 1:QE], 0.0).then_inc(zeroed, 1)
            v.wait_ge(zeroed, 1)

            def spread_group(n, h, k):
                v.wait_ge(edges_in[h], landed(k, EDGE_DMAS))
                if any_yet(QUADS * free(n)):
                    v.wait_ge(pre_made, QUADS * free(n))
                v.tensor_scalar(spread[:, h, :], seed[:, h, :], keep.iota[:, 0:1], None, ALU.is_equal).then_inc(spread_made, 1)

            def scan(n, h, k):
                for j in range(QUADS):
                    q = QUADS * n + j
                    v.wait_ge(msg_made, made(q))
                    if any_yet(free(q)):
                        v.wait_ge(turned, free(q))
                    if any_yet(made(q - 1)):
                        v.wait_ge(run_made, made(q - 1))
                    v.tensor_tensor_scan(run[:, j % 2, :], same[:, h, j * QE:(j + 1) * QE], msg[:, j % 2, :], run[:, (j - 1) % 2, QE - 1:QE], ALU.mult, ALU.add).then_inc(run_made, 1)

            skewed(v, GROUPS, spread_group, scan)


def edges_max3(nc, a, t, keep):
    with ExitStack() as ctx:
        m = Memory(nc, ctx, "edge3")
        far, ix = m.sb("far", [P, 2, GE], BF16), m.sb("ix", [P, 2, TILES], U32)
        rows, run, out = m.sb("rows", [P, 2, TILES, D]), m.sb("run", [P, 2, QE]), m.sb("out", [P, 2, TILES, D])
        in_ps, turn_ps = ([m.ps(f"{x}{i}", [P, QE]) for i in range(2)] for x in ("in", "turn"))
        edges_in, ix_in, rows_in, stored = ([m.sem(f"{x}{i}") for i in range(2)] for x in ("edges_in", "ix_in", "rows_in", "stored"))
        turned_in, run_made, turned, out_made, zeroed = (m.sem(x) for x in ("turned_in", "run_made", "turned", "out_made", "zeroed"))
        block = ctx.enter_context(nc.Block())
        nothing = lambda n, h, k: None

        @block.sync
        def _(sp):
            def load(n, h, k):
                if any_yet(landed_before(k, TILES)):
                    sp.wait_ge(rows_in[h], landed_before(k, TILES))
                sp.dma_start(ix[:, h, :], t["row3"].rearrange("(g p e) -> p g e", p=P, e=TILES)[:, bass.ds(n, 1), :].rearrange("p o e -> p (o e)")).then_inc(ix_in[h], 16)
                if any_yet(QUADS * free(n)):
                    sp.wait_ge(run_made, QUADS * free(n))
                sp.nop(nofuse=True)
                sp.dma_start(far[:, h, :], row_to_all(t["far"], n)).then_inc(edges_in[h], 16)

            def store(n, h, k):
                sp.wait_ge(out_made, QUADS * made(n))
                sp.dma_start(by_group(t["max3"], n), out[:, h, :, :].rearrange("p t f -> p (t f)")).then_inc(stored[h], 16)

            skewed(sp, GROUPS, load, store)
            for h in range(2):
                sp.wait_ge(stored[h], landed(GROUPS // 2 - 1, 1))

        @block.gpsimd
        def _(pool):
            def gather(n, h, k):
                pool_wait(pool, ix_in[h], landed(k, 1))
                if any_yet(QUADS * free(n)):
                    pool_wait(pool, turned_in, QUADS * free(n))
                for e in range(TILES):
                    pool.indirect_dma_start(out=rows[:, h, e, :], out_offset=None, in_=t["rel"][:, :], in_offset=bass.IndirectOffsetOnAxis(ap=ix[:, h, e:e + 1], axis=0)).then_inc(rows_in[h], 16)

            skewed(pool, GROUPS, gather, nothing)

        @block.tensor
        def _(pe):
            def group(n, h, k):
                def turn_in(j):
                    q = QUADS * n + j
                    if any_yet(free(q)):
                        pe.wait_ge(run_made, free(q))
                    for c in range(QUAD):
                        mm = pe.transpose(in_ps[j % 2][:, c * P:(c + 1) * P], rows[:, h, j * QUAD + c, :], keep.ident[:, :])
                    mm.then_inc(turned_in, 1)

                def turn_out(j):
                    q = QUADS * n + j
                    pe.wait_ge(run_made, made(q))
                    if any_yet(free(q)):
                        pe.wait_ge(out_made, free(q))
                    for c in range(QUAD):
                        mm = pe.transpose(turn_ps[j % 2][:, c * P:(c + 1) * P], run[:, j % 2, c * P:(c + 1) * P], keep.ident[:, :])
                    mm.then_inc(turned, 1)

                pe.wait_ge(rows_in[h], landed(k, TILES))
                turn_in(0)
                for j in range(1, QUADS):
                    turn_in(j)
                    turn_out(j - 1)
                turn_out(QUADS - 1)

            skewed(pe, GROUPS, nothing, group)

        @block.scalar
        def _(act):
            def group(n, h, k):
                if any_yet(landed_before(k, 1)):
                    act.wait_ge(stored[h], landed_before(k, 1))
                for j in range(QUADS):
                    act.wait_ge(turned, made(QUADS * n + j))
                    act.copy(out[:, h, j * QUAD:(j + 1) * QUAD, :], turn_ps[j % 2][:, :].rearrange("p (c f) -> p c f", f=D)).then_inc(out_made, 1)

            skewed(act, GROUPS, nothing, group)

        @block.vector
        def _(v):
            v.memset(run[:, 1, QE - 1:QE], 0.0).then_inc(zeroed, 1)
            v.wait_ge(zeroed, 1)

            def scan(n, h, k):
                v.wait_ge(edges_in[h], landed(k, 1))
                for j in range(QUADS):
                    q = QUADS * n + j
                    v.wait_ge(turned_in, made(q))
                    if any_yet(free(q)):
                        v.wait_ge(turned, free(q))
                    if any_yet(made(q - 1)):
                        v.wait_ge(run_made, made(q - 1))
                    v.tensor_tensor_scan(run[:, j % 2, :], far[:, h, j * QE:(j + 1) * QE], in_ps[j % 2][:, :], run[:, (j - 1) % 2, QE - 1:QE], ALU.add, ALU.max).then_inc(run_made, 1)

            skewed(v, GROUPS, nothing, scan)


def edges_attend2(nc, a, t, keep):
    with ExitStack() as ctx:
        m = Memory(nc, ctx, "edge2")
        seeds, seed, far = m.sb("seeds", [P, 2, TILES, D]), m.sb("seed", [P, 2, GE], BF16), m.sb("far", [P, 2, GE], BF16)
        ix, heads, negident = m.sb("ix", [P, 2, TILES], U32), m.sb("heads", [P, P]), m.sb("negident", [P, P])
        spread, rows = m.sb("spread", [P, 2, GE]), m.sb("rows", [P, 2, TILES, 2 * D])
        q_sb, prod, top = m.sb("q", [P, QE]), m.sb("prod", [P, QE]), m.sb("top", [P, 2, QE + 1])
        fall, fade, ex, val = m.sb("fall", [P, QE]), m.sb("fade", [P, 2, QE]), m.sb("ex", [P, 2, QE]), m.sb("val", [P, QE])
        num, den = m.sb("num", [P, 2, QE]), m.sb("den", [P, 2, QE])
        out = m.sb("out", [P, 2, TILES, TW])
        q_ps, k_ps, s_ps0, s_ps1, v_ps, num_ps, den_ps = (m.ps(x, [P, QE]) for x in ("q", "k", "s0", "s1", "v", "num", "den"))
        s_ps = [s_ps0, s_ps1]
        consts_in, zeroed = m.sem("consts_in"), m.sem("zeroed")
        edges_in, ix_in, rows_in, stored = ([m.sem(f"{x}{i}") for i in range(2)] for x in ("edges_in", "ix_in", "rows_in", "stored"))
        (spread_made, q_spread, q_made, k_turned, prod_made, s_made, top_made, fall_made, s_less, fade_made, ex_made, v_turned, val_made,
         num_made, den_made, num_turned, den_turned, num_out, den_out) = (m.sem(x) for x in (
             "spread_made", "q_spread", "q_made", "k_turned", "prod_made", "s_made", "top_made", "fall_made", "s_less", "fade_made",
             "ex_made", "v_turned", "val_made", "num_made", "den_made", "num_turned", "den_turned", "num_out", "den_out"))
        diff_made, carried = m.sem("diff_made"), m.sem("carried")
        block = ctx.enter_context(nc.Block())
        EDGE_DMAS = 3
        nothing = lambda n, h, k: None

        @block.sync
        def _(sp):
            sp.dma_start(heads[:, :], a["heads"]).then_inc(consts_in, 16)
            sp.dma_start(negident[:, :], a["negident"]).then_inc(consts_in, 16)

            def load(n, h, k):
                if any_yet(landed_before(k, TILES)):
                    sp.wait_ge(rows_in[h], landed_before(k, TILES))
                sp.dma_start(ix[:, h, :], a["src_grp"].bitcast(U32).rearrange("(g p e) -> p g e", p=P, e=TILES)[:, bass.ds(n, 1), :].rearrange("p o e -> p (o e)")).then_inc(ix_in[h], 16)
                if any_yet(QUADS * free(n)):
                    sp.wait_ge(den_made, QUADS * free(n))
                sp.dma_start(seeds[:, h, :, :].rearrange("p t f -> p (t f)"), by_group(t["seeds"][0:EP, :], n)).then_inc(edges_in[h], 16)
                sp.dma_start(seed[:, h, :], row_to_all(t["seed"], n)).then_inc(edges_in[h], 16)
                sp.dma_start(far[:, h, :], row_to_all(t["far"], n)).then_inc(edges_in[h], 16)

            def store(n, h, k):
                sp.wait_ge(num_out, QUADS * made(n))
                sp.wait_ge(den_out, QUADS * made(n))
                sp.dma_start(by_group(t["sum2"], n), out[:, h, :, :].rearrange("p t f -> p (t f)")).then_inc(stored[h], 16)

            skewed(sp, GROUPS, load, store)
            for h in range(2):
                sp.wait_ge(stored[h], landed(GROUPS // 2 - 1, 1))

        @block.gpsimd
        def _(pool):
            def gather(n, h, k):
                pool_wait(pool, ix_in[h], landed(k, 1))
                if any_yet(QUADS * free(n)):
                    pool_wait(pool, v_turned, QUADS * free(n))
                for e in range(TILES):
                    pool.indirect_dma_start(out=rows[:, h, e, :], out_offset=None, in_=t["kv"][:, :], in_offset=bass.IndirectOffsetOnAxis(ap=ix[:, h, e:e + 1], axis=0)).then_inc(rows_in[h], 16)

            skewed(pool, GROUPS, gather, nothing)

        @block.tensor
        def _(pe):
            pe.wait_ge(consts_in, 16 * 2)

            def group(n, h, k):
                def queries_keys(j):
                    q = QUADS * n + j
                    if any_yet(q):
                        pe.wait_ge(q_made, q)
                    for c in range(QUAD):
                        e = j * QUAD + c
                        mm = pe.matmul(q_ps[:, c * P:(c + 1) * P], seeds[:, h, e, :], spread[:, h, e * P:(e + 1) * P], start=True, stop=True)
                    mm.then_inc(q_spread, 1)
                    if any_yet(q):
                        pe.wait_ge(prod_made, q)
                    for c in range(QUAD):
                        mm = pe.transpose(k_ps[:, c * P:(c + 1) * P], rows[:, h, j * QUAD + c, 0:D], keep.ident[:, :])
                    mm.then_inc(k_turned, 1)

                def scores(j):
                    q = QUADS * n + j
                    pe.wait_ge(prod_made, made(q))
                    if any_yet(free(q)):
                        pe.wait_ge(ex_made, free(q))
                    pe.matmul(s_ps[j % 2][:, :], heads[:, :], prod[:, :], start=True, stop=False, skip_group_check=True).then_inc(s_made, 1)

                def values(j):
                    q = QUADS * n + j
                    if any_yet(q):
                        pe.wait_ge(val_made, q)
                    for c in range(QUAD):
                        mm = pe.transpose(v_ps[:, c * P:(c + 1) * P], rows[:, h, j * QUAD + c, D:2 * D], keep.ident[:, :])
                    mm.then_inc(v_turned, 1)

                def less_top(j):
                    q = QUADS * n + j
                    pe.wait_ge(top_made, made(q))
                    pe.matmul(s_ps[j % 2][:, :], negident[:, :], top[:, j % 2, 1:QE + 1], start=False, stop=True, skip_group_check=True).then_inc(s_less, 1)

                def turn_out(j):
                    q = QUADS * n + j
                    pe.wait_ge(num_made, made(q))
                    if any_yet(q):
                        pe.wait_ge(num_out, q)
                    for c in range(QUAD):
                        mm = pe.transpose(num_ps[:, c * P:(c + 1) * P], num[:, j % 2, c * P:(c + 1) * P], keep.ident[:, :])
                    mm.then_inc(num_turned, 1)
                    pe.wait_ge(den_made, made(q))
                    if any_yet(q):
                        pe.wait_ge(den_out, q)
                    for c in range(QUAD):
                        mm = pe.transpose(den_ps[:, c * P:(c + 1) * P], den[:, j % 2, c * P:(c + 1) * P], keep.ident[:, :])
                    mm.then_inc(den_turned, 1)

                pe.wait_ge(edges_in[h], landed(k, EDGE_DMAS))
                pe.wait_ge(spread_made, made(n))
                pe.wait_ge(rows_in[h], landed(k, TILES))
                queries_keys(0)
                for j in range(QUADS):
                    scores(j)
                    if j + 1 < QUADS:
                        queries_keys(j + 1)
                    values(j)
                    less_top(j)
                    if j:
                        turn_out(j - 1)
                turn_out(QUADS - 1)

            skewed(pe, GROUPS, nothing, group)

        @block.scalar
        def _(act):
            def group(n, h, k):
                def copy_q(j):
                    q = QUADS * n + j
                    act.wait_ge(q_spread, made(q))
                    if any_yet(q):
                        act.wait_ge(prod_made, q)
                    act.copy(q_sb[:, :], q_ps[:, :]).then_inc(q_made, 1)

                def exps(j):
                    q = QUADS * n + j
                    act.wait_ge(s_less, made(q))
                    if any_yet(free(q)):
                        act.wait_ge(den_made, free(q))
                    act.activation(ex[:, j % 2, :], s_ps[j % 2][:, :], ACT.Exp).then_inc(ex_made, 1)
                    act.wait_ge(fall_made, made(q))
                    act.activation(fade[:, j % 2, :], fall[:, :], ACT.Exp).then_inc(fade_made, 1)

                def copy_out(j):
                    q = QUADS * n + j
                    act.wait_ge(num_turned, made(q))
                    act.copy(out[:, h, j * QUAD:(j + 1) * QUAD, 0:D], num_ps[:, :].rearrange("p (c f) -> p c f", f=D)).then_inc(num_out, 1)
                    act.wait_ge(den_turned, made(q))
                    act.copy(out[:, h, j * QUAD:(j + 1) * QUAD, D:TW], den_ps[:, :].rearrange("p (c a f) -> p c a f", c=QUAD, f=HC)[:, :, :, 0]).then_inc(den_out, 1)

                if any_yet(landed_before(k, 1)):
                    act.wait_ge(stored[h], landed_before(k, 1))
                copy_q(0)
                for j in range(QUADS):
                    if j + 1 < QUADS:
                        copy_q(j + 1)
                    exps(j)
                    if j:
                        copy_out(j - 1)
                copy_out(QUADS - 1)

            skewed(act, GROUPS, nothing, group)

        @block.vector
        def _(v):
            v.memset(top[:, 1, QE:QE + 1], 0.0).then_inc(zeroed, 1)
            v.memset(num[:, 1, QE - 1:QE], 0.0).then_inc(zeroed, 1)
            v.memset(den[:, 1, QE - 1:QE], 0.0).then_inc(zeroed, 1)
            v.wait_ge(zeroed, 3)

            def spread_group(n, h, k):
                v.wait_ge(edges_in[h], landed(k, EDGE_DMAS))
                if any_yet(QUADS * free(n)):
                    v.wait_ge(q_spread, QUADS * free(n))
                v.tensor_scalar(spread[:, h, :], seed[:, h, :], keep.iota[:, 0:1], None, ALU.is_equal).then_inc(spread_made, 1)

            def attend(n, h, k):
                def maxima(j):
                    q = QUADS * n + j
                    v.wait_ge(q_made, made(q))
                    v.wait_ge(k_turned, made(q))
                    if any_yet(q):
                        v.wait_ge(s_made, q)
                    v.tensor_tensor(prod[:, :], k_ps[:, :], q_sb[:, :], ALU.mult).then_inc(prod_made, 1)
                    if any_yet(free(q)):
                        v.wait_ge(s_less, free(q))
                    v.tensor_copy(top[:, j % 2, 0:1], top[:, (j - 1) % 2, QE:QE + 1]).then_inc(carried, 1)
                    v.wait_ge(carried, made(q))
                    v.wait_ge(s_made, made(q))
                    v.tensor_tensor_scan(top[:, j % 2, 1:QE + 1], far[:, h, j * QE:(j + 1) * QE], s_ps[j % 2][:, :], top[:, j % 2, 0:1], ALU.add, ALU.max).then_inc(top_made, 1)
                    v.wait_ge(top_made, made(q))
                    if any_yet(q):
                        v.wait_ge(fade_made, q)
                    v.tensor_tensor(fall[:, :], top[:, j % 2, 0:QE], top[:, j % 2, 1:QE + 1], ALU.subtract).then_inc(diff_made, 1)
                    v.wait_ge(diff_made, made(q))
                    v.tensor_tensor(fall[:, :], fall[:, :], far[:, h, j * QE:(j + 1) * QE], ALU.add).then_inc(fall_made, 1)

                def sums(j):
                    q = QUADS * n + j
                    v.wait_ge(ex_made, made(q))
                    v.wait_ge(v_turned, made(q))
                    if any_yet(q):
                        v.wait_ge(den_made, q)
                    v.tensor_tensor(val[:, :], v_ps[:, :], ex[:, j % 2, :], ALU.mult).then_inc(val_made, 1)
                    v.wait_ge(fade_made, made(q))
                    v.wait_ge(val_made, made(q))
                    if any_yet(free(q)):
                        v.wait_ge(den_turned, free(q))
                    v.tensor_tensor_scan(num[:, j % 2, :], fade[:, j % 2, :], val[:, :], num[:, (j - 1) % 2, QE - 1:QE], ALU.mult, ALU.add).then_inc(num_made, 1)
                    v.tensor_tensor_scan(den[:, j % 2, :], fade[:, j % 2, :], ex[:, j % 2, :], den[:, (j - 1) % 2, QE - 1:QE], ALU.mult, ALU.add).then_inc(den_made, 1)

                maxima(0)
                for j in range(1, QUADS):
                    maxima(j)
                    sums(j - 1)
                sums(QUADS - 1)

            skewed(v, GROUPS, spread_group, attend)


def build(nc, a, out):
    ctx = ExitStack()
    with ctx:
        def dram(name, shape, dt=F32):
            return nc.dram_tensor(name, shape, dt, kind="Internal").ap()

        t = {"x": a["x"]}
        for name in ("same", "far", "seed"):
            t[name] = dram(name, (1, EP), BF16)
        t["digits"] = dram("digits", (2, EP), BF16)
        t["row3"] = dram("row3", (EP,), U32)
        t["rs"] = dram("rs", (FB * P,))
        t["seeds"] = dram("seeds", (EP + NP, D))
        for k in range(ACCS):
            t[f"acc{k}"] = dram(f"acc{k}", (NP + P, D))
        for name in ("nodes", "a1", "own1", "upd", "own2", "own3"):
            t[name] = dram(name, (NP, D))
        t["kv"] = dram("kv", (NP, 2 * D))
        rel = t["rel"] = dram("rel", (RELS * NP, D))
        for r in range(RELS):
            t[f"rel{r}"] = rel[r * NP:(r + 1) * NP, :]
        t["sum1"], t["sum2"], t["max3"] = dram("sum1", (EP, D)), dram("sum2", (EP, TW)), dram("max3", (EP, D))

        class Keep:
            pass

        keep, m = Keep(), Memory(nc, ctx, "keep")
        keep.ident, keep.iota, keep.eps = m.sb("ident", [P, P]), m.sb("iota", [P, 1]), m.sb("eps", [P, 1])
        keep.has, keep.last_ix, keep.seed_ix = m.sb("has", [P, NB]), m.sb("lastix", [P, NB], U32), m.sb("seedix", [P, NB], U32)
        keep.first_ix = m.sb("firstix", [GROUPS, TILES], U32)

        prologue(nc, a, t, keep)
        node_phase(nc, a, t, keep, 0, out)
        seed_tiles(nc, t, keep, "tiles0")
        edges_sum0(nc, a, t, keep)
        node_phase(nc, a, t, keep, 1, out)
        seed_tiles(nc, t, keep, "tiles1")
        edges_sum1(nc, a, t, keep)
        node_phase(nc, a, t, keep, 2, out)
        seed_tiles(nc, t, keep, "tiles2")
        edges_attend2(nc, a, t, keep)
        node_phase(nc, a, t, keep, 3, out)
        edges_max3(nc, a, t, keep)
        node_phase(nc, a, t, keep, 4, out)


def constants():
    p, e = np.arange(P), np.arange(GE) % P
    node = lambda blocks: (np.arange(blocks)[None, :] * P + p[:, None]).astype(np.float32)
    return {
        "ident": np.eye(P, dtype=np.float32),
        "negident": -np.eye(P, dtype=np.float32),
        "iota": p[:, None].astype(np.float32),
        "eps": np.full((P, 1), EPS, np.float32),
        "place": np.broadcast_to(e, (GROUPS, GE)).astype(np.float32),
        "inside": np.broadcast_to(e > 0, (GROUPS, GE)).astype(np.float32),
        "nid": node(FB),
        "spare": node(NB) + EP,
        "lower": np.tri(P, P, -1, dtype=np.float32),
        "trash": (NP + p[:, None]).astype(np.float32),
        "place_value": np.repeat([[float(P)], [1.0]], P, 1).astype(np.float32),
        "heads": (np.kron(np.eye(HEADS), np.ones((HC, HC))) / np.sqrt(HC)).astype(np.float32),
    }


def laid_out(i):
    def filled(x, rows, value):
        x = np.asarray(x)
        return np.concatenate([x, np.full((rows - len(x), *x.shape[1:]), value, x.dtype)])

    def grouped(x):
        return np.ascontiguousarray(x.reshape(GROUPS, TILES, P).transpose(0, 2, 1)).reshape(-1)

    g = {k: np.asarray(v) for k, v in i.items()}
    src, dst = filled(g["src"], EP, N), filled(g["dst"], EP, NP - 1)
    zero = np.zeros(D, np.float32)
    msg, upd = g["L1_gnn_W_msg"], g["L1_gnn_W_upd"]
    rel_w, rel_b = g["L3_gnn_weight"], g["L3_gnn_bias"]
    return {
        "x": filled(g["x"], NP, 0),
        "src_flat": src, "src_grp": grouped(src),
        "dst_prev": np.concatenate([np.array([-1], dst.dtype), dst]),
        "dst_tiles": dst.reshape(NT, P), "dst_first": np.ascontiguousarray(dst[::P]),
        "typ_grp": grouped(filled(g["edge_type_4"], EP, 0)),
        "w_grp": grouped(filled(g["edge_weight"], EP, 0)),
        "ed_row": filled(g["edge_weight1"], EP, 0).reshape(1, EP),
        "w0": np.ascontiguousarray(g["L0_gnn_W"].T), "b0": g["L0_gnn_b"],
        "w1": np.concatenate([msg[:D], msg[D:2 * D], g["L1_gnn_W_res"], upd[:D]], 1),
        "b1": np.concatenate([zero, g["L1_gnn_b_msg"], zero, g["L1_gnn_b_upd"]]),
        "w_dist": msg[2 * D:], "w_upd": upd[D:],
        "w2": np.concatenate([g[f"L2_gnn_W{x}"] for x in "kvqr"], 1),
        "b2": np.concatenate([g[f"L2_gnn_b{x}"] for x in "kvqr"]),
        "w3": np.concatenate(list(rel_w), 1), "b3": rel_b.reshape(-1),
    }


def kernel(**inputs):
    import concourse.bacc as bacc
    from concourse.bass_utils import run_bass_kernel_spmd

    nc = bacc.Bacc("TRN2", target_bir_lowering=False, num_devices=1)
    arrays = {f"in_{k}": np.ascontiguousarray(v) for k, v in {**laid_out(inputs), **constants()}.items()}
    a = {k[3:]: nc.dram_tensor(k, v.shape, mybir.dt.from_np(v.dtype), kind="ExternalInput").ap() for k, v in arrays.items()}
    out = nc.dram_tensor("out", (NP, D), F32, kind="ExternalOutput").ap()
    build(nc, a, out)
    r = run_bass_kernel_spmd(nc, [arrays], core_ids=[0])
    return r.results[0]["out"][:N]
```

```python
from contextlib import ExitStack

import concourse.bass as bass
import numpy as np
from concourse import mybir

F32, BF16, I32, U32 = mybir.dt.float32, mybir.dt.bfloat16, mybir.dt.int32, mybir.dt.uint32
ALU, ACT, AX = mybir.AluOpType, mybir.ActivationFunctionType, mybir.AxisListType

P = 128
D = 128
N, E = 12500, 200000
QUAD = 4
QE = QUAD * P
TILES = 16
QUADS = TILES // QUAD
GE = TILES * P
GROUPS = -(-E // GE)
EP = GROUPS * GE
NT = EP // P
NB = -(-N // P)
NP = NB * P
STEP = 7
STEPS = NB // STEP
FB, FSTEP = 100, 10
HEADS, HC = 4, 32
RELS = 4
ACCS = 4
TW = D + HEADS
FAR = 3.0e38
EPS = 1e-5


def made(n):
    return n + 1


def free(n):
    return n - 1


def landed(k, dmas):
    return 16 * dmas * (k + 1)


def landed_before(k, dmas):
    return 16 * dmas * k


def any_yet(count):
    return not isinstance(count, int) or count > 0


def skewed(eng, steps, front, back):
    last = steps // 2 - 1
    front(0, 0, 0)
    front(1, 1, 0)
    back(0, 0, 0)
    front(2, 0, 1)
    back(1, 1, 0)
    with eng.Fori(1, last) as i:
        front(2 * i + 1, 1, i)
        back(2 * i, 0, i)
        front(2 * i + 2, 0, i + 1)
        back(2 * i + 1, 1, i)
    front(steps - 1, 1, last)
    back(steps - 2, 0, last)
    back(steps - 1, 1, last)


def two_ahead(eng, steps, front, back):
    last = steps // 2 - 1
    front(0, 0, 0)
    front(1, 1, 0)

    def both(i):
        front(2 * i + 2, 0, i + 1)
        back(2 * i, 0, i)
        front(2 * i + 3, 1, i + 1)
        back(2 * i + 1, 1, i)

    both(0)
    with eng.Fori(1, last) as i:
        both(i)
    back(steps - 2, 0, last)
    back(steps - 1, 1, last)


def pipelined(eng, stages):
    body = 2 * QUADS
    last = GROUPS // 2 - 1

    def quad(i, q):
        for stage, lag in stages:
            shift, at = divmod(q - lag, body)
            k = i + shift
            if isinstance(k, int) and not 0 <= k <= last:
                continue
            stage(2 * k + at // QUADS, at // QUADS, k, at % QUADS)

    for q in range(min(lag for _, lag in stages), body):
        quad(0, q)
    with eng.Fori(1, last) as i:
        for q in range(body):
            quad(i, q)
    for q in range(body + max(lag for _, lag in stages)):
        quad(last, q)


def at_group(stage):
    return lambda n, h, k, j: stage(n, h, k) if j == 0 else None


def pool_wait(pool, sem, value):
    pool.wait_ge(sem, value)
    pool.nop(nofuse=True)


class Memory:
    def __init__(self, nc, ctx, phase):
        self.nc, self.ctx, self.phase, self.sems = nc, ctx, phase, []
        ctx.callback(self.release)

    def sb(self, name, shape, dt=F32):
        return self.ctx.enter_context(self.nc.sbuf_tensor(f"{self.phase}_{name}", shape, dt))

    def ps(self, name, shape):
        return self.ctx.enter_context(self.nc.psum_tensor(f"{self.phase}_{name}_psum", shape, F32))

    def sem(self, name):
        self.sems.append(self.nc.alloc_semaphore(name=f"{self.phase}_{name}"))
        return self.sems[-1]

    def release(self):
        if self.sems:
            self.nc.clear_and_free_semaphores(self.sems)
            self.nc.all_engine_barrier()


def by_group(flat, n):
    return flat.rearrange("(g p t) f -> p g (t f)", p=P, t=TILES)[:, bass.ds(n, 1), :].rearrange("p o e -> p (o e)")


def edge_row(v, after, row, edge, part, part2):
    after(v.tensor_scalar(part, edge, P - 1, 4, ALU.bitwise_and, ALU.logical_shift_left))
    after(v.tensor_scalar(part2, edge, 7, TILES - 1, ALU.logical_shift_right, ALU.bitwise_and))
    after(v.tensor_tensor(part, part, part2, ALU.bitwise_or))
    after(v.tensor_scalar(part2, edge, 11, 11, ALU.logical_shift_right, ALU.logical_shift_left))
    after(v.tensor_tensor(row, part, part2, ALU.bitwise_or))


def by_step(flat, n):
    return flat.rearrange("(b p) f -> p b f", p=P)[:, bass.ds(n * STEP, STEP), :]


def row_to_all(row, n):
    return row[0:1, bass.ds(n * GE, GE)].broadcast_to([P, GE])


def prologue(nc, a, t, keep):
    with ExitStack() as ctx:
        m = Memory(nc, ctx, "pro")
        cur, prev, src = m.sb("cur", [GROUPS, GE], I32), m.sb("prev", [GROUPS, GE], I32), m.sb("src", [GROUPS, GE], I32)
        place, inside = m.sb("place", [GROUPS, GE]), m.sb("inside", [GROUPS, GE])
        same, far, seed = m.sb("same", [GROUPS, GE], BF16), m.sb("far", [GROUPS, GE], BF16), m.sb("seed", [GROUPS, GE], BF16)
        starts, digit = m.sb("starts", [GROUPS, GE]), m.sb("digit", [GROUPS, GE], I32)
        digits = m.sb("digits", [GROUPS, 2, GE], BF16)
        typ = m.sb("typ", [P, NT], I32)
        firsti, first, junk = m.sb("firsti", [P, NT], I32), m.sb("first", [P, NT]), m.sb("junk", [P, NT])
        nid = m.sb("nid", [P, FB])
        spare = m.sb("spare", [P, NB])
        before, tile_of, within, rs = (m.sb(x, [P, FB]) for x in ("before", "tileof", "within", "rs"))
        tile_ix = m.sb("tileix", [P, FB], U32)
        stage = m.sb("stage", [P, 2, FSTEP], U32)
        rows = m.sb("rows", [P, 2, FSTEP, P], I32)
        junk2 = m.sb("junk2", [P, P])
        rs_next = m.sb("rsnext", [P, NB])
        edge, part, part2 = (m.sb(x, [P, NB], I32) for x in ("edge", "part", "part2"))
        zero = m.sb("zero", [P, TILES * D])
        consts_in, edges_in, more_in = m.sem("consts_in"), m.sem("edges_in"), m.sem("more_in")
        dve, zeroed, stored, rs_out, rs_in = m.sem("dve"), m.sem("zeroed"), m.sem("stored"), m.sem("rs_out"), m.sem("rs_in")
        within_made = m.sem("within_made")
        zero_made, staged, counted = m.sem("zero_made"), m.sem("staged"), m.sem("counted")
        rows_in = [m.sem("rows_in0"), m.sem("rows_in1")]
        rows_ready = m.sem("rows_ready")
        block = ctx.enter_context(nc.Block())
        ROWS_READY = 3
        seeds = t["seeds"]

        @block.sync
        def _(sp):
            for to, of in ((nid, a["nid"]), (spare, a["spare"]), (keep.ident, a["ident"]), (keep.iota, a["iota"]), (keep.eps, a["eps"]), (keep.first_ix, a["dst_first"].rearrange("(g t) -> g t", t=TILES).bitcast(U32))):
                sp.dma_start(to[:, :], of).then_inc(consts_in, 16)
            sp.dma_start(firsti[:, :], a["dst_first"].rearrange("(o t) -> o t", o=1).broadcast_to([P, NT])).then_inc(consts_in, 16)
            sp.dma_start(cur[:, :], a["dst_prev"][1:1 + EP].rearrange("(g e) -> g e", e=GE)).then_inc(edges_in, 16)
            sp.dma_start(prev[:, :], a["dst_prev"][0:EP].rearrange("(g e) -> g e", e=GE)).then_inc(edges_in, 16)
            sp.dma_start(place[:, :], a["place"]).then_inc(edges_in, 16)
            sp.dma_start(inside[:, :], a["inside"]).then_inc(edges_in, 16)
            sp.dma_start(src[:, :], a["src_flat"].rearrange("(g e) -> g e", e=GE)).then_inc(more_in, 16)
            sp.dma_start(typ[:, :], a["typ_pt"]).then_inc(more_in, 16)
            sp.dma_start(keep.src_ix[:, :], a["src_pt"].bitcast(U32)).then_inc(more_in, 16)
            sp.wait_ge(rows_ready, ROWS_READY)
            sp.dma_start(t["same"].rearrange("o (g e) -> (o g) e", e=GE), same[:, :]).then_inc(stored, 16)
            sp.dma_start(t["far"].rearrange("o (g e) -> (o g) e", e=GE), far[:, :]).then_inc(stored, 16)
            sp.dma_start(t["seed"].rearrange("o (g e) -> (o g) e", e=GE), seed[:, :]).then_inc(stored, 16)
            sp.dma_start(t["digits"].rearrange("d (g e) -> g d e", e=GE), digits[:, :, :]).then_inc(stored, 16)
            sp.wait_ge(counted, 1)
            with nc.allow_non_contiguous_dma("a node's number per partition"):
                sp.dma_start(t["rs"][0:FB * P].rearrange("(b p) -> p b", p=P), rs[:, :]).then_inc(rs_out, 16)
                sp.wait_ge(rs_out, 16)
                sp.dma_start(rs_next[:, :], t["rs"][1:1 + NP].rearrange("(b p) -> p b", p=P)).then_inc(rs_in, 16)
            sp.wait_ge(stored, 16 * 4)

        @block.scalar
        def _(act):
            act.wait_ge(zero_made, 1)
            with act.Fori(0, GROUPS) as g:
                nc.scalar.dma_start(seeds[bass.ds(g * GE, GE), :].rearrange("(p t) f -> p (t f)", p=P), zero[:, :]).then_inc(zeroed, 16)
            for k in range(ACCS):
                rows_k = (NP + P) // P
                for lo in range(0, rows_k, TILES):
                    w = min(TILES, rows_k - lo)
                    act.dma_start(t[f"acc{k}"].rearrange("(p t) f -> p (t f)", p=P)[:, lo * D:(lo + w) * D], zero[:, 0:w * D]).then_inc(zeroed, 16)
            act.wait_ge(zeroed, 16 * (GROUPS + ACCS * -(-((NP + P) // P) // TILES)))

        @block.gpsimd
        def _(pool):
            def gather(n, h, k):
                pool_wait(pool, staged, made(n))
                for c in range(FSTEP):
                    pool.indirect_dma_start(out=rows[:, h, c, :], out_offset=None, in_=a["dst_tiles"][:, :], in_offset=bass.IndirectOffsetOnAxis(ap=stage[:, h, c:c + 1], axis=0)).then_inc(rows_in[h], 16)

            skewed(pool, FB // FSTEP, gather, lambda n, h, k: None)

        @block.vector
        def _(v):
            steps = 0

            def after(ins):
                nonlocal steps
                ins.then_inc(dve, 1)
                steps += 1
                v.wait_ge(dve, steps)

            v.memset(zero[:, :], 0.0).then_inc(zero_made, 1)
            v.wait_ge(edges_in, 16 * 4)
            after(v.tensor_tensor(same[:, :], cur[:, :], prev[:, :], ALU.is_equal))
            v.tensor_scalar(far[:, :], same[:, :], -1.0, FAR, ALU.add, ALU.mult).then_inc(rows_ready, 1)
            after(v.tensor_scalar(starts[:, :], same[:, :], -1.0, 1.0, ALU.mult, ALU.add))
            after(v.tensor_tensor(starts[:, :], starts[:, :], place[:, :], ALU.mult))
            v.tensor_tensor_scan(seed[:, :], inside[:, :], starts[:, :], 0.0, ALU.mult, ALU.max).then_inc(rows_ready, 1)
            v.wait_ge(more_in, 16 * 3)
            after(v.tensor_scalar(digit[:, :], src[:, :], 7, None, ALU.logical_shift_right))
            after(v.tensor_copy(digits[:, 0, :], digit[:, :]))
            after(v.tensor_scalar(digit[:, :], src[:, :], P - 1, None, ALU.bitwise_and))
            v.tensor_copy(digits[:, 1, :], digit[:, :]).then_inc(rows_ready, 1)
            v.scalar_tensor_tensor(keep.rel_ix[:, :], typ[:, :], float(NP), keep.src_ix[:, :], ALU.mult, ALU.add)
            v.wait_ge(consts_in, 16 * 7)
            after(v.tensor_copy(first[:, :], firsti[:, :]))
            for b in range(FB):
                after(v.tensor_scalar(junk[:, :], first[:, :], nid[:, b:b + 1], 0.0, ALU.is_lt, ALU.add, accum_out=before[:, b:b + 1]))
            after(v.tensor_scalar(tile_of[:, :], before[:, :], -1.0, 0.0, ALU.add, ALU.max))
            after(v.tensor_copy(tile_ix[:, :], tile_of[:, :]))

            def to_stage(n, h, k):
                if any_yet(landed_before(k, FSTEP)):
                    v.wait_ge(rows_in[h], landed_before(k, FSTEP))
                v.tensor_copy(stage[:, h, :], tile_ix[:, bass.ds(n * FSTEP, FSTEP)]).then_inc(staged, 1)

            def count(n, h, k):
                v.wait_ge(rows_in[h], landed(k, FSTEP))
                for c in range(FSTEP):
                    counted_one = v.tensor_scalar(junk2[:, :], rows[:, h, c, :], nid[:, bass.ds(n * FSTEP + c, 1)], 0.0, ALU.is_lt, ALU.add, accum_out=within[:, bass.ds(n * FSTEP + c, 1)])
                    counted_one.then_inc(within_made, 1)
                    v.wait_ge(within_made, FSTEP * n + c + 1)

            skewed(v, FB // FSTEP, to_stage, count)
            v.scalar_tensor_tensor(rs[:, :], tile_of[:, :], float(P), within[:, :], ALU.mult, ALU.add).then_inc(counted, 1)
            v.wait_ge(rs_in, 16)
            v.wait_ge(counted, 1)
            after(v.tensor_tensor(keep.has[:, :], rs_next[:, :], rs[:, 0:NB], ALU.is_gt))
            after(v.tensor_scalar(edge[:, :], rs_next[:, :], -1.0, 0.0, ALU.add, ALU.max))
            edge_row(v, after, keep.last_ix[:, :].bitcast(I32), edge[:, :], part[:, :], part2[:, :])
            after(v.tensor_copy(edge[:, :], rs[:, 0:NB]))
            edge_row(v, after, part[:, :], edge[:, :], part[:, :], part2[:, :])
            after(v.tensor_copy(rs_next[:, :], part[:, :]))
            after(v.tensor_tensor(rs_next[:, :], rs_next[:, :], spare[:, :], ALU.subtract))
            after(v.tensor_tensor(rs_next[:, :], rs_next[:, :], keep.has[:, :], ALU.mult))
            after(v.tensor_tensor(keep.seed_ix[:, :], rs_next[:, :], spare[:, :], ALU.add))


def seed_tiles(nc, t, keep, phase):
    with ExitStack() as ctx:
        m = Memory(nc, ctx, phase)
        rows = m.sb("rows", [GROUPS, TILES, D])
        gathered, stored = m.sem("gathered"), m.sem("stored")
        block = ctx.enter_context(nc.Block())
        firsts = t["seeds"][0:EP, :].rearrange("(g p t) f -> g p t f", p=P, t=TILES)[:, 0, :, :]

        @block.gpsimd
        def _(pool):
            for c in range(TILES):
                pool.indirect_dma_start(out=rows[:, c, :], out_offset=None, in_=t["nodes"][:, :], in_offset=bass.IndirectOffsetOnAxis(ap=keep.first_ix[:, c:c + 1], axis=0)).then_inc(gathered, 16)

        @block.sync
        def _(sp):
            sp.wait_ge(gathered, 16 * TILES)
            sp.dma_start(firsts, rows[:, :, :]).then_inc(stored, 16)
            sp.wait_ge(stored, 16)


def node_phase(nc, a, t, keep, layer, out):
    ins = [["x"], ["x", "acc0", "acc1", "acc2", "acc3"], ["own", "upd"], ["own"], ["own"]][layer]
    cat = [D, 4 * D, 4 * D, 5 * D, 0][layer]
    own = [None, 2 * D, 3 * D, 4 * D, None][layer]
    seeded = [0, D, 2 * D, None, None][layer]
    outs = [[("nodes", 0, D)],
            [("a1", 0, D), ("nodes", D, D), ("own", 2 * D, D), ("upd", 3 * D, D)],
            [("kv", 0, 2 * D), ("nodes", 2 * D, D), ("own", 3 * D, D)],
            [("rel0", 0, D), ("rel1", D, D), ("rel2", 2 * D, D), ("rel3", 3 * D, D), ("own", 4 * D, D)],
            []][layer]
    got = [0, 0, D, TW, D][layer]
    norm = layer > 0
    if layer in (2, 3, 4):
        ins = [f"own{layer - 1}" if x == "own" else x for x in ins]
    outs = [(f"own{layer}" if x == "own" else x, c, w) for x, c, w in outs]
    with ExitStack() as ctx:
        m = Memory(nc, ctx, f"node{layer}")
        xin = [m.sb(f"in_{x}", [P, 2, STEP, D]) for x in ins]
        xh = m.sb("xh", [P, 2, STEP, D])
        ixs = m.sb("ixs", [P, 2, 2 * STEP], U32)
        if got:
            res = m.sb("res", [P, 2, STEP, got])
            resT = m.sb("resT", [P, STEP * P])
        if norm:
            stats, mv = m.sb("stats", [P, STEP, 6]), m.sb("mv", [P, STEP, 2])
            dev, inv = m.sb("dev", [P, STEP]), m.sb("inv", [P, STEP])
        if layer == 2:
            wupd = m.sb("wupd", [P, D])
            upd_ps = m.ps("upd_ps", [P, 1024])
        if layer == 3:
            den = m.sb("den", [P, STEP, HEADS])
        if cat:
            w, bias = m.sb("w", [P, cat]), m.sb("bias", [P, cat])
            xT = m.sb("xT", [P, 2, STEP * P])
            res_out = m.sb("out", [P, 2, STEP, cat])
            mm_ps = [m.ps(f"mm{i}", [P, 1024]) for i in range(2)]
        tr_ps = m.ps("tr", [P, 1024])
        weights_in = m.sem("weights_in")
        in_landed = [m.sem("in_landed0"), m.sem("in_landed1")]
        res_landed = [m.sem("res_landed0"), m.sem("res_landed1")]
        out_landed = [m.sem("out_landed0"), m.sem("out_landed1")]
        seeds_landed = [m.sem("seeds_landed0"), m.sem("seeds_landed1")]
        staged, xh_made, tr_made, xT_made = (m.sem(x) for x in ("staged", "xh_made", "tr_made", "xT_made"))
        mm_made, mm_used, dev_made, mv_made, dve = (m.sem(x) for x in ("mm_made", "mm_used", "dev_made", "mv_made", "dve"))
        pre_made, preT_made, upd_made, res_masked = (m.sem(x) for x in ("pre_made", "preT_made", "upd_made", "res_masked"))
        block = ctx.enter_context(nc.Block())
        n_out = len(outs) if outs else 1
        n_weights = (2 if cat else 0) + (layer == 2)
        nothing = lambda n, h, k: None

        @block.sync
        def _(sp):
            if cat:
                sp.dma_start(w[:, :], a[f"w{layer}"]).then_inc(weights_in, 16)
                sp.dma_start(bias[:, :], a[f"b{layer}"].rearrange("(o c) -> o c", o=1).broadcast_to([P, cat])).then_inc(weights_in, 16)
            if layer == 2:
                sp.dma_start(wupd[:, :], a["w_upd"]).then_inc(weights_in, 16)

            def load(n, h, k):
                if any_yet(free(n)):
                    sp.wait_ge(xh_made, free(n))
                for x, to in zip(ins, xin):
                    sp.dma_start(to[:, h, :, :], by_step(t[x], n)).then_inc(in_landed[h], 16)

            def store(n, h, k):
                if cat:
                    sp.wait_ge(mm_used, STEP * (n + 1))
                    for x, c, wd in outs:
                        sp.dma_start(by_step(t[x], n), res_out[:, h, :, c:c + wd]).then_inc(out_landed[h], 16)
                else:
                    sp.wait_ge(xh_made, made(n))
                    sp.dma_start(by_step(out, n), xh[:, h, :, :]).then_inc(out_landed[h], 16)

            skewed(sp, STEPS, load, store)
            for h in range(2):
                sp.wait_ge(out_landed[h], landed(STEPS // 2 - 1, n_out))

        @block.gpsimd
        def _(pool):
            table = {2: "sum1", 3: "sum2", 4: "max3"}.get(layer)

            def gather(n, h, k):
                pool_wait(pool, staged, made(n))
                if any_yet(free(n)):
                    pool_wait(pool, xh_made, free(n))
                for b in range(STEP):
                    pool.indirect_dma_start(out=res[:, h, b, :], out_offset=None, in_=t[table][:, :], in_offset=bass.IndirectOffsetOnAxis(ap=ixs[:, h, b:b + 1], axis=0)).then_inc(res_landed[h], 16)

            def scatter(n, h, k):
                pool_wait(pool, staged, made(n))
                pool_wait(pool, mm_used, STEP * (n + 1))
                for b in range(STEP):
                    pool.indirect_dma_start(out=t["seeds"][:, :], out_offset=bass.IndirectOffsetOnAxis(ap=ixs[:, h, STEP + b:STEP + b + 1], axis=0), in_=res_out[:, h, b, seeded:seeded + D], in_offset=None).then_inc(seeds_landed[h], 16)

            skewed(pool, STEPS, gather if got else nothing, scatter if seeded is not None else nothing)
            if seeded is not None:
                for h in range(2):
                    pool_wait(pool, seeds_landed[h], landed(STEPS // 2 - 1, STEP))

        @block.tensor
        def _(pe):
            if n_weights:
                pe.wait_ge(weights_in, 16 * n_weights)

            def front(n, h, k):
                if layer == 2:
                    pe.wait_ge(res_masked, made(n))
                    if any_yet(made(n - 1)):
                        pe.wait_ge(xT_made, made(n - 1))
                    for b in range(STEP):
                        mm = pe.transpose(tr_ps[:, b * P:(b + 1) * P], res[:, h, b, :], keep.ident[:, :])
                    mm.then_inc(pre_made, 1)
                    pe.wait_ge(preT_made, made(n))
                    for b in range(STEP):
                        mm = pe.matmul(upd_ps[:, b * P:(b + 1) * P], resT[:, b * P:(b + 1) * P], wupd[:, :], start=True, stop=True)
                    mm.then_inc(upd_made, 1)
                pe.wait_ge(xh_made, made(n))
                if any_yet(made(n - 1)):
                    pe.wait_ge(xT_made, made(n - 1))
                for b in range(STEP):
                    mm = pe.transpose(tr_ps[:, b * P:(b + 1) * P], xh[:, h, b, :], keep.ident[:, :])
                mm.then_inc(tr_made, 1)

            def back(n, h, k):
                pe.wait_ge(xT_made, made(n))
                for b in range(STEP):
                    if any_yet(STEP * n + b - 1):
                        pe.wait_ge(mm_used, STEP * n + b - 1)
                    slot = mm_ps[(h * STEP + b) % 2]
                    rows = xT[:, h, b * P:(b + 1) * P]
                    mm = pe.matmul(slot[:, 0:min(cat, 512)], rows, w[:, 0:min(cat, 512)], start=True, stop=own is None or own >= 512)
                    if own is not None and own < 512:
                        mm = pe.matmul(slot[:, own:own + D], rows, keep.ident[:, :], start=False, stop=True)
                    if cat > 512:
                        pe.matmul(slot[:, 512:cat], rows, w[:, 512:cat], start=True, stop=False)
                        mm = pe.matmul(slot[:, own:own + D], rows, keep.ident[:, :], start=False, stop=True)
                    mm.then_inc(mm_made, 1)

            if cat:
                skewed(pe, STEPS, front, back)

        @block.scalar
        def _(act):

            def front(n, h, k):
                if layer == 2:
                    act.wait_ge(pre_made, made(n))
                    if any_yet(made(n - 1)):
                        act.wait_ge(upd_made, made(n - 1))
                    act.copy(resT[:, :], tr_ps[:, 0:STEP * P]).then_inc(preT_made, 1)
                if norm:
                    act.wait_ge(mv_made, made(n))
                    act.activation(dev[:, :], mv[:, :, 1], ACT.Sqrt, bias=keep.eps[:, :]).then_inc(dev_made, 1)
                if cat:
                    act.wait_ge(tr_made, made(n))
                    if any_yet(STEP * free(n)):
                        act.wait_ge(mm_made, STEP * free(n))
                    act.copy(xT[:, h, :], tr_ps[:, 0:STEP * P]).then_inc(xT_made, 1)

            skewed(act, STEPS, front, nothing)

        @block.vector
        def _(v):
            if cat:
                v.wait_ge(weights_in, 16 * n_weights)
            chain = {0: 0, 1: 6, 2: 4, 3: 7, 4: 4}[layer]
            done = 0

            def after(ins, n):
                nonlocal done
                ins.then_inc(dve, 1)
                done += 1
                v.wait_ge(dve, chain * n + done)

            def front(n, h, k):
                nonlocal done
                done = 0
                if seeded is not None:
                    if any_yet(landed_before(k, STEP)):
                        v.wait_ge(seeds_landed[h], landed_before(k, STEP))
                if got or seeded is not None:
                    if got:
                        if any_yet(landed_before(k, STEP)):
                            v.wait_ge(res_landed[h], landed_before(k, STEP))
                    v.tensor_copy(ixs[:, h, 0:STEP], keep.last_ix[:, bass.ds(n * STEP, STEP)])
                    v.tensor_copy(ixs[:, h, STEP:], keep.seed_ix[:, bass.ds(n * STEP, STEP)]).then_inc(staged, 1)
                v.wait_ge(in_landed[h], landed(k, len(ins)))
                if got:
                    v.wait_ge(res_landed[h], landed(k, STEP))
                    has = keep.has[:, bass.ds(n * STEP, STEP)]
                y = xin[0][:, h, :, :]
                if layer == 0:
                    if any_yet(free(n)):
                        v.wait_ge(tr_made, free(n))
                    v.tensor_copy(xh[:, h, :, :], y).then_inc(xh_made, 1)
                    return
                if layer == 1:
                    for other in xin[1:]:
                        after(v.tensor_tensor(y, y, other[:, h, :, :], ALU.add), n)
                if layer in (2, 4):
                    masked = v.tensor_tensor(res[:, h, :, :], res[:, h, :, :], has.unsqueeze(2).broadcast_to([P, STEP, D]), ALU.mult)
                if layer == 2:
                    masked.then_inc(res_masked, 1)
                    z = xin[1][:, h, :, :]
                    v.wait_ge(upd_made, made(n))
                    after(v.tensor_tensor(z, z, upd_ps[:, 0:STEP * P].rearrange("p (b f) -> p b f", f=D), ALU.add), n)
                    after(v.scalar_tensor_tensor(y, z, 0.0, y, ALU.max, ALU.add), n)
                if layer == 3:
                    after(v.tensor_scalar(den[:, :, :], res[:, h, :, D:TW], 1.0, None, ALU.max), n)
                    after(v.reciprocal(den[:, :, :], den[:, :, :]), n)
                    after(v.tensor_tensor(den[:, :, :], den[:, :, :], has.unsqueeze(2).broadcast_to([P, STEP, HEADS]), ALU.mult), n)
                    num = res[:, h, :, 0:D].rearrange("p b (a c) -> p b a c", c=HC)
                    after(v.tensor_tensor(num, num, den[:, :, :].unsqueeze(3).broadcast_to([P, STEP, HEADS, HC]), ALU.mult), n)
                    after(v.tensor_tensor(y, y, res[:, h, :, 0:D], ALU.add), n)
                if layer == 4:
                    after(masked, n)
                    after(v.tensor_tensor(y, y, res[:, h, :, :], ALU.add), n)
                for b in range(STEP):
                    st = v.bn_stats(stats[:, b, :], y[:, b, :])
                after(st, n)
                if any_yet(made(n - 1)):
                    v.wait_ge(dev_made, made(n - 1))
                v.nop(nofuse=True)
                for b in range(STEP):
                    ag = v.bn_aggr(mv[:, b, :], stats[:, b, :])
                ag.then_inc(mv_made, 1)
                v.wait_ge(dev_made, made(n))
                after(v.reciprocal(inv[:, :], dev[:, :]), n)
                if cat:
                    if any_yet(free(n)):
                        v.wait_ge(tr_made, free(n))
                else:
                    if any_yet(landed_before(k, n_out)):
                        v.wait_ge(out_landed[h], landed_before(k, n_out))
                for b in range(STEP):
                    last = v.tensor_scalar(xh[:, h, b, :], y[:, b, :], mv[:, b, 0:1], inv[:, b:b + 1], ALU.subtract, ALU.mult)
                last.then_inc(xh_made, 1)
                assert done == chain, (layer, done)

            def back(n, h, k):
                if any_yet(landed_before(k, n_out)):
                    v.wait_ge(out_landed[h], landed_before(k, n_out))
                if seeded is not None:
                    if any_yet(landed_before(k, STEP)):
                        v.wait_ge(seeds_landed[h], landed_before(k, STEP))
                for b in range(STEP):
                    v.wait_ge(mm_made, STEP * n + b + 1)
                    v.tensor_tensor(res_out[:, h, b, :], mm_ps[(h * STEP + b) % 2][:, 0:cat], bias[:, :], ALU.add).then_inc(mm_used, 1)

            skewed(v, STEPS, front, back if cat else nothing)


def edges_sum0(nc, a, t, keep):
    with ExitStack() as ctx:
        m = Memory(nc, ctx, "edge0")
        seeds, seed = m.sb("seeds", [P, 2, TILES, D]), m.sb("seed", [P, 2, GE], BF16)
        spread = m.sb("spread", [P, 2, GE])
        digits, w = m.sb("digits", [2, 2, GE], BF16), m.sb("w", [P, 2, TILES])
        srcf, dup, flag, ix = m.sb("srcf", [P, 2, TILES]), m.sb("dup", [P, 2, TILES]), m.sb("flag", [P, TILES]), m.sb("ix", [P, 2, TILES], U32)
        away = m.sb("away", [P, TILES])
        lower, trash = m.sb("lower", [P, P]), m.sb("trash", [P, 1])
        place_value_in, place_value = m.sb("place_value_in", [2, P]), m.sb("place_value", [2, P], BF16)
        equal, masked = m.sb("equal", [P, 2, QUAD, P]), m.sb("masked", [P, QUAD, P])
        weighted, sums = m.sb("weighted", [P, 2, QUAD, D]), m.sb("sums", [P, 2, TILES, D])
        src_ps, row_ps, sum_ps = ([m.ps(f"{x}{i}", [P, QE]) for i in range(2)] for x in ("src", "row", "sum"))
        consts_in, place_value_made = m.sem("consts_in"), m.sem("place_value_made")
        edges_in = [m.sem(f"edges_in{h}") for h in range(2)]
        spread_made, src_made, equal_made, masked_made, dup_made, row_made, weighted_made, sum_made, sums_made, ix_made, ix_step = (
            m.sem(x) for x in ("spread_made", "src_made", "equal_made", "masked_made", "dup_made", "row_made", "weighted_made", "sum_made",
                               "sums_made", "ix_made", "ix_step"))
        added = [m.sem(f"added{k}") for k in range(ACCS)]
        block = ctx.enter_context(nc.Block())
        PER_ACC = TILES // ACCS
        EDGE_DMAS = 4
        IX_STEPS = 3

        @block.sync
        def _(sp):
            for to, of in ((lower, a["lower"]), (trash, a["trash"]), (place_value_in, a["place_value"])):
                sp.dma_start(to[:, :], of).then_inc(consts_in, 16)

            def load(n, h, k):
                if any_yet(QUADS * free(n)):
                    sp.wait_ge(weighted_made, QUADS * free(n))
                sp.dma_start(seed[:, h, :], row_to_all(t["seed"], n)).then_inc(edges_in[h], 16)
                sp.dma_start(seeds[:, h, :, :].rearrange("p t f -> p (t f)"), by_group(t["seeds"][0:EP, :], n)).then_inc(edges_in[h], 16)
                sp.dma_start(digits[:, h, :], t["digits"][:, bass.ds(n * GE, GE)]).then_inc(edges_in[h], 16)
                sp.dma_start(w[:, h, :], a["w_pt"][:, bass.ds(n * TILES, TILES)]).then_inc(edges_in[h], 16)

            pipelined(sp, [(at_group(load), 0)])

        @block.gpsimd
        def _(pool):
            def add(n, h, k, j):
                if j == 0:
                    pool_wait(pool, ix_made, made(n))
                pool_wait(pool, sums_made, QUADS * n + j + 1)
                for c in range(QUAD):
                    e = j * QUAD + c
                    if any_yet(16 * (PER_ACC * n + e // ACCS)):
                        pool_wait(pool, added[e % ACCS], 16 * (PER_ACC * n + e // ACCS))
                    pool.indirect_dma_start(out=t[f"acc{e % ACCS}"][:, :], out_offset=bass.IndirectOffsetOnAxis(ap=ix[:, h, e:e + 1], axis=0), in_=sums[:, h, e, :], in_offset=None, compute_op=ALU.add).then_inc(added[e % ACCS], 16)

            pipelined(pool, [(add, 0)])
            for k in range(ACCS):
                pool_wait(pool, added[k], 16 * PER_ACC * GROUPS)

        @block.tensor
        def _(pe):
            pe.wait_ge(place_value_made, 1)

            def spread_quad(n, h, k, j):
                q = QUADS * n + j
                if j == 0:
                    pe.wait_ge(edges_in[h], landed(k, EDGE_DMAS))
                    pe.wait_ge(spread_made, made(n))
                if any_yet(free(q)):
                    pe.wait_ge(equal_made, free(q))
                pe.matmul(src_ps[j % 2][:, :], place_value[:, :], digits[:, h, j * QE:(j + 1) * QE], start=True, stop=True).then_inc(src_made, 1)
                if any_yet(free(q)):
                    pe.wait_ge(weighted_made, free(q))
                for c in range(QUAD):
                    e = j * QUAD + c
                    mm = pe.matmul(row_ps[j % 2][:, c * D:(c + 1) * D], spread[:, h, e * P:(e + 1) * P], seeds[:, h, e, :], start=True, stop=True)
                mm.then_inc(row_made, 1)

            def sum_quad(n, h, k, j):
                q = QUADS * n + j
                pe.wait_ge(equal_made, made(q))
                pe.wait_ge(weighted_made, made(q))
                if any_yet(free(q)):
                    pe.wait_ge(sums_made, free(q))
                for c in range(QUAD):
                    mm = pe.matmul(sum_ps[j % 2][:, c * D:(c + 1) * D], equal[:, j % 2, c, :], weighted[:, j % 2, c, :], start=True, stop=True)
                mm.then_inc(sum_made, 1)

            pipelined(pe, [(spread_quad, 0), (sum_quad, 1)])

        @block.scalar
        def _(act):
            def weigh(n, h, k, j):
                q = QUADS * n + j
                if j == 0:
                    act.wait_ge(edges_in[h], landed(k, EDGE_DMAS))
                act.wait_ge(row_made, made(q))
                if any_yet(free(q)):
                    act.wait_ge(sum_made, free(q))
                for c in range(QUAD):
                    e = j * QUAD + c
                    ins = act.activation(weighted[:, j % 2, c, :], row_ps[j % 2][:, c * D:(c + 1) * D], ACT.Copy, scale=w[:, h, e:e + 1])
                ins.then_inc(weighted_made, 1)

            def copy_sums(n, h, k, j):
                act.wait_ge(sum_made, made(QUADS * n + j))
                for s in added:
                    if any_yet(16 * (PER_ACC * (n - 2) + j + 1)):
                        act.wait_ge(s, 16 * (PER_ACC * (n - 2) + j + 1))
                act.copy(sums[:, h, j * QUAD:(j + 1) * QUAD, :], sum_ps[j % 2][:, :].rearrange("p (c f) -> p c f", f=D)).then_inc(sums_made, 1)

            pipelined(act, [(weigh, 0), (copy_sums, 1)])

        @block.vector
        def _(v):
            v.wait_ge(consts_in, 16 * 3)
            v.tensor_copy(place_value[:, :], place_value_in[:, :]).then_inc(place_value_made, 1)

            def spread_group(n, h, k):
                v.wait_ge(edges_in[h], landed(k, EDGE_DMAS))
                if any_yet(QUADS * free(n)):
                    v.wait_ge(row_made, QUADS * free(n))
                v.tensor_copy(srcf[:, h, :], keep.src_ix[:, bass.ds(n * TILES, TILES)])
                v.tensor_scalar(spread[:, h, :], seed[:, h, :], keep.iota[:, 0:1], None, ALU.is_equal).then_inc(spread_made, 1)

            def compare(n, h, k, j):
                q = QUADS * n + j
                v.wait_ge(spread_made, made(n))
                v.wait_ge(src_made, made(q))
                if any_yet(free(q)):
                    v.wait_ge(sum_made, free(q))
                own = srcf[:, h, j * QUAD:(j + 1) * QUAD].unsqueeze(2).broadcast_to([P, QUAD, P])
                v.tensor_tensor(equal[:, j % 2, :, :], src_ps[j % 2][:, :].rearrange("p (c f) -> p c f", f=P), own, ALU.is_equal).then_inc(equal_made, 1)

            def count(n, h, k, j):
                q = QUADS * n + j
                v.wait_ge(equal_made, made(q))
                if any_yet(q):
                    v.wait_ge(dup_made, q)
                v.tensor_tensor(masked[:, :, :], equal[:, j % 2, :, :], lower[:, :].unsqueeze(1).broadcast_to([P, QUAD, P]), ALU.mult).then_inc(masked_made, 1)
                v.wait_ge(masked_made, made(q))
                v.tensor_reduce(dup[:, h, j * QUAD:(j + 1) * QUAD], masked[:, :, :], AX.X, ALU.add).then_inc(dup_made, 1)

            def indices(n, h, k):
                v.wait_ge(dup_made, QUADS * n + QUADS)
                if any_yet(n):
                    v.wait_ge(ix_made, n)
                v.tensor_scalar(away[:, :], srcf[:, h, :], -1.0, trash[:, 0:1], ALU.mult, ALU.add).then_inc(ix_step, 1)
                v.tensor_scalar(flag[:, :], dup[:, h, :], 0.0, None, ALU.is_gt).then_inc(ix_step, 1)
                v.wait_ge(ix_step, IX_STEPS * n + 2)
                v.tensor_tensor(flag[:, :], flag[:, :], away[:, :], ALU.mult).then_inc(ix_step, 1)
                v.wait_ge(ix_step, IX_STEPS * n + 3)
                for s in added:
                    if any_yet(16 * PER_ACC * free(n)):
                        v.wait_ge(s, 16 * PER_ACC * free(n))
                v.tensor_tensor(ix[:, h, :], flag[:, :], srcf[:, h, :], ALU.add).then_inc(ix_made, 1)

            pipelined(v, [(at_group(spread_group), -2), (compare, 0), (count, 0), (at_group(indices), 3)])


class Gathered:

    def __init__(self, m, width, out_width, edge_dmas):
        self.ix = m.sb("ix", [P, 2, TILES], U32)
        self.rows = m.sb("rows", [P, 2, TILES, width])
        self.out = m.sb("out", [P, 2, TILES, out_width])
        self.ix_made = m.sem("ix_made")
        self.edges_in, self.stored = ([m.sem(f"{x}{h}") for h in range(2)] for x in ("edges_in", "stored"))
        self.rows_in = [[m.sem(f"rows_in{h}_{j}") for j in range(QUADS)] for h in range(2)]
        self.edge_dmas = edge_dmas

    def gather(self, pool, table, rows_read):
        def gather_quad(n, h, k, j):
            if j == 0:
                pool_wait(pool, self.ix_made, made(n))
            if any_yet(QUADS * (n - 2) + j + 1):
                pool_wait(pool, rows_read, QUADS * (n - 2) + j + 1)
            for e in range(j * QUAD, (j + 1) * QUAD):
                pool.indirect_dma_start(out=self.rows[:, h, e, :], out_offset=None, in_=table[:, :], in_offset=bass.IndirectOffsetOnAxis(ap=self.ix[:, h, e:e + 1], axis=0)).then_inc(self.rows_in[h][j], 16)

        pipelined(pool, [(gather_quad, 0)])

    def first_indices(self, act, all_ix):
        for n in range(2):
            act.copy(self.ix[:, n, :], all_ix[:, n * TILES:(n + 1) * TILES]).then_inc(self.ix_made, 1)

    def next_indices(self, act, all_ix, n, h, k, j):
        if j == QUADS - 1 and (not isinstance(n, int) or n + 2 < GROUPS):
            for s in self.rows_in[h]:
                act.wait_ge(s, landed(k, QUAD))
            act.copy(self.ix[:, h, :], all_ix[:, bass.ds(n * TILES + 2 * TILES, TILES)]).then_inc(self.ix_made, 1)


def edges_sum1(nc, a, t, keep):
    with ExitStack() as ctx:
        m = Memory(nc, ctx, "edge1")
        g = Gathered(m, D, D, 4)
        seeds, seed, same = m.sb("seeds", [P, 2, TILES, D]), m.sb("seed", [P, 2, GE], BF16), m.sb("same", [P, 2, GE], BF16)
        dist, w_dist = m.sb("dist", [1, 2, GE]), m.sb("w_dist", [1, D])
        spread = m.sb("spread", [P, 2, GE])
        msg, run = m.sb("msg", [P, 2, QE]), m.sb("run", [P, 2, QE])
        msg_ps, turn_ps = ([m.ps(f"{x}{i}", [P, QE]) for i in range(2)] for x in ("msg", "turn"))
        consts_in = m.sem("consts_in")
        spread_made, pre_made, msg_made, run_made, turned, out_made, zeroed = (m.sem(x) for x in ("spread_made", "pre_made", "msg_made", "run_made", "turned", "out_made", "zeroed"))
        block = ctx.enter_context(nc.Block())

        @block.sync
        def _(sp):
            sp.dma_start(w_dist[:, :], a["w_dist"]).then_inc(consts_in, 16)

            def load(n, h, k):
                if any_yet(QUADS * free(n)):
                    sp.wait_ge(run_made, QUADS * free(n))
                sp.dma_start(seed[:, h, :], row_to_all(t["seed"], n)).then_inc(g.edges_in[h], 16)
                sp.dma_start(seeds[:, h, :, :].rearrange("p t f -> p (t f)"), by_group(t["seeds"][0:EP, :], n)).then_inc(g.edges_in[h], 16)
                sp.dma_start(same[:, h, :], row_to_all(t["same"], n)).then_inc(g.edges_in[h], 16)
                sp.dma_start(dist[:, h, :], a["ed_row"][:, bass.ds(n * GE, GE)]).then_inc(g.edges_in[h], 16)

            def store(n, h, k):
                sp.wait_ge(out_made, QUADS * made(n))
                sp.dma_start(by_group(t["sum1"], n), g.out[:, h, :, :].rearrange("p t f -> p (t f)")).then_inc(g.stored[h], 16)

            two_ahead(sp, GROUPS, load, store)
            for h in range(2):
                sp.wait_ge(g.stored[h], landed(GROUPS // 2 - 1, 1))

        @block.gpsimd
        def _(pool):
            g.gather(pool, t["a1"], pre_made)

        @block.tensor
        def _(pe):
            pe.wait_ge(consts_in, 16)

            def sum_quad(n, h, k, j):
                q = QUADS * n + j
                if j == 0:
                    pe.wait_ge(g.edges_in[h], landed(k, g.edge_dmas))
                    pe.wait_ge(spread_made, made(n))
                ps = msg_ps[j % 2]
                if any_yet(free(q)):
                    pe.wait_ge(msg_made, free(q))
                pe.matmul(ps[:, :], w_dist[:, :], dist[:, h, j * QE:(j + 1) * QE], start=True, stop=False)
                for c in range(QUAD):
                    e = j * QUAD + c
                    pe.matmul(ps[:, c * P:(c + 1) * P], seeds[:, h, e, :], spread[:, h, e * P:(e + 1) * P], start=False, stop=False)
                pe.wait_ge(g.rows_in[h][j], landed(k, QUAD))
                for c in range(QUAD):
                    mm = pe.matmul(ps[:, c * P:(c + 1) * P], g.rows[:, h, j * QUAD + c, :], keep.ident[:, :], start=False, stop=c == QUAD - 1)
                mm.then_inc(pre_made, 1)

            def turn_quad(n, h, k, j):
                q = QUADS * n + j
                pe.wait_ge(run_made, made(q))
                if any_yet(free(q)):
                    pe.wait_ge(out_made, free(q))
                for c in range(QUAD):
                    mm = pe.transpose(turn_ps[j % 2][:, c * P:(c + 1) * P], run[:, j % 2, c * P:(c + 1) * P], keep.ident[:, :])
                mm.then_inc(turned, 1)

            pipelined(pe, [(sum_quad, 0), (turn_quad, 1)])

        @block.scalar
        def _(act):
            def relu(n, h, k, j):
                q = QUADS * n + j
                act.wait_ge(pre_made, made(q))
                if any_yet(free(q)):
                    act.wait_ge(run_made, free(q))
                act.activation(msg[:, j % 2, :], msg_ps[j % 2][:, :], ACT.Relu).then_inc(msg_made, 1)
                g.next_indices(act, keep.src_ix, n, h, k, j)

            def copy_out(n, h, k, j):
                if j == 0 and any_yet(landed_before(k, 1)):
                    act.wait_ge(g.stored[h], landed_before(k, 1))
                act.wait_ge(turned, made(QUADS * n + j))
                act.copy(g.out[:, h, j * QUAD:(j + 1) * QUAD, :], turn_ps[j % 2][:, :].rearrange("p (c f) -> p c f", f=D)).then_inc(out_made, 1)

            g.first_indices(act, keep.src_ix)
            pipelined(act, [(relu, 0), (copy_out, 1)])

        @block.vector
        def _(v):
            v.memset(run[:, 1, QE - 1:QE], 0.0).then_inc(zeroed, 1)
            v.wait_ge(zeroed, 1)

            def spread_group(n, h, k):
                v.wait_ge(g.edges_in[h], landed(k, g.edge_dmas))
                if any_yet(QUADS * free(n)):
                    v.wait_ge(pre_made, QUADS * free(n))
                v.tensor_scalar(spread[:, h, :], seed[:, h, :], keep.iota[:, 0:1], None, ALU.is_equal).then_inc(spread_made, 1)

            def scan(n, h, k, j):
                q = QUADS * n + j
                v.wait_ge(msg_made, made(q))
                if any_yet(free(q)):
                    v.wait_ge(turned, free(q))
                if any_yet(q):
                    v.wait_ge(run_made, q)
                v.tensor_tensor_scan(run[:, j % 2, :], same[:, h, j * QE:(j + 1) * QE], msg[:, j % 2, :], run[:, (j - 1) % 2, QE - 1:QE], ALU.mult, ALU.add).then_inc(run_made, 1)

            pipelined(v, [(at_group(spread_group), -1), (scan, 0)])


def edges_max3(nc, a, t, keep):
    with ExitStack() as ctx:
        m = Memory(nc, ctx, "edge3")
        g = Gathered(m, D, D, 1)
        far, run = m.sb("far", [P, 2, GE], BF16), m.sb("run", [P, 2, QE])
        in_ps, turn_ps = ([m.ps(f"{x}{i}", [P, QE]) for i in range(2)] for x in ("in", "turn"))
        turned_in, run_made, turned, out_made, zeroed = (m.sem(x) for x in ("turned_in", "run_made", "turned", "out_made", "zeroed"))
        block = ctx.enter_context(nc.Block())

        @block.sync
        def _(sp):
            def load(n, h, k):
                if any_yet(QUADS * free(n)):
                    sp.wait_ge(run_made, QUADS * free(n))
                sp.nop(nofuse=True)
                sp.dma_start(far[:, h, :], row_to_all(t["far"], n)).then_inc(g.edges_in[h], 16)

            def store(n, h, k):
                sp.wait_ge(out_made, QUADS * made(n))
                sp.dma_start(by_group(t["max3"], n), g.out[:, h, :, :].rearrange("p t f -> p (t f)")).then_inc(g.stored[h], 16)

            two_ahead(sp, GROUPS, load, store)
            for h in range(2):
                sp.wait_ge(g.stored[h], landed(GROUPS // 2 - 1, 1))

        @block.gpsimd
        def _(pool):
            g.gather(pool, t["rel"], turned_in)

        @block.tensor
        def _(pe):
            def turn_in(n, h, k, j):
                q = QUADS * n + j
                pe.wait_ge(g.rows_in[h][j], landed(k, QUAD))
                if any_yet(free(q)):
                    pe.wait_ge(run_made, free(q))
                for c in range(QUAD):
                    mm = pe.transpose(in_ps[j % 2][:, c * P:(c + 1) * P], g.rows[:, h, j * QUAD + c, :], keep.ident[:, :])
                mm.then_inc(turned_in, 1)

            def turn_out(n, h, k, j):
                q = QUADS * n + j
                pe.wait_ge(run_made, made(q))
                if any_yet(free(q)):
                    pe.wait_ge(out_made, free(q))
                for c in range(QUAD):
                    mm = pe.transpose(turn_ps[j % 2][:, c * P:(c + 1) * P], run[:, j % 2, c * P:(c + 1) * P], keep.ident[:, :])
                mm.then_inc(turned, 1)

            pipelined(pe, [(turn_in, 0), (turn_out, 1)])

        @block.scalar
        def _(act):
            def copy_out(n, h, k, j):
                if j == 0 and any_yet(landed_before(k, 1)):
                    act.wait_ge(g.stored[h], landed_before(k, 1))
                act.wait_ge(turned, made(QUADS * n + j))
                act.copy(g.out[:, h, j * QUAD:(j + 1) * QUAD, :], turn_ps[j % 2][:, :].rearrange("p (c f) -> p c f", f=D)).then_inc(out_made, 1)
                g.next_indices(act, keep.rel_ix, n, h, k, j)

            g.first_indices(act, keep.rel_ix)
            pipelined(act, [(copy_out, 0)])

        @block.vector
        def _(v):
            v.memset(run[:, 1, QE - 1:QE], 0.0).then_inc(zeroed, 1)
            v.wait_ge(zeroed, 1)

            def scan(n, h, k, j):
                q = QUADS * n + j
                if j == 0:
                    v.wait_ge(g.edges_in[h], landed(k, 1))
                v.wait_ge(turned_in, made(q))
                if any_yet(free(q)):
                    v.wait_ge(turned, free(q))
                if any_yet(q):
                    v.wait_ge(run_made, q)
                v.tensor_tensor_scan(run[:, j % 2, :], far[:, h, j * QE:(j + 1) * QE], in_ps[j % 2][:, :], run[:, (j - 1) % 2, QE - 1:QE], ALU.add, ALU.max).then_inc(run_made, 1)

            pipelined(v, [(scan, 0)])


def edges_attend2(nc, a, t, keep):
    with ExitStack() as ctx:
        m = Memory(nc, ctx, "edge2")
        g = Gathered(m, 2 * D, TW, 3)
        seeds, seed, far = m.sb("seeds", [P, 2, TILES, D]), m.sb("seed", [P, 2, GE], BF16), m.sb("far", [P, 2, GE], BF16)
        heads, negident = m.sb("heads", [P, P]), m.sb("negident", [P, P])
        spread = m.sb("spread", [P, 2, GE])
        q_sb, prod, top = m.sb("q", [P, 2, QE]), m.sb("prod", [P, 2, QE]), m.sb("top", [P, 2, QE + 1])
        fall, fade, ex, val = m.sb("fall", [P, 2, QE]), m.sb("fade", [P, 2, QE]), m.sb("ex", [P, 2, QE]), m.sb("val", [P, 2, QE])
        num, den = m.sb("num", [P, 2, QE]), m.sb("den", [P, 2, QE])
        q_ps, k_ps, s_ps0, s_ps1, s_ps2, v_ps, num_ps, den_ps = (m.ps(x, [P, QE]) for x in ("q", "k", "s0", "s1", "s2", "v", "num", "den"))
        s_ps = [s_ps0, s_ps1]
        consts_in, zeroed = m.sem("consts_in"), m.sem("zeroed")
        (spread_made, q_spread, q_made, k_turned, prod_made, s_made, top_made, fall_made, s_less, fade_made, ex_made, v_turned, val_made,
         num_made, den_made, num_turned, den_turned, num_out, den_out) = (m.sem(x) for x in (
             "spread_made", "q_spread", "q_made", "k_turned", "prod_made", "s_made", "top_made", "fall_made", "s_less", "fade_made",
             "ex_made", "v_turned", "val_made", "num_made", "den_made", "num_turned", "den_turned", "num_out", "den_out"))
        diff_made, carried = m.sem("diff_made"), m.sem("carried")
        block = ctx.enter_context(nc.Block())

        @block.sync
        def _(sp):
            sp.dma_start(heads[:, :], a["heads"]).then_inc(consts_in, 16)
            sp.dma_start(negident[:, :], a["negident"]).then_inc(consts_in, 16)

            def load(n, h, k):
                if any_yet(QUADS * free(n)):
                    sp.wait_ge(fall_made, QUADS * free(n))
                sp.dma_start(seed[:, h, :], row_to_all(t["seed"], n)).then_inc(g.edges_in[h], 16)
                sp.dma_start(seeds[:, h, :, :].rearrange("p t f -> p (t f)"), by_group(t["seeds"][0:EP, :], n)).then_inc(g.edges_in[h], 16)
                sp.dma_start(far[:, h, :], row_to_all(t["far"], n)).then_inc(g.edges_in[h], 16)

            def store(n, h, k):
                sp.wait_ge(num_out, QUADS * made(n))
                sp.wait_ge(den_out, QUADS * made(n))
                sp.dma_start(by_group(t["sum2"], n), g.out[:, h, :, :].rearrange("p t f -> p (t f)")).then_inc(g.stored[h], 16)

            two_ahead(sp, GROUPS, load, store)
            for h in range(2):
                sp.wait_ge(g.stored[h], landed(GROUPS // 2 - 1, 1))

        @block.gpsimd
        def _(pool):
            g.gather(pool, t["kv"], v_turned)

        @block.tensor
        def _(pe):
            pe.wait_ge(consts_in, 16 * 2)

            def queries_keys(n, h, k, j):
                q = QUADS * n + j
                if j == 0:
                    pe.wait_ge(g.edges_in[h], landed(k, g.edge_dmas))
                    pe.wait_ge(spread_made, made(n))
                if any_yet(q):
                    pe.wait_ge(q_made, q)
                for c in range(QUAD):
                    e = j * QUAD + c
                    mm = pe.matmul(q_ps[:, c * P:(c + 1) * P], seeds[:, h, e, :], spread[:, h, e * P:(e + 1) * P], start=True, stop=True)
                mm.then_inc(q_spread, 1)
                pe.wait_ge(g.rows_in[h][j], landed(k, QUAD))
                if any_yet(q):
                    pe.wait_ge(prod_made, q)
                for c in range(QUAD):
                    mm = pe.transpose(k_ps[:, c * P:(c + 1) * P], g.rows[:, h, j * QUAD + c, 0:D], keep.ident[:, :])
                mm.then_inc(k_turned, 1)

            def scores(n, h, k, j):
                q = QUADS * n + j
                pe.wait_ge(prod_made, made(q))
                if any_yet(free(q)):
                    pe.wait_ge(ex_made, free(q))
                pe.matmul(s_ps[j % 2][:, :], heads[:, :], prod[:, j % 2, :], start=True, stop=False, skip_group_check=True).then_inc(s_made, 1)

            def values(n, h, k, j):
                q = QUADS * n + j
                if any_yet(q):
                    pe.wait_ge(val_made, q)
                for c in range(QUAD):
                    mm = pe.transpose(v_ps[:, c * P:(c + 1) * P], g.rows[:, h, j * QUAD + c, D:2 * D], keep.ident[:, :])
                mm.then_inc(v_turned, 1)

            def less_top(n, h, k, j):
                q = QUADS * n + j
                pe.wait_ge(top_made, made(q))
                pe.matmul(s_ps[j % 2][:, :], negident[:, :], top[:, j % 2, 1:QE + 1], start=False, stop=True, skip_group_check=True).then_inc(s_less, 1)

            def turn_out(n, h, k, j):
                q = QUADS * n + j
                pe.wait_ge(num_made, made(q))
                if any_yet(q):
                    pe.wait_ge(num_out, q)
                for c in range(QUAD):
                    mm = pe.transpose(num_ps[:, c * P:(c + 1) * P], num[:, j % 2, c * P:(c + 1) * P], keep.ident[:, :])
                mm.then_inc(num_turned, 1)
                pe.wait_ge(den_made, made(q))
                if any_yet(q):
                    pe.wait_ge(den_out, q)
                for c in range(QUAD):
                    mm = pe.transpose(den_ps[:, c * P:(c + 1) * P], den[:, j % 2, c * P:(c + 1) * P], keep.ident[:, :])
                mm.then_inc(den_turned, 1)

            pipelined(pe, [(less_top, 2), (queries_keys, 0), (scores, 1), (values, 2), (turn_out, 3)])

        @block.scalar
        def _(act):
            def copy_q(n, h, k, j):
                q = QUADS * n + j
                act.wait_ge(q_spread, made(q))
                if any_yet(free(q)):
                    act.wait_ge(prod_made, free(q))
                act.copy(q_sb[:, j % 2, :], q_ps[:, :]).then_inc(q_made, 1)

            def exps(n, h, k, j):
                q = QUADS * n + j
                act.wait_ge(s_less, made(q))
                if any_yet(free(q)):
                    act.wait_ge(den_made, free(q))
                act.activation(ex[:, j % 2, :], s_ps[j % 2][:, :], ACT.Exp).then_inc(ex_made, 1)
                act.wait_ge(fall_made, made(q))
                act.activation(fade[:, j % 2, :], fall[:, j % 2, :], ACT.Exp).then_inc(fade_made, 1)

            def copy_out(n, h, k, j):
                q = QUADS * n + j
                if j == 0 and any_yet(landed_before(k, 1)):
                    act.wait_ge(g.stored[h], landed_before(k, 1))
                act.wait_ge(num_turned, made(q))
                act.copy(g.out[:, h, j * QUAD:(j + 1) * QUAD, 0:D], num_ps[:, :].rearrange("p (c f) -> p c f", f=D)).then_inc(num_out, 1)
                act.wait_ge(den_turned, made(q))
                act.copy(g.out[:, h, j * QUAD:(j + 1) * QUAD, D:TW], den_ps[:, :].rearrange("p (c a f) -> p c a f", c=QUAD, f=HC)[:, :, :, 0]).then_inc(den_out, 1)

            def indices(n, h, k, j):
                g.next_indices(act, keep.src_ix, n, h, k, j)

            g.first_indices(act, keep.src_ix)
            pipelined(act, [(exps, 2), (copy_q, 0), (copy_out, 3), (indices, 1)])

        @block.vector
        def _(v):
            v.memset(top[:, 1, QE:QE + 1], 0.0).then_inc(zeroed, 1)
            v.memset(num[:, 1, QE - 1:QE], 0.0).then_inc(zeroed, 1)
            v.memset(den[:, 1, QE - 1:QE], 0.0).then_inc(zeroed, 1)
            v.wait_ge(zeroed, 3)

            def spread_group(n, h, k):
                v.wait_ge(g.edges_in[h], landed(k, g.edge_dmas))
                if any_yet(QUADS * free(n)):
                    v.wait_ge(q_spread, QUADS * free(n))
                v.tensor_scalar(spread[:, h, :], seed[:, h, :], keep.iota[:, 0:1], None, ALU.is_equal).then_inc(spread_made, 1)

            def products(n, h, k, j):
                q = QUADS * n + j
                v.wait_ge(q_made, made(q))
                v.wait_ge(k_turned, made(q))
                if any_yet(free(q)):
                    v.wait_ge(s_made, free(q))
                v.tensor_tensor(prod[:, j % 2, :], k_ps[:, :], q_sb[:, j % 2, :], ALU.mult).then_inc(prod_made, 1)

            def maxima(n, h, k, j):
                q = QUADS * n + j
                if any_yet(free(q)):
                    v.wait_ge(s_less, free(q))
                v.tensor_copy(top[:, j % 2, 0:1], top[:, (j - 1) % 2, QE:QE + 1]).then_inc(carried, 1)
                v.wait_ge(s_made, made(q))
                v.wait_ge(carried, made(q))
                v.tensor_tensor_scan(top[:, j % 2, 1:QE + 1], far[:, h, j * QE:(j + 1) * QE], s_ps[j % 2][:, :], top[:, j % 2, 0:1], ALU.add, ALU.max).then_inc(top_made, 1)

            def falls(n, h, k, j):
                q = QUADS * n + j
                v.wait_ge(top_made, made(q))
                if any_yet(free(q)):
                    v.wait_ge(fade_made, free(q))
                v.tensor_tensor(fall[:, j % 2, :], top[:, j % 2, 0:QE], top[:, j % 2, 1:QE + 1], ALU.subtract).then_inc(diff_made, 1)
                v.wait_ge(diff_made, made(q))
                v.tensor_tensor(fall[:, j % 2, :], fall[:, j % 2, :], far[:, h, j * QE:(j + 1) * QE], ALU.add).then_inc(fall_made, 1)

            def sums(n, h, k, j):
                q = QUADS * n + j
                v.wait_ge(ex_made, made(q))
                v.wait_ge(v_turned, made(q))
                if any_yet(q):
                    v.wait_ge(den_made, q)
                v.tensor_tensor(val[:, j % 2, :], v_ps[:, :], ex[:, j % 2, :], ALU.mult).then_inc(val_made, 1)
                v.wait_ge(fade_made, made(q))
                if any_yet(free(q)):
                    v.wait_ge(den_turned, free(q))
                v.tensor_tensor_scan(den[:, j % 2, :], fade[:, j % 2, :], ex[:, j % 2, :], den[:, (j - 1) % 2, QE - 1:QE], ALU.mult, ALU.add).then_inc(den_made, 1)
                v.wait_ge(val_made, made(q))
                v.tensor_tensor_scan(num[:, j % 2, :], fade[:, j % 2, :], val[:, j % 2, :], num[:, (j - 1) % 2, QE - 1:QE], ALU.mult, ALU.add).then_inc(num_made, 1)

            pipelined(v, [(at_group(spread_group), -1), (maxima, 1), (products, 0), (falls, 1), (sums, 2)])


def build(nc, a, out):
    ctx = ExitStack()
    with ctx:
        def dram(name, shape, dt=F32):
            return nc.dram_tensor(name, shape, dt, kind="Internal").ap()

        t = {"x": a["x"]}
        for name in ("same", "far", "seed"):
            t[name] = dram(name, (1, EP), BF16)
        t["digits"] = dram("digits", (2, EP), BF16)
        t["rs"] = dram("rs", (FB * P,))
        t["seeds"] = dram("seeds", (EP + NP, D))
        for k in range(ACCS):
            t[f"acc{k}"] = dram(f"acc{k}", (NP + P, D))
        for name in ("nodes", "a1", "own1", "upd", "own2", "own3"):
            t[name] = dram(name, (NP, D))
        t["kv"] = dram("kv", (NP, 2 * D))
        rel = t["rel"] = dram("rel", (RELS * NP, D))
        for r in range(RELS):
            t[f"rel{r}"] = rel[r * NP:(r + 1) * NP, :]
        t["sum1"], t["sum2"], t["max3"] = dram("sum1", (EP, D)), dram("sum2", (EP, TW)), dram("max3", (EP, D))

        class Keep:
            pass

        keep, m = Keep(), Memory(nc, ctx, "keep")
        keep.ident, keep.iota, keep.eps = m.sb("ident", [P, P]), m.sb("iota", [P, 1]), m.sb("eps", [P, 1])
        keep.has, keep.last_ix, keep.seed_ix = m.sb("has", [P, NB]), m.sb("lastix", [P, NB], U32), m.sb("seedix", [P, NB], U32)
        keep.first_ix = m.sb("firstix", [GROUPS, TILES], U32)
        keep.src_ix, keep.rel_ix = m.sb("srcix", [P, NT], U32), m.sb("relix", [P, NT], U32)

        prologue(nc, a, t, keep)
        node_phase(nc, a, t, keep, 0, out)
        seed_tiles(nc, t, keep, "tiles0")
        edges_sum0(nc, a, t, keep)
        node_phase(nc, a, t, keep, 1, out)
        seed_tiles(nc, t, keep, "tiles1")
        edges_sum1(nc, a, t, keep)
        node_phase(nc, a, t, keep, 2, out)
        seed_tiles(nc, t, keep, "tiles2")
        edges_attend2(nc, a, t, keep)
        node_phase(nc, a, t, keep, 3, out)
        edges_max3(nc, a, t, keep)
        node_phase(nc, a, t, keep, 4, out)


def constants():
    p, e = np.arange(P), np.arange(GE) % P
    node = lambda blocks: (np.arange(blocks)[None, :] * P + p[:, None]).astype(np.float32)
    return {
        "ident": np.eye(P, dtype=np.float32),
        "negident": -np.eye(P, dtype=np.float32),
        "iota": p[:, None].astype(np.float32),
        "eps": np.full((P, 1), EPS, np.float32),
        "place": np.broadcast_to(e, (GROUPS, GE)).astype(np.float32),
        "inside": np.broadcast_to(e > 0, (GROUPS, GE)).astype(np.float32),
        "nid": node(FB),
        "spare": node(NB) + EP,
        "lower": np.tri(P, P, -1, dtype=np.float32),
        "trash": (NP + p[:, None]).astype(np.float32),
        "place_value": np.repeat([[float(P)], [1.0]], P, 1).astype(np.float32),
        "heads": (np.kron(np.eye(HEADS), np.ones((HC, HC))) / np.sqrt(HC)).astype(np.float32),
    }


def laid_out(i):
    def filled(x, rows, value):
        x = np.asarray(x)
        return np.concatenate([x, np.full((rows - len(x), *x.shape[1:]), value, x.dtype)])

    def by_partition(x):
        return np.ascontiguousarray(x.reshape(NT, P).T)

    g = {k: np.asarray(v) for k, v in i.items()}
    src, dst = filled(g["src"], EP, N), filled(g["dst"], EP, NP - 1)
    zero = np.zeros(D, np.float32)
    msg, upd = g["L1_gnn_W_msg"], g["L1_gnn_W_upd"]
    rel_w, rel_b = g["L3_gnn_weight"], g["L3_gnn_bias"]
    return {
        "x": filled(g["x"], NP, 0),
        "src_flat": src, "src_pt": by_partition(src),
        "dst_prev": np.concatenate([np.array([-1], dst.dtype), dst]),
        "dst_tiles": dst.reshape(NT, P), "dst_first": np.ascontiguousarray(dst[::P]),
        "typ_pt": by_partition(filled(g["edge_type_4"], EP, 0)),
        "w_pt": by_partition(filled(g["edge_weight"], EP, 0)),
        "ed_row": filled(g["edge_weight1"], EP, 0).reshape(1, EP),
        "w0": np.ascontiguousarray(g["L0_gnn_W"].T), "b0": g["L0_gnn_b"],
        "w1": np.concatenate([msg[:D], msg[D:2 * D], g["L1_gnn_W_res"], upd[:D]], 1),
        "b1": np.concatenate([zero, g["L1_gnn_b_msg"], zero, g["L1_gnn_b_upd"]]),
        "w_dist": msg[2 * D:], "w_upd": upd[D:],
        "w2": np.concatenate([g[f"L2_gnn_W{x}"] for x in "kvqr"], 1),
        "b2": np.concatenate([g[f"L2_gnn_b{x}"] for x in "kvqr"]),
        "w3": np.concatenate(list(rel_w), 1), "b3": rel_b.reshape(-1),
    }


def kernel(**inputs):
    import concourse.bacc as bacc
    from concourse.bass_utils import run_bass_kernel_spmd

    nc = bacc.Bacc("TRN2", target_bir_lowering=False, num_devices=1)
    arrays = {f"in_{k}": np.ascontiguousarray(v) for k, v in {**laid_out(inputs), **constants()}.items()}
    a = {k[3:]: nc.dram_tensor(k, v.shape, mybir.dt.from_np(v.dtype), kind="ExternalInput").ap() for k, v in arrays.items()}
    out = nc.dram_tensor("out", (NP, D), F32, kind="ExternalOutput").ap()
    build(nc, a, out)
    r = run_bass_kernel_spmd(nc, [arrays], core_ids=[0])
    return r.results[0]["out"][:N]
```

```python
from contextlib import ExitStack

import concourse.bass as bass
import numpy as np
from concourse import mybir

F32, BF16, I32, U32 = mybir.dt.float32, mybir.dt.bfloat16, mybir.dt.int32, mybir.dt.uint32
ALU, ACT, AX = mybir.AluOpType, mybir.ActivationFunctionType, mybir.AxisListType

P = 128
D = 128
N, E = 12500, 200000
QUAD = 4
QE = QUAD * P
TILES = 16
QUADS = TILES // QUAD
GE = TILES * P
GROUPS = -(-E // GE)
EP = GROUPS * GE
NT = EP // P
NB = -(-N // P)
NP = NB * P
STEP = 7
STEPS = NB // STEP
FB, FSTEP = 100, 10
HEADS, HC = 4, 32
RELS = 4
CHUNKS = -(-NT // P)
ACCS = 4
TW = D + HEADS
FAR = 3.0e38
EPS = 1e-5


def made(n):
    return n + 1


def free(n):
    return n - 1


def landed(k, dmas):
    return 16 * dmas * (k + 1)


def landed_before(k, dmas):
    return 16 * dmas * k


def any_yet(count):
    return not isinstance(count, int) or count > 0


def skewed(eng, steps, front, back):
    last = steps // 2 - 1
    front(0, 0, 0)
    front(1, 1, 0)
    back(0, 0, 0)
    front(2, 0, 1)
    back(1, 1, 0)
    with eng.Fori(1, last) as i:
        front(2 * i + 1, 1, i)
        back(2 * i, 0, i)
        front(2 * i + 2, 0, i + 1)
        back(2 * i + 1, 1, i)
    front(steps - 1, 1, last)
    back(steps - 2, 0, last)
    back(steps - 1, 1, last)


def two_ahead(eng, steps, front, back):
    last = steps // 2 - 1
    front(0, 0, 0)
    front(1, 1, 0)

    def both(i):
        front(2 * i + 2, 0, i + 1)
        back(2 * i, 0, i)
        front(2 * i + 3, 1, i + 1)
        back(2 * i + 1, 1, i)

    both(0)
    with eng.Fori(1, last) as i:
        both(i)
    back(steps - 2, 0, last)
    back(steps - 1, 1, last)


def stepped(eng, stages):
    last = STEPS // 2 - 1
    ahead = (1 + max(lead for _, lead in stages)) // 2

    def step(i, s):
        for stage, lead in stages:
            shift, h = divmod(s + lead, 2)
            k = i + shift
            if isinstance(k, int) and not 0 <= k <= last:
                continue
            stage(2 * k + h, h, k)

    for s in range(-max(lead for _, lead in stages), 2):
        step(0, s)
    with eng.Fori(1, last + 1 - ahead) as i:
        step(i, 0)
        step(i, 1)
    for s in range(2 * ahead):
        step(last + 1 - ahead, s)


def pipelined(eng, stages):
    body = 2 * QUADS
    last = GROUPS // 2 - 1

    def quad(i, q):
        for stage, lag in stages:
            shift, at = divmod(q - lag, body)
            k = i + shift
            if isinstance(k, int) and not 0 <= k <= last:
                continue
            stage(2 * k + at // QUADS, at // QUADS, k, at % QUADS)

    for q in range(min(lag for _, lag in stages), body):
        quad(0, q)
    with eng.Fori(1, last) as i:
        for q in range(body):
            quad(i, q)
    for q in range(body + max(lag for _, lag in stages)):
        quad(last, q)


def at_group(stage):
    return lambda n, h, k, j: stage(n, h, k) if j == 0 else None


def pool_wait(pool, sem, value):
    pool.wait_ge(sem, value)
    pool.nop(nofuse=True)


class Memory:
    def __init__(self, nc, ctx, phase):
        self.nc, self.ctx, self.phase, self.sems = nc, ctx, phase, []
        ctx.callback(self.release)

    def sb(self, name, shape, dt=F32):
        return self.ctx.enter_context(self.nc.sbuf_tensor(f"{self.phase}_{name}", shape, dt))

    def ps(self, name, shape):
        return self.ctx.enter_context(self.nc.psum_tensor(f"{self.phase}_{name}_psum", shape, F32))

    def sem(self, name):
        self.sems.append(self.nc.alloc_semaphore(name=f"{self.phase}_{name}"))
        return self.sems[-1]

    def release(self):
        if self.sems:
            self.nc.clear_and_free_semaphores(self.sems)
            self.nc.all_engine_barrier()


def by_group(flat, n):
    return flat.rearrange("(g p t) f -> p g (t f)", p=P, t=TILES)[:, bass.ds(n, 1), :].rearrange("p o e -> p (o e)")


def edge_row(v, after, row, edge, part, part2):
    after(v.tensor_scalar(part, edge, P - 1, 4, ALU.bitwise_and, ALU.logical_shift_left))
    after(v.tensor_scalar(part2, edge, 7, TILES - 1, ALU.logical_shift_right, ALU.bitwise_and))
    after(v.tensor_tensor(part, part, part2, ALU.bitwise_or))
    after(v.tensor_scalar(part2, edge, 11, 11, ALU.logical_shift_right, ALU.logical_shift_left))
    after(v.tensor_tensor(row, part, part2, ALU.bitwise_or))


def by_step(flat, n):
    return flat.rearrange("(b p) f -> p b f", p=P)[:, bass.ds(n * STEP, STEP), :]


def row_to_all(row, n):
    return row[0:1, bass.ds(n * GE, GE)].broadcast_to([P, GE])


def prologue(nc, a, t, keep):
    with ExitStack() as ctx:
        m = Memory(nc, ctx, "pro")
        cur, prev, src = m.sb("cur", [GROUPS, GE], I32), m.sb("prev", [GROUPS, GE], I32), m.sb("src", [GROUPS, GE], I32)
        place, inside = m.sb("place", [GROUPS, GE]), m.sb("inside", [GROUPS, GE])
        same, far, seed = m.sb("same", [GROUPS, GE], BF16), m.sb("far", [GROUPS, GE], BF16), m.sb("seed", [GROUPS, GE], BF16)
        starts, digit = m.sb("starts", [GROUPS, GE]), m.sb("digit", [GROUPS, GE], I32)
        digits = m.sb("digits", [GROUPS, 2, GE], BF16)
        typ = m.sb("typ", [P, NT], I32)
        first, low, high = (m.sb(x, [P, CHUNKS], I32) for x in ("first", "low", "high"))
        lowf, highf = m.sb("lowf", [P, CHUNKS]), m.sb("highf", [P, CHUNKS])
        low_hot, high_hot = m.sb("low_hot", [P, CHUNKS, P]), m.sb("high_hot", [P, CHUNKS, FB])
        place_row, upper, ones = m.sb("place_row", [P, P]), m.sb("upper", [P, P]), m.sb("ones", [P, P])
        hist, smaller = m.sb("hist", [P, FB]), m.sb("smaller", [P, FB])
        hist_ps, within_ps, total_ps = m.ps("hist", [P, FB]), m.ps("smaller", [P, FB]), m.ps("total", [P, FB])
        nid = m.sb("nid", [P, FB])
        spare = m.sb("spare", [P, NB])
        before, tile_of, within, rs = (m.sb(x, [P, FB]) for x in ("before", "tileof", "within", "rs"))
        tile_ix = m.sb("tileix", [P, FB], U32)
        stage = m.sb("stage", [P, 2, FSTEP], U32)
        rows = m.sb("rows", [P, 2, FSTEP, P], I32)
        junk2 = m.sb("junk2", [P, P])
        rs_next = m.sb("rsnext", [P, NB])
        edge, part, part2 = (m.sb(x, [P, NB], I32) for x in ("edge", "part", "part2"))
        zero = m.sb("zero", [P, TILES * D])
        consts_in, edges_in, more_in = m.sem("consts_in"), m.sem("edges_in"), m.sem("more_in")
        dve, zeroed, stored, rs_out, rs_in = m.sem("dve"), [m.sem("zeroed0"), m.sem("zeroed1")], m.sem("stored"), m.sem("rs_out"), m.sem("rs_in")
        within_made = m.sem("within_made")
        hot_made, hist_made, hist_copied, smaller_made = m.sem("hot_made"), m.sem("hist_made"), m.sem("hist_copied"), m.sem("smaller_made")
        zero_made, staged, counted = m.sem("zero_made"), m.sem("staged"), m.sem("counted")
        rows_in = [m.sem("rows_in0"), m.sem("rows_in1")]
        rows_ready = m.sem("rows_ready")
        block = ctx.enter_context(nc.Block())
        ROWS_READY = 3
        seeds = t["seeds"]

        @block.sync
        def _(sp):
            for to, of in ((nid, a["nid"]), (spare, a["spare"]), (keep.ident, a["ident"]), (keep.iota, a["iota"]), (keep.eps, a["eps"]), (first, a["first_pt"]), (place_row, a["place_row"]), (upper, a["upper"]), (keep.first_ix, a["dst_first"].rearrange("(g t) -> g t", t=TILES).bitcast(U32))):
                sp.dma_start(to[:, :], of).then_inc(consts_in, 16)
            sp.dma_start(cur[:, :], a["dst_prev"][1:1 + EP].rearrange("(g e) -> g e", e=GE)).then_inc(edges_in, 16)
            sp.dma_start(prev[:, :], a["dst_prev"][0:EP].rearrange("(g e) -> g e", e=GE)).then_inc(edges_in, 16)
            sp.dma_start(place[:, :], a["place"]).then_inc(edges_in, 16)
            sp.dma_start(inside[:, :], a["inside"]).then_inc(edges_in, 16)
            sp.dma_start(src[:, :], a["src_flat"].rearrange("(g e) -> g e", e=GE)).then_inc(more_in, 16)
            sp.dma_start(typ[:, :], a["typ_pt"]).then_inc(more_in, 16)
            sp.dma_start(keep.src_ix[:, :], a["src_pt"].bitcast(U32)).then_inc(more_in, 16)
            sp.wait_ge(rows_ready, ROWS_READY)
            sp.dma_start(t["same"].rearrange("o (g e) -> (o g) e", e=GE), same[:, :]).then_inc(stored, 16)
            sp.dma_start(t["far"].rearrange("o (g e) -> (o g) e", e=GE), far[:, :]).then_inc(stored, 16)
            sp.dma_start(t["seed"].rearrange("o (g e) -> (o g) e", e=GE), seed[:, :]).then_inc(stored, 16)
            sp.dma_start(t["digits"].rearrange("d (g e) -> g d e", e=GE), digits[:, :, :]).then_inc(stored, 16)
            sp.wait_ge(counted, 1)
            with nc.allow_non_contiguous_dma("a node's number per partition"):
                sp.dma_start(t["rs"][0:FB * P].rearrange("(b p) -> p b", p=P), rs[:, :]).then_inc(rs_out, 16)
                sp.wait_ge(rs_out, 16)
                sp.dma_start(rs_next[:, :], t["rs"][1:1 + NP].rearrange("(b p) -> p b", p=P)).then_inc(rs_in, 16)
            sp.wait_ge(stored, 16 * 4)

        @block.scalar
        def _(act):
            act.wait_ge(zero_made, 1)

            def clear(g, h, k):
                if any_yet(k):
                    act.wait_ge(zeroed[h], 16 * k)
                act.dma_start(seeds[bass.ds(g * GE, GE), :].rearrange("(p t) f -> p (t f)", p=P), zero[:, :]).then_inc(zeroed[h], 16)

            for g in range(2):
                clear(g, g, 0)
            with act.Fori(1, GROUPS // 2) as i:
                for h in range(2):
                    clear(2 * i + h, h, i)
            for h in range(2):
                act.wait_ge(zeroed[h], 16 * (GROUPS // 2))

        @block.tensor
        def _(pe):
            pe.wait_ge(hot_made, 1)
            for c in range(CHUNKS):
                mm = pe.matmul(hist_ps[:, :], low_hot[:, c, :], high_hot[:, c, :], start=c == 0, stop=c == CHUNKS - 1)
            mm.then_inc(hist_made, 1)
            pe.wait_ge(hist_copied, 1)
            pe.matmul(within_ps[:, :], upper[:, :], hist[:, :], start=True, stop=True)
            pe.matmul(total_ps[:, :], ones[:, :], hist[:, :], start=True, stop=True).then_inc(smaller_made, 1)

        @block.gpsimd
        def _(pool):
            def gather(n, h, k):
                pool_wait(pool, staged, made(n))
                for c in range(FSTEP):
                    pool.indirect_dma_start(out=rows[:, h, c, :], out_offset=None, in_=a["dst_tiles"][:, :], in_offset=bass.IndirectOffsetOnAxis(ap=stage[:, h, c:c + 1], axis=0)).then_inc(rows_in[h], 16)

            skewed(pool, FB // FSTEP, gather, lambda n, h, k: None)

        @block.vector
        def _(v):
            steps = 0

            def after(ins):
                nonlocal steps
                ins.then_inc(dve, 1)
                steps += 1
                v.wait_ge(dve, steps)

            v.memset(zero[:, :], 0.0).then_inc(zero_made, 1)
            after(v.memset(ones[:, :], 1.0))
            v.wait_ge(consts_in, 16 * 9)
            after(v.tensor_scalar(low[:, :], first[:, :], P - 1, None, ALU.bitwise_and))
            after(v.tensor_scalar(high[:, :], first[:, :], 7, None, ALU.logical_shift_right))
            after(v.tensor_copy(lowf[:, :], low[:, :]))
            after(v.tensor_copy(highf[:, :], high[:, :]))
            for c in range(CHUNKS):
                v.tensor_scalar(low_hot[:, c, :], place_row[:, :], lowf[:, c:c + 1], None, ALU.is_equal)
                hot = v.tensor_scalar(high_hot[:, c, :], place_row[:, 0:FB], highf[:, c:c + 1], None, ALU.is_equal)
            hot.then_inc(hot_made, 1)
            v.wait_ge(hist_made, 1)
            v.tensor_copy(hist[:, :], hist_ps[:, :]).then_inc(hist_copied, 1)
            v.wait_ge(smaller_made, 1)
            after(v.tensor_tensor_scan(smaller[:, :], ones[:, 0:FB], total_ps[:, :], 0.0, ALU.mult, ALU.add))
            after(v.tensor_tensor(smaller[:, :], smaller[:, :], total_ps[:, :], ALU.subtract))
            after(v.tensor_tensor(before[:, :], smaller[:, :], within_ps[:, :], ALU.add))
            after(v.tensor_scalar(tile_of[:, :], before[:, :], -1.0, 0.0, ALU.add, ALU.max))
            after(v.tensor_copy(tile_ix[:, :], tile_of[:, :]))
            for h in range(2):
                v.tensor_copy(stage[:, h, :], tile_ix[:, h * FSTEP:(h + 1) * FSTEP]).then_inc(staged, 1)
            v.wait_ge(edges_in, 16 * 4)
            after(v.tensor_tensor(same[:, :], cur[:, :], prev[:, :], ALU.is_equal))
            v.tensor_scalar(far[:, :], same[:, :], -1.0, FAR, ALU.add, ALU.mult).then_inc(rows_ready, 1)
            after(v.tensor_scalar(starts[:, :], same[:, :], -1.0, 1.0, ALU.mult, ALU.add))
            after(v.tensor_tensor(starts[:, :], starts[:, :], place[:, :], ALU.mult))
            v.tensor_tensor_scan(seed[:, :], inside[:, :], starts[:, :], 0.0, ALU.mult, ALU.max).then_inc(rows_ready, 1)
            v.wait_ge(more_in, 16 * 3)
            after(v.tensor_scalar(digit[:, :], src[:, :], 7, None, ALU.logical_shift_right))
            after(v.tensor_copy(digits[:, 0, :], digit[:, :]))
            after(v.tensor_scalar(digit[:, :], src[:, :], P - 1, None, ALU.bitwise_and))
            v.tensor_copy(digits[:, 1, :], digit[:, :]).then_inc(rows_ready, 1)
            v.scalar_tensor_tensor(keep.rel_ix[:, :], typ[:, :], float(NP), keep.src_ix[:, :], ALU.mult, ALU.add)
            def to_stage(n, h, k):
                if isinstance(n, int) and n < 2:
                    return
                v.wait_ge(rows_in[h], landed_before(k, FSTEP))
                v.tensor_copy(stage[:, h, :], tile_ix[:, bass.ds(n * FSTEP, FSTEP)]).then_inc(staged, 1)

            def count(n, h, k):
                v.wait_ge(rows_in[h], landed(k, FSTEP))
                for c in range(FSTEP):
                    counted_one = v.tensor_scalar(junk2[:, :], rows[:, h, c, :], nid[:, bass.ds(n * FSTEP + c, 1)], 0.0, ALU.is_lt, ALU.add, accum_out=within[:, bass.ds(n * FSTEP + c, 1)])
                    counted_one.then_inc(within_made, 1)
                    v.wait_ge(within_made, FSTEP * n + c + 1)

            skewed(v, FB // FSTEP, to_stage, count)
            v.scalar_tensor_tensor(rs[:, :], tile_of[:, :], float(P), within[:, :], ALU.mult, ALU.add).then_inc(counted, 1)
            v.wait_ge(rs_in, 16)
            v.wait_ge(counted, 1)
            after(v.tensor_tensor(keep.has[:, :], rs_next[:, :], rs[:, 0:NB], ALU.is_gt))
            after(v.tensor_scalar(edge[:, :], rs_next[:, :], -1.0, 0.0, ALU.add, ALU.max))
            edge_row(v, after, keep.last_ix[:, :].bitcast(I32), edge[:, :], part[:, :], part2[:, :])
            after(v.tensor_copy(edge[:, :], rs[:, 0:NB]))
            edge_row(v, after, part[:, :], edge[:, :], part[:, :], part2[:, :])
            after(v.tensor_copy(rs_next[:, :], part[:, :]))
            after(v.tensor_tensor(rs_next[:, :], rs_next[:, :], spare[:, :], ALU.subtract))
            after(v.tensor_tensor(rs_next[:, :], rs_next[:, :], keep.has[:, :], ALU.mult))
            after(v.tensor_tensor(keep.seed_ix[:, :], rs_next[:, :], spare[:, :], ALU.add))


def seed_tiles(nc, t, keep, phase):
    with ExitStack() as ctx:
        m = Memory(nc, ctx, phase)
        rows = m.sb("rows", [GROUPS, TILES, D])
        gathered, stored = m.sem("gathered"), m.sem("stored")
        block = ctx.enter_context(nc.Block())
        firsts = t["seeds"][0:EP, :].rearrange("(g p t) f -> g p t f", p=P, t=TILES)[:, 0, :, :]

        @block.gpsimd
        def _(pool):
            for c in range(TILES):
                pool.indirect_dma_start(out=rows[:, c, :], out_offset=None, in_=t["nodes"][:, :], in_offset=bass.IndirectOffsetOnAxis(ap=keep.first_ix[:, c:c + 1], axis=0)).then_inc(gathered, 16)

        @block.sync
        def _(sp):
            sp.wait_ge(gathered, 16 * TILES)
            sp.dma_start(firsts, rows[:, :, :]).then_inc(stored, 16)
            sp.wait_ge(stored, 16)


def node_phase(nc, a, t, keep, layer, out):
    ins = [["x"], ["x", "acc0", "acc1", "acc2", "acc3"], ["own", "upd"], ["own"], ["own"]][layer]
    cat = [D, 4 * D, 4 * D, 5 * D, 0][layer]
    own = [None, 2 * D, 3 * D, 4 * D, None][layer]
    seeded = [0, D, 2 * D, None, None][layer]
    outs = [[("nodes", 0, D)],
            [("a1", 0, D), ("nodes", D, D), ("own", 2 * D, D), ("upd", 3 * D, D)],
            [("kv", 0, 2 * D), ("nodes", 2 * D, D), ("own", 3 * D, D)],
            [("rel0", 0, D), ("rel1", D, D), ("rel2", 2 * D, D), ("rel3", 3 * D, D), ("own", 4 * D, D)],
            []][layer]
    got = [0, 0, D, TW, D][layer]
    norm = layer > 0
    if layer in (2, 3, 4):
        ins = [f"own{layer - 1}" if x == "own" else x for x in ins]
    outs = [(f"own{layer}" if x == "own" else x, c, w) for x, c, w in outs]
    with ExitStack() as ctx:
        m = Memory(nc, ctx, f"node{layer}")
        xin = [m.sb(f"in_{x}", [P, 2, STEP, D]) for x in ins]
        xh = m.sb("xh", [P, 2, STEP, D])
        last_ix, seed_ix = m.sb("last_ix", [P, 2, STEP], U32), m.sb("seed_ix", [P, 2, STEP], U32)
        if got:
            res = m.sb("res", [P, 2, STEP, got])
            resT = m.sb("resT", [P, STEP * P])
        if norm:
            stats, mv = m.sb("stats", [P, STEP, 6]), m.sb("mv", [P, STEP, 2])
            dev, inv, shift = m.sb("dev", [P, STEP]), m.sb("inv", [P, STEP]), m.sb("shift", [P, STEP])
        if layer == 2:
            wupd = m.sb("wupd", [P, D])
            upd_ps = [m.ps(f"upd{i}", [P, 1024]) for i in range(2)]
        if layer == 0:
            zero, zero_made, zeroed = m.sb("zero", [P, STEP * D]), m.sem("zero_made"), m.sem("zeroed")
        if layer == 3:
            den = m.sb("den", [P, STEP, HEADS])
        if cat:
            w, bias = m.sb("w", [P, cat]), m.sb("bias", [P, cat])
            xT = m.sb("xT", [P, 2, STEP * P])
            res_out = m.sb("out", [P, 2, STEP, cat])
            turns = 3 if layer < 2 else 1
            mm_ps = [m.ps(f"mm{i}", [P, 1024 if cat > 512 else 512]) for i in range(2 * turns)]

            def slot_of(h, b):
                return mm_ps[(h * STEP + b) % 2] if turns == 1 else mm_ps[turns * h + b % turns]

            def last_use(n, b):
                if turns == 1:
                    return STEP * n + b - 1
                return STEP * n + b - turns + 1 if b >= turns else STEP * (n - 1)
        tr_ps = m.ps("tr", [P, 1024])
        shift_made = m.sem("shift_made")
        weights_in, own_added = m.sem("weights_in"), m.sem("own_added")
        in_landed = [m.sem("in_landed0"), m.sem("in_landed1")]
        res_landed = [m.sem("res_landed0"), m.sem("res_landed1")]
        out_landed = [m.sem("out_landed0"), m.sem("out_landed1")]
        seeds_landed = [m.sem("seeds_landed0"), m.sem("seeds_landed1")]
        last_ix_made, seed_ix_made = m.sem("last_ix_made"), m.sem("seed_ix_made")
        xh_made, tr_made, xT_made = (m.sem(x) for x in ("xh_made", "tr_made", "xT_made"))
        mm_made, mm_used, dev_made, mv_made, dve = (m.sem(x) for x in ("mm_made", "mm_used", "dev_made", "mv_made", "dve"))
        pre_made, preT_made, upd_made, res_masked = (m.sem(x) for x in ("pre_made", "preT_made", "upd_made", "res_masked"))
        block = ctx.enter_context(nc.Block())
        n_out = len(outs) if outs else 1
        n_weights = (2 if cat else 0) + (layer == 2)

        @block.sync
        def _(sp):
            if cat:
                sp.dma_start(w[:, :], a[f"w{layer}"]).then_inc(weights_in, 16)
                sp.dma_start(bias[:, :], a[f"b{layer}"].rearrange("(o c) -> o c", o=1).broadcast_to([P, cat])).then_inc(weights_in, 16)
            if layer == 2:
                sp.dma_start(wupd[:, :], a["w_upd"]).then_inc(weights_in, 16)

            def load(n, h, k):
                if any_yet(free(n)):
                    sp.wait_ge(xh_made, free(n))
                for x, to in zip(ins, xin):
                    sp.dma_start(to[:, h, :, :], by_step(t[x], n)).then_inc(in_landed[h], 16)

            def store(n, h, k):
                if cat:
                    sp.wait_ge(mm_used, STEP * (n + 1))
                    for x, c, wd in outs:
                        sp.dma_start(by_step(t[x], n), res_out[:, h, :, c:c + wd]).then_inc(out_landed[h], 16)
                else:
                    sp.wait_ge(xh_made, made(n))
                    sp.dma_start(by_step(out, n), xh[:, h, :, :]).then_inc(out_landed[h], 16)

            stepped(sp, [(load, 3), (store, 0)])
            for h in range(2):
                sp.wait_ge(out_landed[h], landed(STEPS // 2 - 1, n_out))

        @block.gpsimd
        def _(pool):
            table = {2: "sum1", 3: "sum2", 4: "max3"}.get(layer)

            def gather(n, h, k):
                pool_wait(pool, last_ix_made, made(n))
                if any_yet(free(n)):
                    pool_wait(pool, pre_made if layer == 2 else xh_made, free(n))
                for b in range(STEP):
                    pool.indirect_dma_start(out=res[:, h, b, :], out_offset=None, in_=t[table][:, :], in_offset=bass.IndirectOffsetOnAxis(ap=last_ix[:, h, b:b + 1], axis=0)).then_inc(res_landed[h], 16)

            def scatter(n, h, k):
                pool_wait(pool, seed_ix_made, made(n))
                pool_wait(pool, mm_used, STEP * (n + 1))
                for b in range(STEP):
                    pool.indirect_dma_start(out=t["seeds"][:, :], out_offset=bass.IndirectOffsetOnAxis(ap=seed_ix[:, h, b:b + 1], axis=0), in_=res_out[:, h, b, seeded:seeded + D], in_offset=None).then_inc(seeds_landed[h], 16)

            if got or seeded is not None:
                stepped(pool, ([(gather, 3)] if got else []) + ([(scatter, 0)] if seeded is not None else []))
            if seeded is not None:
                for h in range(2):
                    pool_wait(pool, seeds_landed[h], landed(STEPS // 2 - 1, STEP))

        @block.tensor
        def _(pe):
            if n_weights:
                pe.wait_ge(weights_in, 16 * n_weights)
            if own is not None:
                pe.wait_ge(own_added, 1)

            def update(n, h, k):
                pe.wait_ge(res_masked, made(n))
                if any_yet(free(n)):
                    pe.wait_ge(xT_made, free(n))
                for b in range(STEP):
                    mm = pe.transpose(tr_ps[:, b * P:(b + 1) * P], res[:, h, b, :], keep.ident[:, :])
                mm.then_inc(pre_made, 1)
                pe.wait_ge(preT_made, made(n))
                if any_yet(free(n)):
                    pe.wait_ge(xh_made, free(n))
                for b in range(STEP):
                    mm = pe.matmul(upd_ps[h][:, b * P:(b + 1) * P], resT[:, b * P:(b + 1) * P], wupd[:, :], start=True, stop=True)
                mm.then_inc(upd_made, 1)

            def turn(n, h, k):
                pe.wait_ge(xh_made, made(n))
                if any_yet(made(n - 1)):
                    pe.wait_ge(xT_made, made(n - 1))
                for b in range(STEP):
                    mm = pe.transpose(tr_ps[:, b * P:(b + 1) * P], xh[:, h, b, :], keep.ident[:, :])
                mm.then_inc(tr_made, 1)

            def multiply(n, h, k):
                pe.wait_ge(xT_made, made(n))
                for b in range(STEP):
                    if any_yet(last_use(n, b)):
                        pe.wait_ge(mm_used, last_use(n, b))
                    slot = slot_of(h, b)
                    rows = xT[:, h, b * P:(b + 1) * P]
                    for c in range(0, cat, 512):
                        mm = pe.matmul(slot[:, c:min(cat, c + 512)], rows, w[:, c:min(cat, c + 512)], start=True, stop=True)
                    mm.then_inc(mm_made, 1)

            if cat:
                stepped(pe, [(multiply, 0)] + ([(update, 2)] if layer == 2 else []) + [(turn, 1)])

        @block.scalar
        def _(act):

            def last_indices(n, h, k):
                if any_yet(landed_before(k, STEP)):
                    act.wait_ge(res_landed[h], landed_before(k, STEP))
                act.copy(last_ix[:, h, :], keep.last_ix[:, bass.ds(n * STEP, STEP)]).then_inc(last_ix_made, 1)

            def seed_indices(n, h, k):
                if any_yet(landed_before(k, STEP)):
                    act.wait_ge(seeds_landed[h], landed_before(k, STEP))
                act.copy(seed_ix[:, h, :], keep.seed_ix[:, bass.ds(n * STEP, STEP)]).then_inc(seed_ix_made, 1)

            def copy_sums(n, h, k):
                act.wait_ge(pre_made, made(n))
                if any_yet(made(n - 1)):
                    act.wait_ge(upd_made, made(n - 1))
                act.copy(resT[:, :], tr_ps[:, 0:STEP * P]).then_inc(preT_made, 1)

            def root_and_copy(n, h, k):
                if norm:
                    act.wait_ge(mv_made, made(n))
                    act.activation(dev[:, :], mv[:, :, 1], ACT.Sqrt, bias=keep.eps[:, :]).then_inc(dev_made, 1)
                    act.wait_ge(shift_made, made(n))
                    if cat:
                        if any_yet(free(n)):
                            act.wait_ge(tr_made, free(n))
                    else:
                        if any_yet(landed_before(k, n_out)):
                            act.wait_ge(out_landed[h], landed_before(k, n_out))
                    for b in range(STEP):
                        rows = act.activation(xh[:, h, b, :], xin[0][:, h, b, :], ACT.Identity, scale=inv[:, b:b + 1], bias=shift[:, b:b + 1])
                    rows.then_inc(xh_made, 1)
                if cat:
                    act.wait_ge(tr_made, made(n))
                    if any_yet(STEP * free(n)):
                        act.wait_ge(mm_made, STEP * free(n))
                    act.copy(xT[:, h, :], tr_ps[:, 0:STEP * P]).then_inc(xT_made, 1)

            def clear_sums(n, h, k):
                for acc in range(ACCS):
                    act.dma_start(by_step(t[f"acc{acc}"][0:NP, :], n), zero[:, :].rearrange("p (b f) -> p b f", f=D)).then_inc(zeroed, 16)

            if layer == 0:
                act.wait_ge(zero_made, 1)
                for acc in range(ACCS):
                    act.dma_start(t[f"acc{acc}"][NP:NP + P, :], zero[:, 0:D]).then_inc(zeroed, 16)
            stepped(act, ([(last_indices, 3)] if got else []) + ([(copy_sums, 2)] if layer == 2 else []) + [(root_and_copy, 1)]
                    + ([(seed_indices, 0)] if seeded is not None else []) + ([(clear_sums, 0)] if layer == 0 else []))
            if layer == 0:
                act.wait_ge(zeroed, 16 * ACCS * (STEPS + 1))

        @block.vector
        def _(v):
            if layer == 0:
                v.memset(zero[:, :], 0.0).then_inc(zero_made, 1)
            if cat:
                v.wait_ge(weights_in, 16 * n_weights)
            if own is not None:
                v.tensor_tensor(w[:, own:own + D], w[:, own:own + D], keep.ident[:, :], ALU.add).then_inc(own_added, 1)
            chain = {0: 0, 1: 6, 2: 4, 3: 7, 4: 4}[layer]
            done = 0

            def after(ins, n):
                nonlocal done
                ins.then_inc(dve, 1)
                done += 1
                v.wait_ge(dve, chain * n + done)

            def mask(n, h, k):
                v.wait_ge(res_landed[h], landed(k, STEP))
                return v.tensor_tensor(res[:, h, :, :], res[:, h, :, :], has_of(n).broadcast_to([P, STEP, D]), ALU.mult)

            def mask_sums(n, h, k):
                mask(n, h, k).then_inc(res_masked, 1)

            def has_of(n):
                return keep.has[:, bass.ds(n * STEP, STEP)].unsqueeze(2)

            def normalise(n, h, k):
                nonlocal done
                done = 0
                v.wait_ge(in_landed[h], landed(k, len(ins)))
                y = xin[0][:, h, :, :]
                if layer == 0:
                    if any_yet(free(n)):
                        v.wait_ge(tr_made, free(n))
                    v.tensor_copy(xh[:, h, :, :], y).then_inc(xh_made, 1)
                    return
                if layer == 1:
                    for other in xin[1:]:
                        after(v.tensor_tensor(y, y, other[:, h, :, :], ALU.add), n)
                if layer == 2:
                    z = xin[1][:, h, :, :]
                    v.wait_ge(upd_made, made(n))
                    after(v.tensor_tensor(z, z, upd_ps[h][:, 0:STEP * P].rearrange("p (b f) -> p b f", f=D), ALU.add), n)
                    after(v.scalar_tensor_tensor(y, z, 0.0, y, ALU.max, ALU.add), n)
                if layer == 3:
                    v.wait_ge(res_landed[h], landed(k, STEP))
                    after(v.tensor_scalar(den[:, :, :], res[:, h, :, D:TW], 1.0, None, ALU.max), n)
                    after(v.reciprocal(den[:, :, :], den[:, :, :]), n)
                    after(v.tensor_tensor(den[:, :, :], den[:, :, :], has_of(n).broadcast_to([P, STEP, HEADS]), ALU.mult), n)
                    num = res[:, h, :, 0:D].rearrange("p b (a c) -> p b a c", c=HC)
                    after(v.tensor_tensor(num, num, den[:, :, :].unsqueeze(3).broadcast_to([P, STEP, HEADS, HC]), ALU.mult), n)
                    after(v.tensor_tensor(y, y, res[:, h, :, 0:D], ALU.add), n)
                if layer == 4:
                    after(mask(n, h, k), n)
                    after(v.tensor_tensor(y, y, res[:, h, :, :], ALU.add), n)
                for b in range(STEP):
                    st = v.bn_stats(stats[:, b, :], y[:, b, :])
                after(st, n)
                if any_yet(made(n - 1)):
                    v.wait_ge(dev_made, made(n - 1))
                v.nop(nofuse=True)
                for b in range(STEP):
                    ag = v.bn_aggr(mv[:, b, :], stats[:, b, :])
                ag.then_inc(mv_made, 1)
                v.wait_ge(dev_made, made(n))
                if any_yet(made(n - 1)):
                    v.wait_ge(xh_made, made(n - 1))
                after(v.reciprocal(inv[:, :], dev[:, :]), n)
                v.scalar_tensor_tensor(shift[:, :], mv[:, :, 0], -1.0, inv[:, :], ALU.mult, ALU.mult).then_inc(shift_made, 1)
                assert done == chain, (layer, done)

            def add_bias(n, h, k):
                if any_yet(landed_before(k, n_out)):
                    v.wait_ge(out_landed[h], landed_before(k, n_out))
                if seeded is not None:
                    if any_yet(landed_before(k, STEP)):
                        v.wait_ge(seeds_landed[h], landed_before(k, STEP))
                for b in range(STEP):
                    v.wait_ge(mm_made, STEP * n + b + 1)
                    v.tensor_tensor(res_out[:, h, b, :], slot_of(h, b)[:, 0:cat], bias[:, :], ALU.add).then_inc(mm_used, 1)

            if layer == 2:
                stepped(v, [(add_bias, 0), (mask_sums, 2), (normalise, 1)])
            else:
                stepped(v, [(normalise, 1)] + ([(add_bias, 0)] if cat else []))


def edges_sum0(nc, a, t, keep):
    with ExitStack() as ctx:
        m = Memory(nc, ctx, "edge0")
        seeds, seed = m.sb("seeds", [P, 2, TILES, D]), m.sb("seed", [P, 2, GE], BF16)
        spread = m.sb("spread", [P, 2, GE])
        digits, w = m.sb("digits", [2, 2, GE], BF16), m.sb("w", [P, 2, TILES])
        srcf, dup, flag, ix = m.sb("srcf", [P, 2, TILES]), m.sb("dup", [P, 2, TILES]), m.sb("flag", [P, TILES]), m.sb("ix", [P, 2, TILES], U32)
        away = m.sb("away", [P, TILES])
        lower, trash = m.sb("lower", [P, P]), m.sb("trash", [P, 1])
        place_value_in, place_value = m.sb("place_value_in", [2, P]), m.sb("place_value", [2, P], BF16)
        equal, masked = m.sb("equal", [P, 2, QUAD, P]), m.sb("masked", [P, QUAD, P])
        weighted, sums = m.sb("weighted", [P, 2, QUAD, D]), m.sb("sums", [P, 2, TILES, D])
        src_ps, row_ps, sum_ps = ([m.ps(f"{x}{i}", [P, QE]) for i in range(2)] for x in ("src", "row", "sum"))
        consts_in, place_value_made = m.sem("consts_in"), m.sem("place_value_made")
        edges_in = [m.sem(f"edges_in{h}") for h in range(2)]
        spread_made, src_made, equal_made, masked_made, dup_made, row_made, weighted_made, sum_made, sums_made, ix_made, ix_step = (
            m.sem(x) for x in ("spread_made", "src_made", "equal_made", "masked_made", "dup_made", "row_made", "weighted_made", "sum_made",
                               "sums_made", "ix_made", "ix_step"))
        added = [m.sem(f"added{k}") for k in range(ACCS)]
        block = ctx.enter_context(nc.Block())
        PER_ACC = TILES // ACCS
        EDGE_DMAS = 3 + QUADS
        IX_STEPS = 3

        @block.sync
        def _(sp):
            for to, of in ((lower, a["lower"]), (trash, a["trash"]), (place_value_in, a["place_value"])):
                sp.dma_start(to[:, :], of).then_inc(consts_in, 16)

            def load(n, h, k):
                if any_yet(QUADS * free(n)):
                    sp.wait_ge(weighted_made, QUADS * free(n))
                sp.dma_start(seed[:, h, :], row_to_all(t["seed"], n)).then_inc(edges_in[h], 16)
                sp.dma_start(digits[:, h, :], t["digits"][:, bass.ds(n * GE, GE)]).then_inc(edges_in[h], 16)
                sp.dma_start(w[:, h, :], a["w_pt"][:, bass.ds(n * TILES, TILES)]).then_inc(edges_in[h], 16)

            def load_seeds(n, h, k, j):
                if any_yet(QUADS * (n - 2) + j + 1):
                    sp.wait_ge(row_made, QUADS * (n - 2) + j + 1)
                sp.dma_start(seeds[:, h, j * QUAD:(j + 1) * QUAD, :].rearrange("p t f -> p (t f)"), by_group(t["seeds"][0:EP, :], n)[:, j * QUAD * D:(j + 1) * QUAD * D]).then_inc(edges_in[h], 16)

            pipelined(sp, [(load_seeds, 0), (at_group(load), 0)])

        @block.gpsimd
        def _(pool):
            def add(n, h, k, j):
                if j == 0:
                    pool_wait(pool, ix_made, made(n))
                pool_wait(pool, sums_made, QUADS * n + j + 1)
                for c in range(QUAD):
                    e = j * QUAD + c
                    if any_yet(16 * (PER_ACC * n + e // ACCS)):
                        pool_wait(pool, added[e % ACCS], 16 * (PER_ACC * n + e // ACCS))
                    pool.indirect_dma_start(out=t[f"acc{e % ACCS}"][:, :], out_offset=bass.IndirectOffsetOnAxis(ap=ix[:, h, e:e + 1], axis=0), in_=sums[:, h, e, :], in_offset=None, compute_op=ALU.add).then_inc(added[e % ACCS], 16)

            pipelined(pool, [(add, 0)])
            for k in range(ACCS):
                pool_wait(pool, added[k], 16 * PER_ACC * GROUPS)

        @block.tensor
        def _(pe):
            pe.wait_ge(place_value_made, 1)

            def spread_quad(n, h, k, j):
                q = QUADS * n + j
                if j == 0:
                    pe.wait_ge(edges_in[h], landed(k, EDGE_DMAS))
                    pe.wait_ge(spread_made, made(n))
                if any_yet(free(q)):
                    pe.wait_ge(equal_made, free(q))
                pe.matmul(src_ps[j % 2][:, :], place_value[:, :], digits[:, h, j * QE:(j + 1) * QE], start=True, stop=True).then_inc(src_made, 1)
                if any_yet(free(q)):
                    pe.wait_ge(weighted_made, free(q))
                for c in range(QUAD):
                    e = j * QUAD + c
                    mm = pe.matmul(row_ps[j % 2][:, c * D:(c + 1) * D], spread[:, h, e * P:(e + 1) * P], seeds[:, h, e, :], start=True, stop=True)
                mm.then_inc(row_made, 1)

            def sum_quad(n, h, k, j):
                q = QUADS * n + j
                pe.wait_ge(equal_made, made(q))
                pe.wait_ge(weighted_made, made(q))
                if any_yet(free(q)):
                    pe.wait_ge(sums_made, free(q))
                for c in range(QUAD):
                    mm = pe.matmul(sum_ps[j % 2][:, c * D:(c + 1) * D], equal[:, j % 2, c, :], weighted[:, j % 2, c, :], start=True, stop=True)
                mm.then_inc(sum_made, 1)

            pipelined(pe, [(spread_quad, 0), (sum_quad, 1)])

        @block.scalar
        def _(act):
            def weigh(n, h, k, j):
                q = QUADS * n + j
                if j == 0:
                    act.wait_ge(edges_in[h], landed(k, EDGE_DMAS))
                act.wait_ge(row_made, made(q))
                if any_yet(free(q)):
                    act.wait_ge(sum_made, free(q))
                for c in range(QUAD):
                    e = j * QUAD + c
                    ins = act.activation(weighted[:, j % 2, c, :], row_ps[j % 2][:, c * D:(c + 1) * D], ACT.Copy, scale=w[:, h, e:e + 1])
                ins.then_inc(weighted_made, 1)

            def copy_sums(n, h, k, j):
                act.wait_ge(sum_made, made(QUADS * n + j))
                if j == 0 and any_yet(free(n)):
                    for s in added:
                        act.wait_ge(s, 16 * PER_ACC * free(n))
                act.copy(sums[:, h, j * QUAD:(j + 1) * QUAD, :], sum_ps[j % 2][:, :].rearrange("p (c f) -> p c f", f=D)).then_inc(sums_made, 1)

            pipelined(act, [(weigh, 0), (copy_sums, 1)])

        @block.vector
        def _(v):
            v.wait_ge(consts_in, 16 * 3)
            v.tensor_copy(place_value[:, :], place_value_in[:, :]).then_inc(place_value_made, 1)

            def spread_group(n, h, k):
                v.wait_ge(edges_in[h], landed(k, EDGE_DMAS))
                if any_yet(QUADS * free(n)):
                    v.wait_ge(row_made, QUADS * free(n))
                v.tensor_copy(srcf[:, h, :], keep.src_ix[:, bass.ds(n * TILES, TILES)])
                v.tensor_scalar(spread[:, h, :], seed[:, h, :], keep.iota[:, 0:1], None, ALU.is_equal).then_inc(spread_made, 1)

            def compare(n, h, k, j):
                q = QUADS * n + j
                v.wait_ge(spread_made, made(n))
                v.wait_ge(src_made, made(q))
                if any_yet(free(q)):
                    v.wait_ge(sum_made, free(q))
                own = srcf[:, h, j * QUAD:(j + 1) * QUAD].unsqueeze(2).broadcast_to([P, QUAD, P])
                v.tensor_tensor(equal[:, j % 2, :, :], src_ps[j % 2][:, :].rearrange("p (c f) -> p c f", f=P), own, ALU.is_equal).then_inc(equal_made, 1)

            def count(n, h, k, j):
                q = QUADS * n + j
                v.wait_ge(equal_made, made(q))
                if any_yet(q):
                    v.wait_ge(dup_made, q)
                v.tensor_tensor(masked[:, :, :], equal[:, j % 2, :, :], lower[:, :].unsqueeze(1).broadcast_to([P, QUAD, P]), ALU.mult).then_inc(masked_made, 1)
                v.wait_ge(masked_made, made(q))
                v.tensor_reduce(dup[:, h, j * QUAD:(j + 1) * QUAD], masked[:, :, :], AX.X, ALU.add).then_inc(dup_made, 1)

            def indices(n, h, k):
                v.wait_ge(dup_made, QUADS * n + QUADS)
                if any_yet(n):
                    v.wait_ge(ix_made, n)
                v.tensor_scalar(away[:, :], srcf[:, h, :], -1.0, trash[:, 0:1], ALU.mult, ALU.add).then_inc(ix_step, 1)
                v.tensor_scalar(flag[:, :], dup[:, h, :], 0.0, None, ALU.is_gt).then_inc(ix_step, 1)
                v.wait_ge(ix_step, IX_STEPS * n + 2)
                v.tensor_tensor(flag[:, :], flag[:, :], away[:, :], ALU.mult).then_inc(ix_step, 1)
                v.wait_ge(ix_step, IX_STEPS * n + 3)
                for s in added:
                    if any_yet(16 * PER_ACC * free(n)):
                        v.wait_ge(s, 16 * PER_ACC * free(n))
                v.tensor_tensor(ix[:, h, :], flag[:, :], srcf[:, h, :], ALU.add).then_inc(ix_made, 1)

            pipelined(v, [(at_group(spread_group), -2), (compare, 0), (count, 0), (at_group(indices), 3)])


class Gathered:

    def __init__(self, m, width, out_width, edge_dmas):
        self.ix = m.sb("ix", [P, 2, TILES], U32)
        self.rows = m.sb("rows", [P, 2, TILES, width])
        self.out = m.sb("out", [P, 2, TILES, out_width])
        self.ix_made = m.sem("ix_made")
        self.edges_in, self.stored = ([m.sem(f"{x}{h}") for h in range(2)] for x in ("edges_in", "stored"))
        self.rows_in = [[m.sem(f"rows_in{h}_{j}") for j in range(QUADS)] for h in range(2)]
        self.edge_dmas = edge_dmas

    def gather(self, pool, table, rows_read):
        def gather_quad(n, h, k, j):
            if j == 0:
                pool_wait(pool, self.ix_made, made(n))
            if any_yet(QUADS * (n - 2) + j + 1):
                pool_wait(pool, rows_read, QUADS * (n - 2) + j + 1)
            for e in range(j * QUAD, (j + 1) * QUAD):
                pool.indirect_dma_start(out=self.rows[:, h, e, :], out_offset=None, in_=table[:, :], in_offset=bass.IndirectOffsetOnAxis(ap=self.ix[:, h, e:e + 1], axis=0)).then_inc(self.rows_in[h][j], 16)

        pipelined(pool, [(gather_quad, 0)])

    def first_indices(self, act, all_ix):
        for n in range(2):
            act.copy(self.ix[:, n, :], all_ix[:, n * TILES:(n + 1) * TILES]).then_inc(self.ix_made, 1)

    def next_indices(self, act, all_ix, n, h, k, j):
        if j == QUADS - 1 and (not isinstance(n, int) or n + 2 < GROUPS):
            for s in self.rows_in[h]:
                act.wait_ge(s, landed(k, QUAD))
            act.copy(self.ix[:, h, :], all_ix[:, bass.ds(n * TILES + 2 * TILES, TILES)]).then_inc(self.ix_made, 1)


def edges_sum1(nc, a, t, keep):
    with ExitStack() as ctx:
        m = Memory(nc, ctx, "edge1")
        g = Gathered(m, D, D, 4)
        seeds, seed, same = m.sb("seeds", [P, 2, TILES, D]), m.sb("seed", [P, 2, GE], BF16), m.sb("same", [P, 2, GE], BF16)
        dist, w_dist = m.sb("dist", [1, 2, GE]), m.sb("w_dist", [1, D])
        spread = m.sb("spread", [P, 2, GE])
        msg, run = m.sb("msg", [P, 2, QE]), m.sb("run", [P, 2, QE])
        msg_ps, turn_ps = ([m.ps(f"{x}{i}", [P, QE]) for i in range(2)] for x in ("msg", "turn"))
        consts_in = m.sem("consts_in")
        spread_made, pre_made, msg_made, run_made, turned, out_made, zeroed = (m.sem(x) for x in ("spread_made", "pre_made", "msg_made", "run_made", "turned", "out_made", "zeroed"))
        block = ctx.enter_context(nc.Block())

        @block.sync
        def _(sp):
            sp.dma_start(w_dist[:, :], a["w_dist"]).then_inc(consts_in, 16)

            def load(n, h, k):
                if any_yet(QUADS * free(n)):
                    sp.wait_ge(run_made, QUADS * free(n))
                sp.dma_start(seed[:, h, :], row_to_all(t["seed"], n)).then_inc(g.edges_in[h], 16)
                sp.dma_start(seeds[:, h, :, :].rearrange("p t f -> p (t f)"), by_group(t["seeds"][0:EP, :], n)).then_inc(g.edges_in[h], 16)
                sp.dma_start(same[:, h, :], row_to_all(t["same"], n)).then_inc(g.edges_in[h], 16)
                sp.dma_start(dist[:, h, :], a["ed_row"][:, bass.ds(n * GE, GE)]).then_inc(g.edges_in[h], 16)

            def store(n, h, k):
                sp.wait_ge(out_made, QUADS * made(n))
                sp.dma_start(by_group(t["sum1"], n), g.out[:, h, :, :].rearrange("p t f -> p (t f)")).then_inc(g.stored[h], 16)

            two_ahead(sp, GROUPS, load, store)
            for h in range(2):
                sp.wait_ge(g.stored[h], landed(GROUPS // 2 - 1, 1))

        @block.gpsimd
        def _(pool):
            g.gather(pool, t["a1"], pre_made)

        @block.tensor
        def _(pe):
            pe.wait_ge(consts_in, 16)

            def sum_quad(n, h, k, j):
                q = QUADS * n + j
                if j == 0:
                    pe.wait_ge(g.edges_in[h], landed(k, g.edge_dmas))
                    pe.wait_ge(spread_made, made(n))
                ps = msg_ps[j % 2]
                if any_yet(free(q)):
                    pe.wait_ge(msg_made, free(q))
                pe.matmul(ps[:, :], w_dist[:, :], dist[:, h, j * QE:(j + 1) * QE], start=True, stop=False)
                for c in range(QUAD):
                    e = j * QUAD + c
                    pe.matmul(ps[:, c * P:(c + 1) * P], seeds[:, h, e, :], spread[:, h, e * P:(e + 1) * P], start=False, stop=False)
                pe.wait_ge(g.rows_in[h][j], landed(k, QUAD))
                for c in range(QUAD):
                    mm = pe.matmul(ps[:, c * P:(c + 1) * P], g.rows[:, h, j * QUAD + c, :], keep.ident[:, :], start=False, stop=c == QUAD - 1)
                mm.then_inc(pre_made, 1)

            def turn_quad(n, h, k, j):
                q = QUADS * n + j
                pe.wait_ge(run_made, made(q))
                if any_yet(free(q)):
                    pe.wait_ge(out_made, free(q))
                for c in range(QUAD):
                    mm = pe.transpose(turn_ps[j % 2][:, c * P:(c + 1) * P], run[:, j % 2, c * P:(c + 1) * P], keep.ident[:, :])
                mm.then_inc(turned, 1)

            pipelined(pe, [(sum_quad, 0), (turn_quad, 1)])

        @block.scalar
        def _(act):
            def relu(n, h, k, j):
                q = QUADS * n + j
                act.wait_ge(pre_made, made(q))
                if any_yet(free(q)):
                    act.wait_ge(run_made, free(q))
                act.activation(msg[:, j % 2, :], msg_ps[j % 2][:, :], ACT.Relu).then_inc(msg_made, 1)
                g.next_indices(act, keep.src_ix, n, h, k, j)

            def copy_out(n, h, k, j):
                if j == 0 and any_yet(landed_before(k, 1)):
                    act.wait_ge(g.stored[h], landed_before(k, 1))
                act.wait_ge(turned, made(QUADS * n + j))
                act.copy(g.out[:, h, j * QUAD:(j + 1) * QUAD, :], turn_ps[j % 2][:, :].rearrange("p (c f) -> p c f", f=D)).then_inc(out_made, 1)

            g.first_indices(act, keep.src_ix)
            pipelined(act, [(relu, 0), (copy_out, 1)])

        @block.vector
        def _(v):
            v.memset(run[:, 1, QE - 1:QE], 0.0).then_inc(zeroed, 1)
            v.wait_ge(zeroed, 1)

            def spread_group(n, h, k):
                v.wait_ge(g.edges_in[h], landed(k, g.edge_dmas))
                if any_yet(QUADS * free(n)):
                    v.wait_ge(pre_made, QUADS * free(n))
                v.tensor_scalar(spread[:, h, :], seed[:, h, :], keep.iota[:, 0:1], None, ALU.is_equal).then_inc(spread_made, 1)

            def scan(n, h, k, j):
                q = QUADS * n + j
                v.wait_ge(msg_made, made(q))
                if any_yet(free(q)):
                    v.wait_ge(turned, free(q))
                if any_yet(q):
                    v.wait_ge(run_made, q)
                v.tensor_tensor_scan(run[:, j % 2, :], same[:, h, j * QE:(j + 1) * QE], msg[:, j % 2, :], run[:, (j - 1) % 2, QE - 1:QE], ALU.mult, ALU.add).then_inc(run_made, 1)

            pipelined(v, [(at_group(spread_group), -1), (scan, 0)])


def edges_max3(nc, a, t, keep):
    with ExitStack() as ctx:
        m = Memory(nc, ctx, "edge3")
        g = Gathered(m, D, D, 1)
        far, run = m.sb("far", [P, 2, GE], BF16), m.sb("run", [P, 2, QE])
        in_ps, turn_ps = ([m.ps(f"{x}{i}", [P, QE]) for i in range(2)] for x in ("in", "turn"))
        turned_in, run_made, turned, out_made, zeroed = (m.sem(x) for x in ("turned_in", "run_made", "turned", "out_made", "zeroed"))
        block = ctx.enter_context(nc.Block())

        @block.sync
        def _(sp):
            def load(n, h, k):
                if any_yet(QUADS * free(n)):
                    sp.wait_ge(run_made, QUADS * free(n))
                sp.nop(nofuse=True)
                sp.dma_start(far[:, h, :], row_to_all(t["far"], n)).then_inc(g.edges_in[h], 16)

            def store(n, h, k):
                sp.wait_ge(out_made, QUADS * made(n))
                sp.dma_start(by_group(t["max3"], n), g.out[:, h, :, :].rearrange("p t f -> p (t f)")).then_inc(g.stored[h], 16)

            two_ahead(sp, GROUPS, load, store)
            for h in range(2):
                sp.wait_ge(g.stored[h], landed(GROUPS // 2 - 1, 1))

        @block.gpsimd
        def _(pool):
            g.gather(pool, t["rel"], turned_in)

        @block.tensor
        def _(pe):
            def turn_in(n, h, k, j):
                q = QUADS * n + j
                pe.wait_ge(g.rows_in[h][j], landed(k, QUAD))
                if any_yet(free(q)):
                    pe.wait_ge(run_made, free(q))
                for c in range(QUAD):
                    mm = pe.transpose(in_ps[j % 2][:, c * P:(c + 1) * P], g.rows[:, h, j * QUAD + c, :], keep.ident[:, :])
                mm.then_inc(turned_in, 1)

            def turn_out(n, h, k, j):
                q = QUADS * n + j
                pe.wait_ge(run_made, made(q))
                if any_yet(free(q)):
                    pe.wait_ge(out_made, free(q))
                for c in range(QUAD):
                    mm = pe.transpose(turn_ps[j % 2][:, c * P:(c + 1) * P], run[:, j % 2, c * P:(c + 1) * P], keep.ident[:, :])
                mm.then_inc(turned, 1)

            pipelined(pe, [(turn_in, 0), (turn_out, 1)])

        @block.scalar
        def _(act):
            def copy_out(n, h, k, j):
                if j == 0 and any_yet(landed_before(k, 1)):
                    act.wait_ge(g.stored[h], landed_before(k, 1))
                act.wait_ge(turned, made(QUADS * n + j))
                act.copy(g.out[:, h, j * QUAD:(j + 1) * QUAD, :], turn_ps[j % 2][:, :].rearrange("p (c f) -> p c f", f=D)).then_inc(out_made, 1)
                g.next_indices(act, keep.rel_ix, n, h, k, j)

            g.first_indices(act, keep.rel_ix)
            pipelined(act, [(copy_out, 0)])

        @block.vector
        def _(v):
            v.memset(run[:, 1, QE - 1:QE], 0.0).then_inc(zeroed, 1)
            v.wait_ge(zeroed, 1)

            def scan(n, h, k, j):
                q = QUADS * n + j
                if j == 0:
                    v.wait_ge(g.edges_in[h], landed(k, 1))
                v.wait_ge(turned_in, made(q))
                if any_yet(free(q)):
                    v.wait_ge(turned, free(q))
                if any_yet(q):
                    v.wait_ge(run_made, q)
                v.tensor_tensor_scan(run[:, j % 2, :], far[:, h, j * QE:(j + 1) * QE], in_ps[j % 2][:, :], run[:, (j - 1) % 2, QE - 1:QE], ALU.add, ALU.max).then_inc(run_made, 1)

            pipelined(v, [(scan, 0)])


def edges_attend2(nc, a, t, keep):
    with ExitStack() as ctx:
        m = Memory(nc, ctx, "edge2")
        g = Gathered(m, 2 * D, TW, 3)
        seeds, seed, far = m.sb("seeds", [P, 2, TILES, D]), m.sb("seed", [P, 2, GE], BF16), m.sb("far", [P, 2, GE], BF16)
        heads, negident = m.sb("heads", [P, P]), m.sb("negident", [P, P])
        spread, away, one = m.sb("spread", [P, 2, GE]), m.sb("away", [P, QE]), m.sb("one", [P, 1])
        q_sb, prod, top = m.sb("q", [P, 2, QE]), m.sb("prod", [P, 2, QE]), m.sb("top", [P, 2, QE + 1])
        fall, fade, ex, val = m.sb("fall", [P, 2, QE]), m.sb("fade", [P, 2, QE]), m.sb("ex", [P, 2, QE]), m.sb("val", [P, 2, QE])
        num, den = m.sb("num", [P, 2, QE]), m.sb("den", [P, 2, QE])
        q_ps, k_ps, v_ps, num_ps, den_ps = (m.ps(x, [P, QE]) for x in ("q", "k", "v", "num", "den"))
        s_ps = [m.ps(f"s{i}", [P, QE]) for i in range(2)]
        consts_in, zeroed = m.sem("consts_in"), m.sem("zeroed")
        (spread_made, q_spread, q_made, k_turned, prod_made, s_made, top_made, fall_made, s_less, fade_made, ex_made, v_turned, val_made,
         num_made, den_made, num_turned, den_turned, num_out, den_out) = (m.sem(x) for x in (
             "spread_made", "q_spread", "q_made", "k_turned", "prod_made", "s_made", "top_made", "fall_made", "s_less", "fade_made",
             "ex_made", "v_turned", "val_made", "num_made", "den_made", "num_turned", "den_turned", "num_out", "den_out"))
        diff_made, carried, away_made, one_made = (m.sem(x) for x in ("diff_made", "carried", "away_made", "one_made"))
        block = ctx.enter_context(nc.Block())

        @block.sync
        def _(sp):
            sp.dma_start(heads[:, :], a["heads"]).then_inc(consts_in, 16)
            sp.dma_start(negident[:, :], a["negident"]).then_inc(consts_in, 16)

            def load(n, h, k):
                if any_yet(QUADS * free(n)):
                    sp.wait_ge(fall_made, QUADS * free(n))
                sp.dma_start(seed[:, h, :], row_to_all(t["seed"], n)).then_inc(g.edges_in[h], 16)
                sp.dma_start(seeds[:, h, :, :].rearrange("p t f -> p (t f)"), by_group(t["seeds"][0:EP, :], n)).then_inc(g.edges_in[h], 16)
                sp.dma_start(far[:, h, :], row_to_all(t["far"], n)).then_inc(g.edges_in[h], 16)

            def store(n, h, k):
                sp.wait_ge(num_out, QUADS * made(n))
                sp.wait_ge(den_out, QUADS * made(n))
                sp.dma_start(by_group(t["sum2"], n), g.out[:, h, :, :].rearrange("p t f -> p (t f)")).then_inc(g.stored[h], 16)

            two_ahead(sp, GROUPS, load, store)
            for h in range(2):
                sp.wait_ge(g.stored[h], landed(GROUPS // 2 - 1, 1))

        @block.gpsimd
        def _(pool):
            g.gather(pool, t["kv"], v_turned)

        @block.tensor
        def _(pe):
            pe.wait_ge(consts_in, 16 * 2)

            def queries_keys(n, h, k, j):
                q = QUADS * n + j
                if j == 0:
                    pe.wait_ge(g.edges_in[h], landed(k, g.edge_dmas))
                pe.wait_ge(spread_made, made(q))
                if any_yet(q):
                    pe.wait_ge(q_made, q)
                for c in range(QUAD):
                    e = j * QUAD + c
                    mm = pe.matmul(q_ps[:, c * P:(c + 1) * P], seeds[:, h, e, :], spread[:, h, e * P:(e + 1) * P], start=True, stop=True)
                mm.then_inc(q_spread, 1)
                pe.wait_ge(g.rows_in[h][j], landed(k, QUAD))
                if any_yet(q):
                    pe.wait_ge(prod_made, q)
                for c in range(QUAD):
                    mm = pe.transpose(k_ps[:, c * P:(c + 1) * P], g.rows[:, h, j * QUAD + c, 0:D], keep.ident[:, :])
                mm.then_inc(k_turned, 1)

            def scores(n, h, k, j):
                q = QUADS * n + j
                pe.wait_ge(prod_made, made(q))
                if any_yet(free(q)):
                    pe.wait_ge(ex_made, free(q))
                pe.matmul(s_ps[j % 2][:, :], heads[:, :], prod[:, j % 2, :], start=True, stop=False, skip_group_check=True).then_inc(s_made, 1)

            def values(n, h, k, j):
                q = QUADS * n + j
                if any_yet(q):
                    pe.wait_ge(val_made, q)
                for c in range(QUAD):
                    mm = pe.transpose(v_ps[:, c * P:(c + 1) * P], g.rows[:, h, j * QUAD + c, D:2 * D], keep.ident[:, :])
                mm.then_inc(v_turned, 1)

            def less_top(n, h, k, j):
                q = QUADS * n + j
                pe.wait_ge(top_made, made(q))
                pe.matmul(s_ps[j % 2][:, :], negident[:, :], top[:, j % 2, 1:QE + 1], start=False, stop=True, skip_group_check=True).then_inc(s_less, 1)

            def turn_out(n, h, k, j):
                q = QUADS * n + j
                pe.wait_ge(num_made, made(q))
                if any_yet(q):
                    pe.wait_ge(num_out, q)
                for c in range(QUAD):
                    mm = pe.transpose(num_ps[:, c * P:(c + 1) * P], num[:, j % 2, c * P:(c + 1) * P], keep.ident[:, :])
                mm.then_inc(num_turned, 1)
                pe.wait_ge(den_made, made(q))
                if any_yet(q):
                    pe.wait_ge(den_out, q)
                for c in range(QUAD):
                    mm = pe.transpose(den_ps[:, c * P:(c + 1) * P], den[:, j % 2, c * P:(c + 1) * P], keep.ident[:, :])
                mm.then_inc(den_turned, 1)

            pipelined(pe, [(less_top, 2), (queries_keys, 0), (scores, 1), (values, 2), (turn_out, 3)])

        @block.scalar
        def _(act):
            def copy_q(n, h, k, j):
                q = QUADS * n + j
                act.wait_ge(q_spread, made(q))
                if any_yet(free(q)):
                    act.wait_ge(prod_made, free(q))
                act.copy(q_sb[:, j % 2, :], q_ps[:, :]).then_inc(q_made, 1)

            def aways(n, h, k, j):
                q = QUADS * n + j
                if j == 0:
                    act.wait_ge(g.edges_in[h], landed(k, g.edge_dmas))
                if any_yet(q):
                    act.wait_ge(spread_made, q)
                act.activation(away[:, :], seed[:, h, j * QE:(j + 1) * QE], ACT.Abs, bias=keep.iota[:, :], scale=-1.0).then_inc(away_made, 1)

            def spreads(n, h, k, j):
                q = QUADS * n + j
                act.wait_ge(away_made, made(q))
                if any_yet(QUADS * (n - 2) + j + 1):
                    act.wait_ge(q_spread, QUADS * (n - 2) + j + 1)
                act.activation(spread[:, h, j * QE:(j + 1) * QE], away[:, :], ACT.Relu, bias=one[:, :], scale=-1.0).then_inc(spread_made, 1)

            def exps(n, h, k, j):
                q = QUADS * n + j
                act.wait_ge(s_less, made(q))
                if any_yet(free(q)):
                    act.wait_ge(den_made, free(q))
                act.activation(ex[:, j % 2, :], s_ps[j % 2][:, :], ACT.Exp).then_inc(ex_made, 1)
                act.wait_ge(fall_made, made(q))
                act.activation(fade[:, j % 2, :], fall[:, j % 2, :], ACT.Exp).then_inc(fade_made, 1)

            def copy_out(n, h, k, j):
                q = QUADS * n + j
                if j == 0 and any_yet(landed_before(k, 1)):
                    act.wait_ge(g.stored[h], landed_before(k, 1))
                act.wait_ge(num_turned, made(q))
                act.copy(g.out[:, h, j * QUAD:(j + 1) * QUAD, 0:D], num_ps[:, :].rearrange("p (c f) -> p c f", f=D)).then_inc(num_out, 1)
                act.wait_ge(den_turned, made(q))
                act.copy(g.out[:, h, j * QUAD:(j + 1) * QUAD, D:TW], den_ps[:, :].rearrange("p (c a f) -> p c a f", c=QUAD, f=HC)[:, :, :, 0]).then_inc(den_out, 1)

            def indices(n, h, k, j):
                g.next_indices(act, keep.src_ix, n, h, k, j)

            g.first_indices(act, keep.src_ix)
            act.wait_ge(one_made, 1)
            pipelined(act, [(aways, -1), (exps, 2), (copy_q, 0), (spreads, -1), (copy_out, 3), (indices, 1)])

        @block.vector
        def _(v):
            v.memset(top[:, 1, QE:QE + 1], 0.0).then_inc(zeroed, 1)
            v.memset(num[:, 1, QE - 1:QE], 0.0).then_inc(zeroed, 1)
            v.memset(den[:, 1, QE - 1:QE], 0.0).then_inc(zeroed, 1)
            v.wait_ge(zeroed, 3)
            v.memset(one[:, :], 1.0).then_inc(one_made, 1)

            def products(n, h, k, j):
                q = QUADS * n + j
                v.wait_ge(q_made, made(q))
                v.wait_ge(k_turned, made(q))
                if any_yet(free(q)):
                    v.wait_ge(s_made, free(q))
                v.tensor_tensor(prod[:, j % 2, :], k_ps[:, :], q_sb[:, j % 2, :], ALU.mult).then_inc(prod_made, 1)

            def maxima(n, h, k, j):
                q = QUADS * n + j
                if j == 0:
                    v.wait_ge(g.edges_in[h], landed(k, g.edge_dmas))
                if any_yet(free(q)):
                    v.wait_ge(s_less, free(q))
                v.tensor_copy(top[:, j % 2, 0:1], top[:, (j - 1) % 2, QE:QE + 1]).then_inc(carried, 1)
                v.wait_ge(s_made, made(q))
                v.tensor_tensor_scan(top[:, j % 2, 1:QE + 1], far[:, h, j * QE:(j + 1) * QE], s_ps[j % 2][:, :], top[:, (j - 1) % 2, QE:QE + 1], ALU.add, ALU.max).then_inc(top_made, 1)

            def falls(n, h, k, j):
                q = QUADS * n + j
                v.wait_ge(top_made, made(q))
                v.wait_ge(carried, made(q))
                if any_yet(free(q)):
                    v.wait_ge(fade_made, free(q))
                v.tensor_tensor(fall[:, j % 2, :], top[:, j % 2, 0:QE], top[:, j % 2, 1:QE + 1], ALU.subtract).then_inc(diff_made, 1)

            def forget(n, h, k, j):
                q = QUADS * n + j
                v.wait_ge(diff_made, made(q))
                v.tensor_tensor(fall[:, j % 2, :], fall[:, j % 2, :], far[:, h, j * QE:(j + 1) * QE], ALU.add).then_inc(fall_made, 1)

            def weigh(n, h, k, j):
                q = QUADS * n + j
                v.wait_ge(ex_made, made(q))
                v.wait_ge(v_turned, made(q))
                if any_yet(free(q)):
                    v.wait_ge(num_made, free(q))
                v.tensor_tensor(val[:, j % 2, :], v_ps[:, :], ex[:, j % 2, :], ALU.mult).then_inc(val_made, 1)

            def sums(n, h, k, j):
                q = QUADS * n + j
                v.wait_ge(fade_made, made(q))
                if any_yet(free(q)):
                    v.wait_ge(den_turned, free(q))
                if any_yet(q):
                    v.wait_ge(num_made, q)
                v.tensor_tensor_scan(den[:, j % 2, :], fade[:, j % 2, :], ex[:, j % 2, :], den[:, (j - 1) % 2, QE - 1:QE], ALU.mult, ALU.add).then_inc(den_made, 1)
                v.wait_ge(val_made, made(q))
                v.tensor_tensor_scan(num[:, j % 2, :], fade[:, j % 2, :], val[:, j % 2, :], num[:, (j - 1) % 2, QE - 1:QE], ALU.mult, ALU.add).then_inc(num_made, 1)

            pipelined(v, [(maxima, 1), (products, 0), (falls, 1), (weigh, 2), (forget, 1), (sums, 2)])


def build(nc, a, out):
    ctx = ExitStack()
    with ctx:
        def dram(name, shape, dt=F32):
            return nc.dram_tensor(name, shape, dt, kind="Internal").ap()

        t = {"x": a["x"]}
        for name in ("same", "far", "seed"):
            t[name] = dram(name, (1, EP), BF16)
        t["digits"] = dram("digits", (2, EP), BF16)
        t["rs"] = dram("rs", (FB * P,))
        t["seeds"] = dram("seeds", (EP + NP, D))
        for k in range(ACCS):
            t[f"acc{k}"] = dram(f"acc{k}", (NP + P, D))
        for name in ("nodes", "a1", "own1", "upd", "own2", "own3"):
            t[name] = dram(name, (NP, D))
        t["kv"] = dram("kv", (NP, 2 * D))
        rel = t["rel"] = dram("rel", (RELS * NP, D))
        for r in range(RELS):
            t[f"rel{r}"] = rel[r * NP:(r + 1) * NP, :]
        t["sum1"], t["sum2"], t["max3"] = dram("sum1", (EP, D)), dram("sum2", (EP, TW)), dram("max3", (EP, D))

        class Keep:
            pass

        keep, m = Keep(), Memory(nc, ctx, "keep")
        keep.ident, keep.iota, keep.eps = m.sb("ident", [P, P]), m.sb("iota", [P, 1]), m.sb("eps", [P, 1])
        keep.has, keep.last_ix, keep.seed_ix = m.sb("has", [P, NB]), m.sb("lastix", [P, NB], U32), m.sb("seedix", [P, NB], U32)
        keep.first_ix = m.sb("firstix", [GROUPS, TILES], U32)
        keep.src_ix, keep.rel_ix = m.sb("srcix", [P, NT], U32), m.sb("relix", [P, NT], U32)

        prologue(nc, a, t, keep)
        node_phase(nc, a, t, keep, 0, out)
        seed_tiles(nc, t, keep, "tiles0")
        edges_sum0(nc, a, t, keep)
        node_phase(nc, a, t, keep, 1, out)
        seed_tiles(nc, t, keep, "tiles1")
        edges_sum1(nc, a, t, keep)
        node_phase(nc, a, t, keep, 2, out)
        seed_tiles(nc, t, keep, "tiles2")
        edges_attend2(nc, a, t, keep)
        node_phase(nc, a, t, keep, 3, out)
        edges_max3(nc, a, t, keep)
        node_phase(nc, a, t, keep, 4, out)


def constants():
    p, e = np.arange(P), np.arange(GE) % P
    node = lambda blocks: (np.arange(blocks)[None, :] * P + p[:, None]).astype(np.float32)
    return {
        "ident": np.eye(P, dtype=np.float32),
        "negident": -np.eye(P, dtype=np.float32),
        "place_row": np.broadcast_to(p, (P, P)).astype(np.float32), "upper": np.tri(P, P, -1, dtype=np.float32).T,
        "iota": p[:, None].astype(np.float32),
        "eps": np.full((P, 1), EPS, np.float32),
        "place": np.broadcast_to(e, (GROUPS, GE)).astype(np.float32),
        "inside": np.broadcast_to(e > 0, (GROUPS, GE)).astype(np.float32),
        "nid": node(FB),
        "spare": node(NB) + EP,
        "lower": np.tri(P, P, -1, dtype=np.float32),
        "trash": (NP + p[:, None]).astype(np.float32),
        "place_value": np.repeat([[float(P)], [1.0]], P, 1).astype(np.float32),
        "heads": (np.kron(np.eye(HEADS), np.ones((HC, HC))) / np.sqrt(HC)).astype(np.float32),
    }


def laid_out(i):
    def filled(x, rows, value):
        x = np.asarray(x)
        return np.concatenate([x, np.full((rows - len(x), *x.shape[1:]), value, x.dtype)])

    def by_partition(x):
        return np.ascontiguousarray(x.reshape(NT, P).T)

    g = {k: np.asarray(v) for k, v in i.items()}
    src, dst = filled(g["src"], EP, N), filled(g["dst"], EP, NP - 1)
    zero = np.zeros(D, np.float32)
    msg, upd = g["L1_gnn_W_msg"], g["L1_gnn_W_upd"]
    rel_w, rel_b = g["L3_gnn_weight"], g["L3_gnn_bias"]
    return {
        "x": filled(g["x"], NP, 0),
        "src_flat": src, "src_pt": by_partition(src),
        "dst_prev": np.concatenate([np.array([-1], dst.dtype), dst]),
        "dst_tiles": dst.reshape(NT, P), "dst_first": np.ascontiguousarray(dst[::P]),
        "first_pt": filled(dst[::P], CHUNKS * P, FB * P).reshape(CHUNKS, P).T,
        "typ_pt": by_partition(filled(g["edge_type_4"], EP, 0)),
        "w_pt": by_partition(filled(g["edge_weight"], EP, 0)),
        "ed_row": filled(g["edge_weight1"], EP, 0).reshape(1, EP),
        "w0": np.ascontiguousarray(g["L0_gnn_W"].T), "b0": g["L0_gnn_b"],
        "w1": np.concatenate([msg[:D], msg[D:2 * D], g["L1_gnn_W_res"], upd[:D]], 1),
        "b1": np.concatenate([zero, g["L1_gnn_b_msg"], zero, g["L1_gnn_b_upd"]]),
        "w_dist": msg[2 * D:], "w_upd": upd[D:],
        "w2": np.concatenate([g[f"L2_gnn_W{x}"] for x in "kvqr"], 1),
        "b2": np.concatenate([g[f"L2_gnn_b{x}"] for x in "kvqr"]),
        "w3": np.concatenate(list(rel_w), 1), "b3": rel_b.reshape(-1),
    }


def kernel(**inputs):
    import concourse.bacc as bacc
    from concourse.bass_utils import run_bass_kernel_spmd

    nc = bacc.Bacc("TRN2", target_bir_lowering=False, num_devices=1)
    arrays = {f"in_{k}": np.ascontiguousarray(v) for k, v in {**laid_out(inputs), **constants()}.items()}
    a = {k[3:]: nc.dram_tensor(k, v.shape, mybir.dt.from_np(v.dtype), kind="ExternalInput").ap() for k, v in arrays.items()}
    out = nc.dram_tensor("out", (NP, D), F32, kind="ExternalOutput").ap()
    build(nc, a, out)
    r = run_bass_kernel_spmd(nc, [arrays], core_ids=[0])
    return r.results[0]["out"][:N]
```
